# Optimizing a Trainium2 kernel written in Bass

```python
import numpy as np
import jax
import jax.numpy as jnp

def _softmax(x, axis=-1):
    return jax.nn.softmax(x, axis=axis)

def _gelu(x):
    return jax.nn.gelu(x, approximate=True)

def _silu(x):
    return jax.nn.silu(x)

def _sigmoid(x):
    return jax.nn.sigmoid(x)

def _layernorm(x, axis=-1, eps=1e-05):
    m = jnp.mean(x, axis=axis, keepdims=True)
    v = jnp.var(x, axis=axis, keepdims=True)
    return (x - m) / jnp.sqrt(v + eps)

def _scatter_add(tgt, idx, src, axis=0):
    return tgt.at[idx].add(src)

def _segment_sum(src, seg, n):
    return jax.ops.segment_sum(src, seg, n)
kernel_name = 'mk_decoder_preln_d2_seqx_r8_0be106'

def setup_inputs(seed: int=0):
    np.random.seed(seed)
    _w = jnp.asarray

    def _rec_inputs():
        import jax
        import jax.numpy as jnp
        _rk = jax.random.key(seed)
        x = -0.000125 + 0.9999 * jax.random.normal(jax.random.fold_in(_rk, 1), (4, 256, 256), jnp.float32)
        _lenS = 256 - jax.random.randint(jax.random.fold_in(_rk, 7), (4,), 0, max(1, 256 // 4) + 1, jnp.int32)
        _lenS2 = 1601 - jax.random.randint(jax.random.fold_in(_rk, 8), (4,), 0, max(1, 1601 // 4) + 1, jnp.int32)
        _ctx_2048P = jax.random.normal(jax.random.fold_in(_rk, 11), (4, 16, 256), jnp.float32)
        _ctx_2048c = jax.random.dirichlet(jax.random.fold_in(_rk, 511), 0.3 * jnp.ones((16,), jnp.float32), (4, 1601))
        _ctx_2048t = jnp.einsum('bsk,bkd->bsd', _ctx_2048c, _ctx_2048P)
        _ctx_2048t = _ctx_2048t * jax.lax.rsqrt(jnp.mean(jnp.square(_ctx_2048t)) + 1e-12) * 0.953939
        ctx_2048 = -1.52775e-05 + 0.999936 * (_ctx_2048t + 0.3 * jax.random.normal(jax.random.fold_in(_rk, 611), (4, 1601, 256), jnp.float32))
        return (x, ctx_2048)
    x, ctx_2048 = _rec_inputs()

    def _L0_attn_setup():
        import jax, jax.numpy as jnp
        import numpy as np
        B, T, C = (4, 256, 256)
        H = 32
        N = C // H
        N_LAYER = 12
        LAYER_ID = 6
        EPS = 1e-05 * 144
        key = jax.random.key(seed)
        ks = jax.random.split(key, 8)
        r01 = LAYER_ID / N_LAYER
        r1a0 = 1.0 - LAYER_ID / N_LAYER
        ddd = jnp.arange(C, dtype=jnp.float32) / C
        time_maa_k = (ddd ** r1a0).reshape(1, 1, C)
        time_maa_v = time_maa_k + 0.3 * r01
        time_maa_r = (ddd ** (0.5 * r1a0)).reshape(1, 1, C)
        time_maa_g = time_maa_r
        h = jnp.arange(H, dtype=jnp.float32) / (H - 1)
        time_decay = (-6.0 + 5.0 * h ** (0.7 + 0.3 * r01)).reshape(H, 1)
        zigzag = (((jnp.arange(H) + 1) % 3).astype(jnp.float32) - 1.0) * 0.1
        time_faaaa = (r01 * (1.0 - h) + zigzag).reshape(H, 1)

        def W(k):
            return jax.random.normal(k, (C, C), dtype=jnp.float32) * 0.02
        return {'x': jax.random.normal(ks[0], (B, T, C), dtype=jnp.float32), 'time_maa_k': time_maa_k, 'time_maa_v': time_maa_v, 'time_maa_r': time_maa_r, 'time_maa_g': time_maa_g, 'time_decay': time_decay, 'time_faaaa': time_faaaa, 'Wr': W(ks[1]), 'Wk': W(ks[2]), 'Wv': W(ks[3]), 'Wg': W(ks[4]), 'Wo': W(ks[5]), 'gamma': jnp.ones((C,), jnp.float32), 'beta': jnp.zeros((C,), jnp.float32)}
    _L0_attn_all = _L0_attn_setup()
    _L0_attn_in = {k: v for k, v in _L0_attn_all.items() if k in ('time_maa_k', 'time_maa_v', 'time_maa_r', 'time_maa_g', 'time_decay', 'time_faaaa', 'Wr', 'Wk', 'Wv', 'Wg', 'Wo', 'gamma', 'beta')}
    del _L0_attn_all

    def _L0_xattn_setup():
        import jax, jax.numpy as jnp
        import numpy as np
        EPS = 1e-06
        NUM_HEADS = 16

        def _feature_map(x):
            return jnp.where(x > 0, x + 1.0, jnp.exp(x))
        key = jax.random.key(seed)
        ks = jax.random.split(key, 7)
        B, L, S, D = (4, 512, 512, 256)
        sc = 1.0 / np.sqrt(D)
        return {'query': jax.random.normal(ks[0], (B, L, D), jnp.float32), 'kv': jax.random.normal(ks[1], (B, S, D), jnp.float32), 'Wq': jax.random.normal(ks[2], (D, D), jnp.float32) * sc, 'Wg': jax.random.normal(ks[3], (D, D), jnp.float32) * sc, 'bg': jnp.ones((D,), jnp.float32), 'Wkv': jax.random.normal(ks[4], (2 * D, D), jnp.float32) * sc, 'Wo': jax.random.normal(ks[5], (D, D), jnp.float32) * sc}
    _L0_xattn_all = _L0_xattn_setup()
    _L0_xattn_in = {k: v for k, v in _L0_xattn_all.items() if k in ('Wq', 'Wg', 'bg', 'Wkv', 'Wo')}
    del _L0_xattn_all

    def _L0_ffn_setup():
        import jax, jax.numpy as jnp
        import numpy as np
        TOP_P = 0.9
        S, B, H, I, E = (256, 4, 256, 512, 8)

        def _top_p_weights(probs, top_p):
            order = jnp.argsort(-probs, axis=-1)
            sp = jnp.take_along_axis(probs, order, axis=-1)
            cum = jnp.cumsum(sp, axis=-1)
            exceed = cum > top_p
            first_idx = jnp.argmax(exceed, axis=-1)
            first = jnp.arange(probs.shape[-1])[None, :] == first_idx[:, None]
            keep = ~exceed | first
            kept = jnp.where(keep, sp, 0.0)
            t_idx = jnp.arange(probs.shape[0])[:, None]
            return jnp.zeros_like(probs).at[t_idx, order].set(kept)
        key = jax.random.key(seed)
        ks = jax.random.split(key, 5)
        scale = 0.02
        return {'hidden_states': jax.random.normal(ks[0], (S, B, H), dtype=jnp.float32), 'router_w': jax.random.normal(ks[1], (E, H), dtype=jnp.float32) * scale, 'gate_w': jax.random.normal(ks[2], (E, I, H), dtype=jnp.float32) * scale, 'up_w': jax.random.normal(ks[3], (E, I, H), dtype=jnp.float32) * scale, 'down_w': jax.random.normal(ks[4], (E, H, I), dtype=jnp.float32) * scale}
    _L0_ffn_all = _L0_ffn_setup()
    _L0_ffn_in = {k: v for k, v in _L0_ffn_all.items() if k in ('router_w', 'gate_w', 'up_w', 'down_w')}
    del _L0_ffn_all

    def _L1_attn_setup():
        import jax, jax.numpy as jnp
        import numpy as np
        DIM = 256
        HEAD_DIM = 128
        H = DIM // HEAD_DIM
        D_H = 128
        CHUNK = 256
        B, L = (1, 1024)
        BASE_LR = 0.01
        LN_EPS = 1e-06
        NS_COEFS = [(4.0848, -6.8946, 2.927), (3.9505, -6.3029, 2.6377), (3.7418, -5.5913, 2.3037), (2.8769, -3.1427, 1.2046), (2.8366, -3.0525, 1.2012)]

        def silu(x):
            return x * jax.nn.sigmoid(x)

        def silu_backprop(dy, x):
            s = jax.nn.sigmoid(x)
            return dy * s * (1 + x * (1 - s))

        def l2_norm(x, eps=1e-05):
            return x / (jnp.linalg.norm(x, axis=-1, keepdims=True) + eps)

        def zeropower_ns5(G):
            X = G
            transposed = G.shape[1] > G.shape[2]
            if transposed:
                X = jnp.swapaxes(X, 1, 2)
            X = X / (jnp.linalg.norm(X, axis=(1, 2), keepdims=True) + 1e-07)
            for a, b, c in NS_COEFS:
                A = X @ jnp.swapaxes(X, 1, 2)
                Bm = b * A + c * (A @ A)
                X = a * X + Bm @ X
            if transposed:
                X = jnp.swapaxes(X, 1, 2)
            return X

        def block_causal_lact_swiglu(w0, w1, w2, q, k, v, lr0, lr1, lr2, momentum):
            bh, l, d = k.shape
            v = jnp.swapaxes(v, 1, 2)
            q = jnp.swapaxes(q, 1, 2)
            w0_norm = jnp.linalg.norm(w0, axis=2, keepdims=True)
            w1_norm = jnp.linalg.norm(w1, axis=2, keepdims=True)
            w2_norm = jnp.linalg.norm(w2, axis=2, keepdims=True)
            outs = []
            for i in range(0, l - CHUNK, CHUNK):
                s, e = (i, i + CHUNK)
                ki = k[:, s:e, :]
                vi = v[:, :, s:e]
                qi = q[:, :, s:e]
                lr0i, lr1i, lr2i = (lr0[:, s:e, :], lr1[:, s:e, :], lr2[:, s:e, :])
                h = w2 @ qi
                gate = silu(w0 @ qi)
                outs.append(w1 @ (gate * h))
                kiT = jnp.swapaxes(ki, 1, 2)
                gate_before = w0 @ kiT
                hidden_before = w2 @ kiT
                hidden = silu(gate_before) * hidden_before
                dhidden = jnp.swapaxes(w1, 1, 2) @ vi
                dhidden_before = dhidden * silu(gate_before)
                dgate = dhidden * hidden_before
                dgate_before = silu_backprop(dgate, gate_before)
                lr1iT = jnp.swapaxes(lr1i, 1, 2)
                dw1 = vi @ jnp.swapaxes(hidden * lr1iT, 1, 2)
                dw0 = dgate_before @ (ki * lr0i)
                dw2 = dhidden_before @ (ki * lr2i)
                if momentum is not None:
                    m_i = jnp.mean(momentum[:, s:e, :], axis=1, keepdims=True)
                    dw0 = dw0 + dw0 * m_i
                    dw1 = dw1 + dw1 * m_i
                    dw2 = dw2 + dw2 * m_i
                dw0 = zeropower_ns5(dw0)
                dw1 = zeropower_ns5(dw1)
                dw2 = zeropower_ns5(dw2)
                w0 = w0 + dw0
                w1 = w1 + dw1
                w2 = w2 + dw2
                w0 = w0 / (jnp.linalg.norm(w0, axis=2, keepdims=True) + 1e-05) * w0_norm
                w1 = w1 / (jnp.linalg.norm(w1, axis=2, keepdims=True) + 1e-05) * w1_norm
                w2 = w2 / (jnp.linalg.norm(w2, axis=2, keepdims=True) + 1e-05) * w2_norm
            qi = q[:, :, l - CHUNK:]
            h = w2 @ qi
            gate = silu(w0 @ qi)
            outs.append(w1 @ (gate * h))
            out = jnp.concatenate(outs, axis=2)
            return jnp.swapaxes(out, 1, 2)

        def _forward(x, W_qkv, W_lr, W_o, W_m, b_m, W_s, b_s, ln_g, ln_b, w0, w1, w2):
            b, l, _ = x.shape
            h, d = (H, HEAD_DIM)
            qkv = silu(x @ W_qkv).reshape(b, l, h, 3 * d)
            ttt_q, ttt_k, ttt_v = jnp.split(qkv, 3, axis=-1)
            ttt_q = l2_norm(ttt_q).reshape(b * h, l, d)
            ttt_k = l2_norm(ttt_k).reshape(b * h, l, d)
            ttt_v = ttt_v.reshape(b * h, l, d)
            base_lr_inv = BASE_LR + jnp.log(-jnp.expm1(jnp.float32(-BASE_LR)))
            lr = jax.nn.softplus(x @ W_lr + base_lr_inv)
            lr = lr.reshape(b, l, 3, h).transpose(2, 0, 3, 1).reshape(3, b * h, l, 1)
            lr0, lr1, lr2 = (lr[0], lr[1], lr[2])
            w0b = jnp.tile(w0, (b, 1, 1))
            w1b = jnp.tile(w1, (b, 1, 1))
            w2b = jnp.tile(w2, (b, 1, 1))
            momentum = jax.nn.sigmoid(x @ W_m + b_m)
            momentum = momentum.reshape(b, l, h, 1).transpose(0, 2, 1, 3).reshape(b * h, l, 1)
            out = block_causal_lact_swiglu(w0b, w1b, w2b, ttt_q, ttt_k, ttt_v, lr0, lr1, lr2, momentum)
            mu = jnp.mean(out, axis=-1, keepdims=True)
            var = jnp.mean(jnp.square(out - mu), axis=-1, keepdims=True)
            out = (out - mu) * jax.lax.rsqrt(var + LN_EPS) * ln_g + ln_b
            scale = silu(x @ W_s + b_s).reshape(b, l, h, 1).transpose(0, 2, 1, 3).reshape(b * h, l, 1)
            out = out * scale
            out = out.reshape(b, h, l, d).transpose(0, 2, 1, 3).reshape(b, l, h * d)
            return out @ W_o
        ks = jax.random.split(jax.random.key(seed), 11)
        sd = 1.0 / np.sqrt(DIM)
        return {'x': jax.random.normal(ks[0], (B, L, DIM), jnp.float32), 'W_qkv': jax.random.normal(ks[1], (DIM, 3 * DIM), jnp.float32) * sd, 'W_lr': jax.random.normal(ks[2], (DIM, 3 * H), jnp.float32) * sd, 'W_o': jax.random.normal(ks[3], (DIM, DIM), jnp.float32) * sd, 'W_m': jax.random.normal(ks[4], (DIM, H), jnp.float32) * sd, 'b_m': jnp.zeros((H,), jnp.float32), 'W_s': jax.random.normal(ks[5], (DIM, H), jnp.float32) * sd, 'b_s': jnp.zeros((H,), jnp.float32), 'ln_g': jnp.ones((HEAD_DIM,), jnp.float32), 'ln_b': jnp.zeros((HEAD_DIM,), jnp.float32), 'w0': jax.random.normal(ks[6], (H, D_H, HEAD_DIM), jnp.float32) / np.sqrt(HEAD_DIM), 'w1': jax.random.normal(ks[7], (H, HEAD_DIM, D_H), jnp.float32) / np.sqrt(D_H), 'w2': jax.random.normal(ks[8], (H, D_H, HEAD_DIM), jnp.float32) / np.sqrt(HEAD_DIM)}
    _L1_attn_all = _L1_attn_setup()
    _L1_attn_in = {k: v for k, v in _L1_attn_all.items() if k in ('W_qkv', 'W_lr', 'W_o', 'W_m', 'b_m', 'W_s', 'b_s', 'ln_g', 'ln_b', 'w0', 'w1', 'w2')}
    del _L1_attn_all

    def _L1_xattn_setup():
        import jax, jax.numpy as jnp
        import numpy as np
        D_MODEL = 256
        NUM_HEADS = 16
        HEAD_DIM = D_MODEL // NUM_HEADS
        key = jax.random.key(seed)
        ks = jax.random.split(key, 10)
        B, S, T = (4, 512, 128)
        s = 1.0 / np.sqrt(D_MODEL)
        inp = {'query': jax.random.normal(ks[0], (B, S, D_MODEL), jnp.float32), 'key_value': jax.random.normal(ks[1], (B, T, D_MODEL), jnp.float32), 'Wq': jax.random.normal(ks[2], (D_MODEL, D_MODEL), jnp.float32) * s, 'bq': jnp.zeros((D_MODEL,), jnp.float32), 'Wk': jax.random.normal(ks[3], (D_MODEL, D_MODEL), jnp.float32) * s, 'bk': jnp.zeros((D_MODEL,), jnp.float32), 'Wv': jax.random.normal(ks[4], (D_MODEL, D_MODEL), jnp.float32) * s, 'bv': jnp.zeros((D_MODEL,), jnp.float32), 'Wo': jax.random.normal(ks[5], (D_MODEL, D_MODEL), jnp.float32) * s, 'bo': jnp.zeros((D_MODEL,), jnp.float32)}
        return inp
    _L1_xattn_all = _L1_xattn_setup()
    _L1_xattn_in = {k: v for k, v in _L1_xattn_all.items() if k in ('Wq', 'bq', 'Wk', 'bk', 'Wv', 'bv', 'Wo', 'bo')}
    del _L1_xattn_all

    def _L1_ffn_setup():
        import jax, jax.numpy as jnp
        import numpy as np
        HIDDEN = 256
        INTER = 688
        LUT_SIZE = 16

        def _ghost_linear(x, idx, lut):
            w = lut[idx]
            return jnp.einsum('bsh,oh->bso', x, w)
        key = jax.random.key(seed)
        k_x, k_lut, k_g, k_u, k_d = jax.random.split(key, 5)
        x = jax.random.normal(k_x, (2, 512, HIDDEN), dtype=jnp.float32)
        lut = jax.random.normal(k_lut, (LUT_SIZE,), dtype=jnp.float32) * 0.02
        gate_idx = jax.random.randint(k_g, (INTER, HIDDEN), 0, LUT_SIZE, dtype=jnp.int32)
        up_idx = jax.random.randint(k_u, (INTER, HIDDEN), 0, LUT_SIZE, dtype=jnp.int32)
        down_idx = jax.random.randint(k_d, (HIDDEN, INTER), 0, LUT_SIZE, dtype=jnp.int32)
        return {'x': x, 'lut': lut, 'gate_idx': gate_idx, 'up_idx': up_idx, 'down_idx': down_idx}
    _L1_ffn_all = _L1_ffn_setup()
    _L1_ffn_in = {k: v for k, v in _L1_ffn_all.items() if k in ('lut', 'gate_idx', 'up_idx', 'down_idx')}
    del _L1_ffn_all
    return {'x': x, 'ctx_2048': ctx_2048, 'L0_attn_time_maa_k': _L0_attn_in['time_maa_k'], 'L0_attn_time_maa_v': _L0_attn_in['time_maa_v'], 'L0_attn_time_maa_r': _L0_attn_in['time_maa_r'], 'L0_attn_time_maa_g': _L0_attn_in['time_maa_g'], 'L0_attn_time_decay': _L0_attn_in['time_decay'], 'L0_attn_time_faaaa': _L0_attn_in['time_faaaa'], 'L0_attn_Wr': _L0_attn_in['Wr'], 'L0_attn_Wk': _L0_attn_in['Wk'], 'L0_attn_Wv': _L0_attn_in['Wv'], 'L0_attn_Wg': _L0_attn_in['Wg'], 'L0_attn_Wo': _L0_attn_in['Wo'], 'L0_attn_gamma': _L0_attn_in['gamma'], 'L0_attn_beta': _L0_attn_in['beta'], 'L0_xattn_Wq': _L0_xattn_in['Wq'], 'L0_xattn_Wg': _L0_xattn_in['Wg'], 'L0_xattn_bg': _L0_xattn_in['bg'], 'L0_xattn_Wkv': _L0_xattn_in['Wkv'], 'L0_xattn_Wo': _L0_xattn_in['Wo'], 'L0_ffn_router_w': _L0_ffn_in['router_w'], 'L0_ffn_gate_w': _L0_ffn_in['gate_w'], 'L0_ffn_up_w': _L0_ffn_in['up_w'], 'L0_ffn_down_w': _L0_ffn_in['down_w'], 'L1_attn_W_qkv': _L1_attn_in['W_qkv'], 'L1_attn_W_lr': _L1_attn_in['W_lr'], 'L1_attn_W_o': _L1_attn_in['W_o'], 'L1_attn_W_m': _L1_attn_in['W_m'], 'L1_attn_b_m': _L1_attn_in['b_m'], 'L1_attn_W_s': _L1_attn_in['W_s'], 'L1_attn_b_s': _L1_attn_in['b_s'], 'L1_attn_ln_g': _L1_attn_in['ln_g'], 'L1_attn_ln_b': _L1_attn_in['ln_b'], 'L1_attn_w0': _L1_attn_in['w0'], 'L1_attn_w1': _L1_attn_in['w1'], 'L1_attn_w2': _L1_attn_in['w2'], 'L1_xattn_Wq': _L1_xattn_in['Wq'], 'L1_xattn_bq': _L1_xattn_in['bq'], 'L1_xattn_Wk': _L1_xattn_in['Wk'], 'L1_xattn_bk': _L1_xattn_in['bk'], 'L1_xattn_Wv': _L1_xattn_in['Wv'], 'L1_xattn_bv': _L1_xattn_in['bv'], 'L1_xattn_Wo': _L1_xattn_in['Wo'], 'L1_xattn_bo': _L1_xattn_in['bo'], 'L1_ffn_lut': _L1_ffn_in['lut'], 'L1_ffn_gate_idx': _L1_ffn_in['gate_idx'], 'L1_ffn_up_idx': _L1_ffn_in['up_idx'], 'L1_ffn_down_idx': _L1_ffn_in['down_idx']}

def reference(x, ctx_2048, L0_attn_time_maa_k, L0_attn_time_maa_v, L0_attn_time_maa_r, L0_attn_time_maa_g, L0_attn_time_decay, L0_attn_time_faaaa, L0_attn_Wr, L0_attn_Wk, L0_attn_Wv, L0_attn_Wg, L0_attn_Wo, L0_attn_gamma, L0_attn_beta, L0_xattn_Wq, L0_xattn_Wg, L0_xattn_bg, L0_xattn_Wkv, L0_xattn_Wo, L0_ffn_router_w, L0_ffn_gate_w, L0_ffn_up_w, L0_ffn_down_w, L1_attn_W_qkv, L1_attn_W_lr, L1_attn_W_o, L1_attn_W_m, L1_attn_b_m, L1_attn_W_s, L1_attn_b_s, L1_attn_ln_g, L1_attn_ln_b, L1_attn_w0, L1_attn_w1, L1_attn_w2, L1_xattn_Wq, L1_xattn_bq, L1_xattn_Wk, L1_xattn_bk, L1_xattn_Wv, L1_xattn_bv, L1_xattn_Wo, L1_xattn_bo, L1_ffn_lut, L1_ffn_gate_idx, L1_ffn_up_idx, L1_ffn_down_idx):
    import jax
    import jax.numpy as jnp

    def _L0_attn_ref(x, time_maa_k, time_maa_v, time_maa_r, time_maa_g, time_decay, time_faaaa, Wr, Wk, Wv, Wg, Wo, gamma, beta):
        import jax, jax.numpy as jnp
        import numpy as np
        B, T, C = (4, 256, 256)
        H = 32
        N = C // H
        N_LAYER = 12
        LAYER_ID = 6
        EPS = 1e-05 * 144
        B, T, C = x.shape
        Hh = time_decay.shape[0]
        Nn = C // Hh
        Q = 32 if T % 32 == 0 else 128 if T % 128 == 0 else T
        nC = T // Q
        xx = jnp.pad(x, ((0, 0), (1, 0), (0, 0)))[:, :T] - x
        xk = x + xx * time_maa_k
        xv = x + xx * time_maa_v
        xr = x + xx * time_maa_r
        xg = x + xx * time_maa_g
        r = (xr @ Wr.T).reshape(B, T, Hh, Nn).transpose(0, 2, 1, 3)
        k = (xk @ Wk.T).reshape(B, T, Hh, Nn).transpose(0, 2, 3, 1)
        v = (xv @ Wv.T).reshape(B, T, Hh, Nn).transpose(0, 2, 1, 3)
        g = jax.nn.silu(xg @ Wg.T)
        w = jnp.exp(-jnp.exp(time_decay))
        u = time_faaaa
        ws = (w ** Q).reshape(1, Hh, 1, 1)
        qa = jnp.arange(Q)
        wk = (w ** (Q - 1 - qa)[None, :]).reshape(1, Hh, 1, Q)
        wb = (w ** qa[None, :]).reshape(1, Hh, Q, 1)
        i = qa[:, None]
        j = qa[None, :]
        pw = w.reshape(Hh, 1, 1) ** jnp.maximum(i - j - 1, 0)[None]
        w_mat = jnp.where(i > j, pw, jnp.where(i == j, u.reshape(Hh, 1, 1), jnp.zeros((), x.dtype))).reshape(1, Hh, Q, Q)
        rr = r.reshape(B, Hh, nC, Q, Nn).transpose(2, 0, 1, 3, 4)
        kk = k.reshape(B, Hh, Nn, nC, Q).transpose(3, 0, 1, 2, 4)
        vv = v.reshape(B, Hh, nC, Q, Nn).transpose(2, 0, 1, 3, 4)

        def step(state, inp):
            rc, kc, vc = inp
            att = rc @ kc * w_mat
            yc = att @ vc + rc @ state * wb
            new_state = ws * state + kc * wk @ vc
            return (new_state, yc)
        state0 = jnp.zeros((B, Hh, Nn, Nn), x.dtype)
        _, ys = jax.lax.scan(step, state0, (rr, kk, vv))
        y = ys.transpose(1, 0, 3, 2, 4).reshape(B, T, Hh, Nn)
        mu = jnp.mean(y, axis=-1, keepdims=True)
        var = jnp.mean(jnp.square(y - mu), axis=-1, keepdims=True)
        yn = ((y - mu) / jnp.sqrt(var + EPS)).reshape(B, T, C) * gamma + beta
        out = yn * g @ Wo.T
        return out

    def _L0_xattn_ref(query, kv, Wq, Wg, bg, Wkv, Wo):
        import jax, jax.numpy as jnp
        import numpy as np
        EPS = 1e-06
        NUM_HEADS = 16

        def _feature_map(x):
            return jnp.where(x > 0, x + 1.0, jnp.exp(x))
        B, L, D = query.shape
        S = kv.shape[1]
        H = NUM_HEADS
        hd = D // H
        q = query @ Wq.T
        gate = jax.nn.sigmoid(query @ Wg.T + bg)
        kvp = kv @ Wkv.T
        k, v = jnp.split(kvp, 2, axis=-1)
        q = _feature_map(q.reshape(B, L, H, hd).transpose(0, 2, 1, 3))
        k = _feature_map(k.reshape(B, S, H, hd).transpose(0, 2, 1, 3))
        v = v.reshape(B, S, H, hd).transpose(0, 2, 1, 3)
        kv_summary = jnp.einsum('bhsd,bhse->bhde', k, v)
        k_sum = k.sum(axis=-2)
        z = 1.0 / (jnp.einsum('bhld,bhd->bhl', q, k_sum)[..., None] + EPS)
        attn = jnp.einsum('bhld,bhde->bhle', q, kv_summary) * z
        attn = attn.transpose(0, 2, 1, 3).reshape(B, L, D)
        out = attn * gate @ Wo.T
        return out

    def _L0_ffn_ref(hidden_states, router_w, gate_w, up_w, down_w):
        import jax, jax.numpy as jnp
        import numpy as np
        TOP_P = 0.9
        S, B, H, I, E = (256, 4, 256, 512, 8)

        def _top_p_weights(probs, top_p):
            order = jnp.argsort(-probs, axis=-1)
            sp = jnp.take_along_axis(probs, order, axis=-1)
            cum = jnp.cumsum(sp, axis=-1)
            exceed = cum > top_p
            first_idx = jnp.argmax(exceed, axis=-1)
            first = jnp.arange(probs.shape[-1])[None, :] == first_idx[:, None]
            keep = ~exceed | first
            kept = jnp.where(keep, sp, 0.0)
            t_idx = jnp.arange(probs.shape[0])[:, None]
            return jnp.zeros_like(probs).at[t_idx, order].set(kept)
        s, b, h = hidden_states.shape
        x = hidden_states.reshape(-1, h)
        probs = jax.nn.softmax(x @ router_w.T, axis=-1)
        w = _top_p_weights(probs, TOP_P)
        out = jnp.zeros_like(x)
        n_exp = router_w.shape[0]
        for e in range(n_exp):
            g = jax.nn.silu(x @ gate_w[e].T)
            u = x @ up_w[e].T
            y = g * u @ down_w[e].T
            out = out + y * w[:, e:e + 1]
        return out.reshape(s, b, h)

    def _L1_attn_ref(x, W_qkv, W_lr, W_o, W_m, b_m, W_s, b_s, ln_g, ln_b, w0, w1, w2):
        import jax, jax.numpy as jnp
        import numpy as np
        DIM = 256
        HEAD_DIM = 128
        H = DIM // HEAD_DIM
        D_H = 128
        CHUNK = 256
        B, L = (1, 1024)
        BASE_LR = 0.01
        LN_EPS = 1e-06
        NS_COEFS = [(4.0848, -6.8946, 2.927), (3.9505, -6.3029, 2.6377), (3.7418, -5.5913, 2.3037), (2.8769, -3.1427, 1.2046), (2.8366, -3.0525, 1.2012)]

        def silu(x):
            return x * jax.nn.sigmoid(x)

        def silu_backprop(dy, x):
            s = jax.nn.sigmoid(x)
            return dy * s * (1 + x * (1 - s))

        def l2_norm(x, eps=1e-05):
            return x / (jnp.linalg.norm(x, axis=-1, keepdims=True) + eps)

        def zeropower_ns5(G):
            X = G
            transposed = G.shape[1] > G.shape[2]
            if transposed:
                X = jnp.swapaxes(X, 1, 2)
            X = X / (jnp.linalg.norm(X, axis=(1, 2), keepdims=True) + 1e-07)
            for a, b, c in NS_COEFS:
                A = X @ jnp.swapaxes(X, 1, 2)
                Bm = b * A + c * (A @ A)
                X = a * X + Bm @ X
            if transposed:
                X = jnp.swapaxes(X, 1, 2)
            return X

        def block_causal_lact_swiglu(w0, w1, w2, q, k, v, lr0, lr1, lr2, momentum):
            bh, l, d = k.shape
            v = jnp.swapaxes(v, 1, 2)
            q = jnp.swapaxes(q, 1, 2)
            w0_norm = jnp.linalg.norm(w0, axis=2, keepdims=True)
            w1_norm = jnp.linalg.norm(w1, axis=2, keepdims=True)
            w2_norm = jnp.linalg.norm(w2, axis=2, keepdims=True)
            outs = []
            for i in range(0, l - CHUNK, CHUNK):
                s, e = (i, i + CHUNK)
                ki = k[:, s:e, :]
                vi = v[:, :, s:e]
                qi = q[:, :, s:e]
                lr0i, lr1i, lr2i = (lr0[:, s:e, :], lr1[:, s:e, :], lr2[:, s:e, :])
                h = w2 @ qi
                gate = silu(w0 @ qi)
                outs.append(w1 @ (gate * h))
                kiT = jnp.swapaxes(ki, 1, 2)
                gate_before = w0 @ kiT
                hidden_before = w2 @ kiT
                hidden = silu(gate_before) * hidden_before
                dhidden = jnp.swapaxes(w1, 1, 2) @ vi
                dhidden_before = dhidden * silu(gate_before)
                dgate = dhidden * hidden_before
                dgate_before = silu_backprop(dgate, gate_before)
                lr1iT = jnp.swapaxes(lr1i, 1, 2)
                dw1 = vi @ jnp.swapaxes(hidden * lr1iT, 1, 2)
                dw0 = dgate_before @ (ki * lr0i)
                dw2 = dhidden_before @ (ki * lr2i)
                if momentum is not None:
                    m_i = jnp.mean(momentum[:, s:e, :], axis=1, keepdims=True)
                    dw0 = dw0 + dw0 * m_i
                    dw1 = dw1 + dw1 * m_i
                    dw2 = dw2 + dw2 * m_i
                dw0 = zeropower_ns5(dw0)
                dw1 = zeropower_ns5(dw1)
                dw2 = zeropower_ns5(dw2)
                w0 = w0 + dw0
                w1 = w1 + dw1
                w2 = w2 + dw2
                w0 = w0 / (jnp.linalg.norm(w0, axis=2, keepdims=True) + 1e-05) * w0_norm
                w1 = w1 / (jnp.linalg.norm(w1, axis=2, keepdims=True) + 1e-05) * w1_norm
                w2 = w2 / (jnp.linalg.norm(w2, axis=2, keepdims=True) + 1e-05) * w2_norm
            qi = q[:, :, l - CHUNK:]
            h = w2 @ qi
            gate = silu(w0 @ qi)
            outs.append(w1 @ (gate * h))
            out = jnp.concatenate(outs, axis=2)
            return jnp.swapaxes(out, 1, 2)

        def _forward(x, W_qkv, W_lr, W_o, W_m, b_m, W_s, b_s, ln_g, ln_b, w0, w1, w2):
            b, l, _ = x.shape
            h, d = (H, HEAD_DIM)
            qkv = silu(x @ W_qkv).reshape(b, l, h, 3 * d)
            ttt_q, ttt_k, ttt_v = jnp.split(qkv, 3, axis=-1)
            ttt_q = l2_norm(ttt_q).reshape(b * h, l, d)
            ttt_k = l2_norm(ttt_k).reshape(b * h, l, d)
            ttt_v = ttt_v.reshape(b * h, l, d)
            base_lr_inv = BASE_LR + jnp.log(-jnp.expm1(jnp.float32(-BASE_LR)))
            lr = jax.nn.softplus(x @ W_lr + base_lr_inv)
            lr = lr.reshape(b, l, 3, h).transpose(2, 0, 3, 1).reshape(3, b * h, l, 1)
            lr0, lr1, lr2 = (lr[0], lr[1], lr[2])
            w0b = jnp.tile(w0, (b, 1, 1))
            w1b = jnp.tile(w1, (b, 1, 1))
            w2b = jnp.tile(w2, (b, 1, 1))
            momentum = jax.nn.sigmoid(x @ W_m + b_m)
            momentum = momentum.reshape(b, l, h, 1).transpose(0, 2, 1, 3).reshape(b * h, l, 1)
            out = block_causal_lact_swiglu(w0b, w1b, w2b, ttt_q, ttt_k, ttt_v, lr0, lr1, lr2, momentum)
            mu = jnp.mean(out, axis=-1, keepdims=True)
            var = jnp.mean(jnp.square(out - mu), axis=-1, keepdims=True)
            out = (out - mu) * jax.lax.rsqrt(var + LN_EPS) * ln_g + ln_b
            scale = silu(x @ W_s + b_s).reshape(b, l, h, 1).transpose(0, 2, 1, 3).reshape(b * h, l, 1)
            out = out * scale
            out = out.reshape(b, h, l, d).transpose(0, 2, 1, 3).reshape(b, l, h * d)
            return out @ W_o
        return _forward(x, W_qkv, W_lr, W_o, W_m, b_m, W_s, b_s, ln_g, ln_b, w0, w1, w2)

    def _L1_xattn_ref(query, key_value, Wq, bq, Wk, bk, Wv, bv, Wo, bo):
        import jax, jax.numpy as jnp
        import numpy as np
        D_MODEL = 256
        NUM_HEADS = 16
        HEAD_DIM = D_MODEL // NUM_HEADS
        B, S, _ = query.shape
        T = key_value.shape[1]
        Q = query @ Wq.T + bq
        K = key_value @ Wk.T + bk
        V = key_value @ Wv.T + bv
        Q = Q.reshape(B, S, NUM_HEADS, HEAD_DIM).transpose(0, 2, 1, 3)
        K = K.reshape(B, T, NUM_HEADS, HEAD_DIM).transpose(0, 2, 1, 3)
        V = V.reshape(B, T, NUM_HEADS, HEAD_DIM).transpose(0, 2, 1, 3)
        scale = 1.0 / np.sqrt(HEAD_DIM).astype(np.float32)
        scores = jnp.einsum('bhsd,bhtd->bhst', Q, K) * scale
        attn = jax.nn.softmax(scores, axis=-1)
        ctx = jnp.einsum('bhst,bhtd->bhsd', attn, V)
        ctx = ctx.transpose(0, 2, 1, 3).reshape(B, S, D_MODEL)
        return ctx @ Wo.T + bo

    def _L1_ffn_ref(x, lut, gate_idx, up_idx, down_idx):
        import jax, jax.numpy as jnp
        import numpy as np
        HIDDEN = 256
        INTER = 688
        LUT_SIZE = 16

        def _ghost_linear(x, idx, lut):
            w = lut[idx]
            return jnp.einsum('bsh,oh->bso', x, w)
        gate = _ghost_linear(x, gate_idx, lut)
        up = _ghost_linear(x, up_idx, lut)
        h = jax.nn.silu(gate) * up
        return _ghost_linear(h, down_idx, lut)
    x = x + _L0_attn_ref(_layernorm(x, axis=-1), L0_attn_time_maa_k, L0_attn_time_maa_v, L0_attn_time_maa_r, L0_attn_time_maa_g, L0_attn_time_decay, L0_attn_time_faaaa, L0_attn_Wr, L0_attn_Wk, L0_attn_Wv, L0_attn_Wg, L0_attn_Wo, L0_attn_gamma, L0_attn_beta)
    x = x + _L0_xattn_ref(_layernorm(x, axis=-1), ctx_2048, L0_xattn_Wq, L0_xattn_Wg, L0_xattn_bg, L0_xattn_Wkv, L0_xattn_Wo)
    x = x + _L0_ffn_ref(_layernorm(x, axis=-1), L0_ffn_router_w, L0_ffn_gate_w, L0_ffn_up_w, L0_ffn_down_w)
    x = x + _L1_attn_ref(_layernorm(x, axis=-1), L1_attn_W_qkv, L1_attn_W_lr, L1_attn_W_o, L1_attn_W_m, L1_attn_b_m, L1_attn_W_s, L1_attn_b_s, L1_attn_ln_g, L1_attn_ln_b, L1_attn_w0, L1_attn_w1, L1_attn_w2)
    x = x + _L1_xattn_ref(_layernorm(x, axis=-1), ctx_2048, L1_xattn_Wq, L1_xattn_bq, L1_xattn_Wk, L1_xattn_bk, L1_xattn_Wv, L1_xattn_bv, L1_xattn_Wo, L1_xattn_bo)
    x = x + _L1_ffn_ref(_layernorm(x, axis=-1), L1_ffn_lut, L1_ffn_gate_idx, L1_ffn_up_idx, L1_ffn_down_idx)
    return x

_drawn_inputs = setup_inputs


def setup_inputs(seed=0):
    import zlib

    import numpy as np

    out = dict(_drawn_inputs(seed))
    spreads = {'L0_attn_gamma': (1.0, 0.6),
     'L0_attn_beta': (0.0, 0.8),
     'L0_xattn_bg': (1.0, 0.6),
     'L1_attn_b_m': (0.0, 0.1),
     'L1_attn_b_s': (0.0, 2.0),
     'L1_attn_ln_g': (1.0, 0.565),
     'L1_attn_ln_b': (0.0, 0.556),
     'L1_xattn_bq': (0.0, 1.676),
     'L1_xattn_bk': (0.0, 2.0),
     'L1_xattn_bv': (0.0, 0.395),
     'L1_xattn_bo': (0.0, 0.37)}
    factors = {'L0_attn_time_maa_v': 3.171,
     'L0_attn_time_maa_r': 3.326,
     'L0_attn_time_maa_g': 3.653,
     'L0_attn_time_faaaa': 8.0,
     'L0_xattn_Wq': 3.663,
     'L0_ffn_router_w': 8.0,
     'L0_ffn_gate_w': 5.865,
     'L0_ffn_up_w': 5.79,
     'L0_ffn_down_w': 5.787,
     'L1_ffn_lut': 6.267}
    for name, (base, spread) in spreads.items():
        noise = np.random.default_rng([zlib.crc32(name.encode()), seed]).standard_normal(out[name].shape)
        drawn = base * np.exp(spread * noise) if base else spread * noise
        out[name] = jnp.asarray(drawn.astype(out[name].dtype))
    for name, factor in factors.items():
        out[name] = (out[name] * factor).astype(out[name].dtype)
    return out
```

```python
from contextlib import ExitStack

import concourse.bass as bass
import concourse.mybir as mybir

F32 = mybir.dt.float32
BF16 = mybir.dt.bfloat16
I32 = mybir.dt.int32
ALU = mybir.AluOpType
ACT = mybir.ActivationFunctionType
AX = mybir.AxisListType

P = 128
BATCH, SEQ, DIM = 4, 256, 256
TOK = SEQ // P
KT = DIM // P
CTX = 1601
CTILES = -(-CTX // P)
LN_EPS = 1e-5


class Signal:

    def __init__(self, sem, per=0):
        self.sem, self.per = sem, per

    def __call__(self, i, k):
        return self.sem, i * self.per + k


def rows(t):
    return min(P, CTX - t * P)


def attention_and_context(nc, d, x_all, x_loaded, consts):
    HEADS, HD = 32, 8
    GROUP_EPS = 1e-5 * 144
    ZEPS = 1e-6
    SC = SEQ + P
    RING = 3
    ATTS = 8
    ident, ones = consts["ident"], consts["ones"]
    with ExitStack() as ctx:
        def sb(name, shape, dt=F32):
            return ctx.enter_context(nc.sbuf_tensor(name, shape, dt))

        def sig(name, per=0):
            return Signal(ctx.enter_context(nc.semaphore(name)), per)

        bank = [ctx.enter_context(nc.psum_tensor(f"a_bank{n}", [P, 512], F32)) for n in range(8)]

        w_names = ["WrT", "WkT", "WvT", "WgT", "WoT", "XWqT", "XWgT", "XWoT"]
        w = {n: sb("a_" + n, [P, KT, DIM]) for n in w_names}
        w["XWkvT"] = sb("a_XWkvT", [P, KT, 2 * DIM])
        cols = {n: sb("a_" + n, [P, KT]) for n in ["maa_k", "maa_v", "maa_r", "maa_g", "xbg"]}
        gamma, beta = sb("gamma", [P, DIM]), sb("beta", [P, DIM])
        delta, strict, diag = sb("delta", [P, SC]), sb("strict", [P, SC]), sb("diag", [P, SC])
        headmask, blk16 = sb("headmask", [P, P // HD]), sb("blk16", [P, P])
        logw, faaaa = sb("logw", [P, HEADS]), sb("faaaa", [P, HEADS])
        decay = sb("decay", [P, HEADS, SC])
        ctxT = sb("ctxT", [P, KT, CTX])
        mean_var, stats = sb("a_mean_var", [P, TOK, 2]), sb("a_stats", [P, TOK, 6])
        rstd, half_neg = sb("a_rstd", [P, TOK]), sb("a_half_neg", [P, 64])
        var_eps, eps, group_eps = sb("a_var_eps", [P, TOK]), sb("a_eps", [P, TOK]), sb("group_eps", [P, 64])
        lnx = sb("a_lnx", [P, TOK, DIM])
        wait_pad = sb("a_wait_pad", [P, 1])
        lnT = sb("a_lnT", [P, KT, SEQ + 1])
        ln2T = sb("a_ln2T", [P, KT, SEQ])
        diff = sb("diff", [P, KT, SEQ])
        mix = {n: sb("mix_" + n, [P, KT, SEQ]) for n in "krvg"}
        r_sb, k_sb = sb("r_sb", [P, KT, SEQ]), sb("k_sb", [P, KT, SEQ])
        r_head = sb("r_head", [P, ATTS, SEQ])
        v_pad = sb("v_pad", [P, TOK, 8, 4 * 40])
        att = sb("att", [P, ATTS, SC])
        y_sb, g_tanh, g_silu = sb("y_sb", [P, KT, SEQ]), sb("g_tanh", [P, TOK, DIM]), sb("g_silu", [P, TOK, DIM])
        y_c, y_sq = sb("y_c", [P, TOK * HEADS, HD]), sb("y_sq", [P, TOK * HEADS, HD])
        g_mean, g_var, g_rstd = (sb(n, [P, TOK * HEADS]) for n in ("g_mean", "g_var", "g_rstd"))
        zT = sb("zT", [P, KT, SEQ])
        x1 = sb("x1", [P, TOK, DIM])
        k_min, k_exp, k_feat = (sb(n, [P, 2, DIM]) for n in ("k_min", "k_exp", "k_feat"))
        v_ones = sb("v_ones", [P, 2, KT, P + 1])
        kv_m, ks_m = sb("kv_m", [P, KT, P]), sb("ks_m", [P, KT, P])
        ks_col = sb("ks_col", [P, KT])
        q_min, q_exp, q_feat = (sb(n, [P, KT, SEQ]) for n in ("q_min", "q_exp", "q_feat"))
        gate, den, aT = sb("gate", [P, KT, SEQ]), sb("den", [P, KT, SEQ]), sb("aT", [P, KT, SEQ])
        hbg = sb("hbg", [P, KT])

        const_in, weights_in = sig("a_const_in"), sig("a_weights_in")
        ctx_in = sig("ctx_in", 16)
        logw_exp, logw_ready, decay_exp, decay_strict, decay_ready = (
            sig(n) for n in ("logw_exp", "logw_ready", "decay_exp", "decay_strict", "decay_ready"))
        zeroed, ones_set, hbg_ready = sig("zeroed"), sig("ones_set"), sig("hbg_ready")
        batch_done = sig("a_batch_done", 1)
        VSTEPS, GSTEPS = 16, 3
        vstep, gstep = sig("a_vstep", VSTEPS), sig("a_gstep", GSTEPS)
        stats_ready, rstd_ready, ln_ready = sig("a_stats_ready", 2), sig("a_rstd_ready", 2), sig("a_ln_ready", 2)
        lnT_psum, lnT_ready = sig("a_lnT_psum", 2), sig("a_lnT_ready", 2)
        ctx_psum, k_min_ready, k_exp_ready = sig("ctx_psum", CTILES), sig("k_min_ready", CTILES), sig("k_exp_ready", CTILES)
        k_feat_ready, v_ready, kv_added = sig("k_feat_ready", CTILES), sig("v_ready", CTILES), sig("kv_added", CTILES)
        kv_ready = sig("kv_ready", 1)
        mix_ready = sig("mix_ready", 4)
        proj_psum, proj_read = sig("proj_psum", 4), sig("proj_read", 4)
        g_ready = sig("g_ready", 1)
        r_head_ready = sig("r_head_ready", HEADS)
        score_psum, att_ready, group_added = sig("score_psum", HEADS), sig("att_ready", HEADS), sig("group_added", 8)
        y_ready, yt_psum = sig("y_ready", 1), sig("yt_psum", 1)
        gvar_ready, grstd_ready, z_ready = sig("gvar_ready", 1), sig("grstd_ready", 1), sig("z_ready", 1)
        zT_psum, zT_ready, o_psum = sig("zT_psum", 1), sig("zT_ready", 1), sig("o_psum", 1)
        q_psum, q_min_ready, q_exp_ready, q_feat_ready = (sig(n, 1) for n in ("q_psum", "q_min_ready", "q_exp_ready", "q_feat_ready"))
        gate_psum, gate_tanh, num_psum, den_psum = (sig(n, 1) for n in ("gate_psum", "gate_tanh", "num_psum", "den_psum"))
        aT_ready, xo_psum = sig("aT_ready", 1), sig("xo_psum", 1)

        ORDER = [(half, q * 4 + m) for half in range(KT) for m in range(4) for q in range(4)]

        def wide(t):
            return t[:, :, :].rearrange("p a b -> p (a b)")

        consts_list = [(delta, d["delta"]), (strict, d["strict"]), (diag, d["diag"]), (headmask, d["headmask"]),
                       (blk16, d["blk16"]), (logw, d["time_decay"].partition_broadcast(P)),
                       (faaaa, d["faaaa"].partition_broadcast(P)), (gamma, d["gamma"].partition_broadcast(P)),
                       (beta, d["beta"].partition_broadcast(P))] + [(cols[n], d[n]) for n in cols]
        weights_list = [(w[n], d[n]) for n in ["XWkvT", "WkT", "WrT", "WvT", "WgT", "WoT", "XWqT", "XWgT", "XWoT"]]

        with nc.Block() as block:
            @block.sync
            def _(sp):
                for t, src in consts_list:
                    sp.dma_start(t[:], src).then_inc(const_in.sem, 16)
                with sp.Fori(0, BATCH) as i:
                    sp.wait_ge(*batch_done(i, 1))
                    sp.dma_start(ctxT[:], d["ctxT"][i].rearrange("(k p) s -> p k s", p=P)).then_inc(ctx_in.sem, 16)

            @block.gpsimd
            def _(pool):
                pool.memset(v_pad[:], 0.0).then_inc(zeroed.sem, 1)
                pool.memset(lnT[:, :, 0:1], 0.0).then_inc(zeroed.sem, 1)
                pool.memset(half_neg[:], -0.5).then_inc(zeroed.sem, 1)
                pool.memset(eps[:], LN_EPS).then_inc(zeroed.sem, 1)
                pool.memset(group_eps[:], GROUP_EPS * HD).then_inc(zeroed.sem, 1)
                pool.memset(v_ones[:, :, :, P:P + 1], 1.0).then_inc(zeroed.sem, 1)
                pool.wait_ge(const_in.sem, 16 * len(consts_list))
                for h in range(HEADS):
                    pool.wait_ge(decay_exp.sem, h + 1)
                    pool.tensor_tensor(decay[:, h, :], decay[:, h, :], strict[:], ALU.mult).then_inc(decay_strict.sem, 1)
                pool.wait_ge(zeroed.sem, 6)
                with pool.Fori(0, BATCH) as i:
                    n = [0]

                    def step(ins):
                        n[0] += 1
                        ins.then_inc(gstep.sem, 1)
                        pool.wait_ge(*gstep(i, n[0]))

                    def rsqrt_var(k):
                        pool.wait_ge(*stats_ready(i, k))
                        step(pool.tensor_tensor(var_eps[:], mean_var[:, :, 1], eps[:, 0:TOK], ALU.add))
                        pool.tensor_tensor(rstd[:], var_eps[:], half_neg[:, 0:TOK], ALU.pow).then_inc(rstd_ready.sem, 1)

                    rsqrt_var(1)
                    pool.wait_ge(*gvar_ready(i, 1))
                    step(pool.tensor_tensor(g_var[:], g_var[:], group_eps[:], ALU.add))
                    pool.tensor_tensor(g_rstd[:], g_var[:], half_neg[:], ALU.pow).then_inc(grstd_ready.sem, 1)
                    rsqrt_var(2)
                    assert n[0] == GSTEPS

            @block.scalar
            def _(act):
                for t, src in weights_list:
                    act.dma_start(t[:], src.rearrange("(k p) n -> p k n", p=P)).then_inc(weights_in.sem, 16)
                act.wait_ge(const_in.sem, 16 * len(consts_list))
                act.activation(logw[:], logw[:], ACT.Exp).then_inc(logw_exp.sem, 1)
                act.wait_ge(logw_ready.sem, 2)
                for h in range(HEADS):
                    act.activation(decay[:, h, :], delta[:], ACT.Exp, scale=logw[:, h:h + 1]).then_inc(decay_exp.sem, 1)
                act.wait_ge(zeroed.sem, 6)
                with act.Fori(0, BATCH) as i:
                    for t in range(CTILES):
                        m = rows(t)
                        act.wait_ge(*k_min_ready(i, t + 1))
                        if t >= 2:
                            act.wait_ge(*kv_added(i, t - 1))
                        act.copy(v_ones[0:m, t % 2, :, 0:P],
                                 bank[5 + t % 2][0:m, DIM:].rearrange("p (a b) -> p a b", a=KT)).then_inc(v_ready.sem, 1)
                        act.activation(k_exp[0:m, t % 2, :], k_min[0:m, t % 2, :], ACT.Exp).then_inc(k_exp_ready.sem, 1)
                    act.wait_ge(*lnT_psum(i, 1))
                    act.copy(lnT[:, :, 1:], bank[0][:].rearrange("p (a b) -> p a b", a=KT)).then_inc(lnT_ready.sem, 1)
                    act.wait_ge(*proj_psum(i, 1))
                    act.copy(wide(k_sb), bank[1][:]).then_inc(proj_read.sem, 1)
                    act.wait_ge(*proj_psum(i, 2))
                    act.copy(wide(r_sb), bank[2][:]).then_inc(proj_read.sem, 1)
                    act.wait_ge(*proj_psum(i, 3))
                    for j in range(TOK):
                        last = act.copy(v_pad[:, j].rearrange("p q (m e) -> p q m e", m=4)[:, :, :, 0:HD],
                                        bank[7][:, j * DIM:(j + 1) * DIM].rearrange("p (q m e) -> p q m e", q=8, m=4))
                    last.then_inc(proj_read.sem, 1)
                    act.wait_ge(*proj_psum(i, 4))
                    act.activation(wide(g_tanh), bank[0][:], ACT.Tanh, scale=0.5).then_inc(proj_read.sem, 1)
                    act.wait_ge(*proj_read(i, 4))
                    for n_, (half, h) in enumerate(ORDER):
                        if n_ >= ATTS:
                            act.wait_ge(*score_psum(i, n_ - ATTS + 1))
                        act.activation(r_head[:, n_ % ATTS, :], r_sb[:, half, :], ACT.Copy,
                                       scale=headmask[:, h:h + 1]).then_inc(r_head_ready.sem, 1)
                    act.wait_ge(*group_added(i, 8))
                    act.copy(wide(y_sb), bank[3][:]).then_inc(y_ready.sem, 1)
                    act.wait_ge(*zT_psum(i, 1))
                    act.copy(wide(zT), bank[1][:]).then_inc(zT_ready.sem, 1)
                    act.wait_ge(*lnT_psum(i, 2))
                    act.copy(wide(ln2T), bank[7][:]).then_inc(lnT_ready.sem, 1)
                    act.wait_ge(*q_min_ready(i, 1))
                    act.activation(wide(q_exp), wide(q_min), ACT.Exp).then_inc(q_exp_ready.sem, 1)
                    act.wait_ge(*gate_psum(i, 1))
                    for k in range(KT):
                        last = act.activation(gate[:, k, :], bank[3][:, k * SEQ:(k + 1) * SEQ], ACT.Tanh,
                                              bias=hbg[:, k:k + 1], scale=0.5)
                    last.then_inc(gate_tanh.sem, 1)

            @block.vector
            def _(dve):
                dve.wait_ge(logw_exp.sem, 1)
                dve.tensor_scalar(logw[:], logw[:], -1.0, None, ALU.mult).then_inc(logw_ready.sem, 1)
                dve.tensor_scalar(hbg[:], cols["xbg"][:], 0.5, None, ALU.mult).then_inc(logw_ready.sem, 1)
                for h in range(HEADS):
                    dve.wait_ge(decay_strict.sem, h + 1)
                    dve.scalar_tensor_tensor(decay[:, h, :], diag[:], faaaa[:, h:h + 1], decay[:, h, :], ALU.mult,
                                             ALU.add).then_inc(decay_ready.sem, 1)
                dve.wait_ge(zeroed.sem, 6)
                dve.wait_ge(decay_ready.sem, HEADS)
                dve.wait_ge(x_loaded.sem, 16)
                dve.sem_inc(batch_done.sem, 1)
                with dve.Fori(0, BATCH) as i:
                    n = [0]

                    def step(ins):
                        n[0] += 1
                        ins.then_inc(vstep.sem, 1)
                        dve.wait_ge(*vstep(i, n[0]))

                    def layer_norm(src, k):
                        for j in range(TOK):
                            last = dve.bn_stats(stats[:, j, :], src(j))
                        step(last)
                        dve.memset(wait_pad[:], 0.0)
                        for j in range(TOK):
                            last = dve.bn_aggr(mean_var[:, j, :], stats[:, j, :])
                        last.then_inc(stats_ready.sem, 1)
                        dve.wait_ge(*rstd_ready(i, k))
                        for j in range(TOK):
                            last = dve.tensor_scalar(lnx[:, j, :], src(j), mean_var[:, j, 0:1], rstd[:, j:j + 1],
                                                     ALU.subtract, ALU.mult)
                        last.then_inc(ln_ready.sem, 1)

                    layer_norm(lambda j: x_all[:, TOK * i + j, :], 1)
                    for t in range(CTILES + 1):
                        if t < CTILES:
                            m, s = rows(t), t % 2
                            dve.wait_ge(*ctx_psum(i, t + 1))
                            dve.tensor_scalar(k_min[0:m, s, :], bank[5 + s][0:m, 0:DIM], 0.0, None,
                                              ALU.min).then_inc(k_min_ready.sem, 1)
                        if t >= 1:
                            m, s = rows(t - 1), (t - 1) % 2
                            dve.wait_ge(*k_exp_ready(i, t))
                            if t >= 3:
                                dve.wait_ge(*kv_added(i, t - 2))
                            dve.scalar_tensor_tensor(k_feat[0:m, s, :], bank[5 + s][0:m, 0:DIM], 0.0, k_exp[0:m, s, :],
                                                     ALU.max, ALU.add).then_inc(k_feat_ready.sem, 1)
                    dve.wait_ge(*kv_added(i, CTILES))
                    for h in range(KT):
                        dve.tensor_tensor(kv_m[:, h, :], bank[3 + h][:, 0:P], blk16[:], ALU.mult)
                        last = dve.tensor_copy(ks_col[:, h:h + 1], bank[3 + h][:, P:P + 1])
                    step(last)
                    for h in range(KT):
                        last = dve.tensor_scalar(ks_m[:, h, :], blk16[:], ks_col[:, h:h + 1], None, ALU.mult)
                    last.then_inc(kv_ready.sem, 1)

                    dve.wait_ge(*lnT_ready(i, 1))
                    step(dve.tensor_tensor(diff[:], lnT[:, :, 0:SEQ], lnT[:, :, 1:], ALU.subtract))
                    for name in "krvg":
                        for k in range(KT):
                            last = dve.scalar_tensor_tensor(mix[name][:, k, :], diff[:, k, :], cols["maa_" + name][:, k:k + 1],
                                                            lnT[:, k, 1:], ALU.mult, ALU.add)
                        last.then_inc(mix_ready.sem, 1)
                    dve.wait_ge(*proj_read(i, 4))
                    dve.scalar_tensor_tensor(wide(g_silu), wide(g_tanh), 1.0, bank[0][:], ALU.add,
                                             ALU.mult).then_inc(g_ready.sem, 1)
                    for n_, (half, h) in enumerate(ORDER):
                        dve.wait_ge(*score_psum(i, n_ + 1))
                        if n_ >= ATTS:
                            dve.wait_ge(*group_added(i, (n_ - ATTS) // 4 + 1))
                        dve.tensor_tensor(att[:, n_ % ATTS, :], bank[(1, 2, 7)[n_ % RING]][:, 0:SC], decay[:, half * 16 + h, :],
                                          ALU.mult).then_inc(att_ready.sem, 1)
                    dve.wait_ge(*yt_psum(i, 1))
                    y4 = bank[4][:].rearrange("p (g e) -> p g e", e=HD)

                    def over(t):
                        return t[:].unsqueeze(2).to_broadcast([P, TOK * HEADS, HD])

                    step(dve.tensor_reduce(g_mean[:], y4, AX.X, ALU.add))
                    step(dve.tensor_scalar(g_mean[:], g_mean[:], 1.0 / HD, None, ALU.mult))
                    step(dve.tensor_tensor(y_c[:], y4, over(g_mean), ALU.subtract))
                    step(dve.tensor_tensor(y_sq[:], y_c[:], y_c[:], ALU.mult))
                    dve.tensor_reduce(g_var[:], y_sq[:], AX.X, ALU.add).then_inc(gvar_ready.sem, 1)
                    dve.wait_ge(*grstd_ready(i, 1))
                    step(dve.tensor_tensor(y_c[:], y_c[:], over(g_rstd), ALU.mult))
                    y2 = y_c[:].rearrange("p (j h) e -> p j (h e)", j=TOK)
                    step(dve.scalar_tensor_tensor(y2, y2, HD ** 0.5, gamma[:].unsqueeze(1).to_broadcast([P, TOK, DIM]),
                                                  ALU.mult, ALU.mult))
                    step(dve.tensor_tensor(y2, y2, beta[:].unsqueeze(1).to_broadcast([P, TOK, DIM]), ALU.add))
                    dve.wait_ge(*g_ready(i, 1))
                    dve.scalar_tensor_tensor(y2, y2, 0.5, g_silu[:], ALU.mult, ALU.mult).then_inc(z_ready.sem, 1)
                    dve.wait_ge(*o_psum(i, 1))
                    for j in range(TOK):
                        last = dve.tensor_tensor(x1[:, j, :], x_all[:, TOK * i + j, :], bank[2][:, j * DIM:(j + 1) * DIM], ALU.add)
                    step(last)

                    layer_norm(lambda j: x1[:, j, :], 2)
                    dve.wait_ge(*q_psum(i, 1))
                    dve.tensor_scalar(wide(q_min), bank[1][:], 0.0, None, ALU.min).then_inc(q_min_ready.sem, 1)
                    dve.wait_ge(*q_exp_ready(i, 1))
                    dve.scalar_tensor_tensor(wide(q_feat), bank[1][:], 0.0, wide(q_exp), ALU.max,
                                             ALU.add).then_inc(q_feat_ready.sem, 1)
                    dve.wait_ge(*den_psum(i, 1))
                    step(dve.tensor_scalar(wide(den), bank[0][:], ZEPS, None, ALU.add))
                    step(dve.reciprocal(wide(den), wide(den)))
                    dve.wait_ge(*num_psum(i, 1))
                    step(dve.tensor_tensor(wide(den), wide(den), bank[4][:], ALU.mult))
                    dve.wait_ge(*gate_tanh(i, 1))
                    step(dve.tensor_scalar(wide(gate), wide(gate), 0.5, 0.5, ALU.mult, ALU.add))
                    dve.tensor_tensor(wide(aT), wide(den), wide(gate), ALU.mult).then_inc(aT_ready.sem, 1)
                    dve.wait_ge(*xo_psum(i, 1))
                    for j in range(TOK):
                        last = dve.tensor_tensor(x_all[:, TOK * i + j, :], x1[:, j, :], bank[2][:, j * DIM:(j + 1) * DIM], ALU.add)
                    last.then_inc(batch_done.sem, 1)
                    assert n[0] == VSTEPS

            @block.tensor
            def _(pe):
                def transposed(dst, src, part):
                    for a in range(KT):
                        for b in range(TOK):
                            last = pe.transpose(dst[:, a * SEQ + b * P:a * SEQ + (b + 1) * P], src[:, b, a * P:(a + 1) * P], ident[:])
                    return last

                def channels_out(dst, weight, act_t):
                    for a in range(KT):
                        for k in range(KT):
                            last = pe.matmul(dst[:, a * SEQ:(a + 1) * SEQ], weight[:, k, a * P:(a + 1) * P], act_t[:, k, :],
                                             start=(k == 0), stop=(k == KT - 1))
                    return last

                def tokens_out(dst, weight, act_t):
                    for j in range(TOK):
                        for k in range(KT):
                            last = pe.matmul(dst[:, j * DIM:(j + 1) * DIM], act_t[:, k, j * P:(j + 1) * P], weight[:, k, :],
                                             start=(k == 0), stop=(k == KT - 1))
                    return last

                pe.wait_ge(x_loaded.sem, 16 * 2)
                pe.wait_ge(weights_in.sem, 16 * len(weights_list))
                with pe.Fori(0, BATCH) as i:
                    def add_kv(t):
                        m, s = rows(t), t % 2
                        pe.wait_ge(*k_feat_ready(i, t + 1))
                        pe.wait_ge(*v_ready(i, t + 1))
                        for h in range(KT):
                            last = pe.matmul(bank[3 + h][:, 0:P + 1], k_feat[0:m, s, h * P:(h + 1) * P], v_ones[0:m, s, h, :],
                                             start=(t == 0), stop=(t == CTILES - 1))
                        last.then_inc(kv_added.sem, 1)

                    pe.wait_ge(*batch_done(i, 1))
                    pe.wait_ge(*ctx_in(i, 16))
                    for t in range(CTILES):
                        m = rows(t)
                        if t >= 2:
                            add_kv(t - 2)
                        for k in range(KT):
                            last = pe.matmul(bank[5 + t % 2][0:m, :], ctxT[:, k, t * P:t * P + m], w["XWkvT"][:, k, :],
                                             start=(k == 0), stop=(k == KT - 1))
                        last.then_inc(ctx_psum.sem, 1)
                    add_kv(CTILES - 2)
                    add_kv(CTILES - 1)

                    pe.wait_ge(*ln_ready(i, 1))
                    transposed(bank[0], lnx, 0).then_inc(lnT_psum.sem, 1)
                    for n_, (name, dst) in enumerate((("k", 1), ("r", 2))):
                        pe.wait_ge(*mix_ready(i, n_ + 1))
                        channels_out(bank[dst], w[f"W{name}T"], mix[name]).then_inc(proj_psum.sem, 1)
                    for n_, (name, dst) in enumerate((("v", 7), ("g", 0))):
                        pe.wait_ge(*mix_ready(i, n_ + 3))
                        tokens_out(bank[dst], w[f"W{name}T"], mix[name]).then_inc(proj_psum.sem, 1)

                    def add_group(n_):
                        pe.wait_ge(*att_ready(i, n_ + 4))
                        half, m = ORDER[n_][0], ORDER[n_][1] % 4
                        for j in range(TOK):
                            for q in range(4):
                                a = att[:, (n_ + q) % ATTS, j * SEQ:j * SEQ + SEQ - j * P]
                                last = pe.matmul(bank[3][32 * q:32 * q + 32, half * SEQ + j * P:(half + 1) * SEQ],
                                                 v_pad[:, j, half * 4 + q, 32 * m:32 * m + 32], a,
                                                 start=(m == 0 and j == 0), stop=(m == 3 and j == TOK - 1))
                        last.then_inc(group_added.sem, 1)

                    pe.wait_ge(*kv_ready(i, 1))
                    pe.wait_ge(*proj_read(i, 3))
                    for n_, (half, h) in enumerate(ORDER):
                        pe.wait_ge(*r_head_ready(i, n_ + 1))
                        if n_ >= RING:
                            pe.wait_ge(*att_ready(i, n_ - RING + 1))
                        b, r = bank[(1, 2, 7)[n_ % RING]], r_head[:, n_ % ATTS, :]
                        pe.matmul(b[:, 0:SEQ], k_sb[:, half, 0:P], r, start=True, stop=True)
                        pe.matmul(b[:, SEQ:SC], k_sb[:, half, P:SEQ], r[:, P:SEQ], start=True,
                                  stop=True).then_inc(score_psum.sem, 1)
                        if n_ >= 5 and (n_ - 5) % 4 == 0:
                            add_group(n_ - 5)
                    add_group(28)
                    pe.wait_ge(*y_ready(i, 1))
                    for j in range(TOK):
                        for a in range(KT):
                            last = pe.transpose(bank[4][:, j * DIM + a * P:j * DIM + (a + 1) * P], y_sb[:, a, j * P:(j + 1) * P], ident[:])
                    last.then_inc(yt_psum.sem, 1)
                    pe.wait_ge(*z_ready(i, 1))
                    transposed(bank[1], y_c[:].rearrange("p (j h) e -> p j (h e)", j=TOK), 1).then_inc(zT_psum.sem, 1)
                    pe.wait_ge(*zT_ready(i, 1))
                    tokens_out(bank[2], w["WoT"], zT).then_inc(o_psum.sem, 1)

                    pe.wait_ge(*ln_ready(i, 2))
                    transposed(bank[7], lnx, 2).then_inc(lnT_psum.sem, 1)
                    pe.wait_ge(*lnT_ready(i, 2))
                    channels_out(bank[1], w["XWqT"], ln2T).then_inc(q_psum.sem, 1)
                    channels_out(bank[3], w["XWgT"], ln2T).then_inc(gate_psum.sem, 1)
                    pe.wait_ge(*q_feat_ready(i, 1))
                    for h in range(KT):
                        last = pe.matmul(bank[0][:, h * SEQ:(h + 1) * SEQ], ks_m[:, h, :], q_feat[:, h, :], start=True, stop=True)
                    last.then_inc(den_psum.sem, 1)
                    for h in range(KT):
                        last = pe.matmul(bank[4][:, h * SEQ:(h + 1) * SEQ], kv_m[:, h, :], q_feat[:, h, :], start=True, stop=True)
                    last.then_inc(num_psum.sem, 1)
                    pe.wait_ge(*aT_ready(i, 1))
                    tokens_out(bank[2], w["XWoT"], aT).then_inc(xo_psum.sem, 1)




def experts(nc, d, x_all, x_loaded, ident, lut_w):
    EXPERTS, INNER, TOP_P = 8, 512, 0.9
    N = BATCH * TOK
    IT = INNER // P
    PAIR = 2
    HALF = N * P // 2
    UNITS = PAIR * 2 * IT
    with ExitStack() as ctx:
        def sb(name, shape, dt=F32):
            return ctx.enter_context(nc.sbuf_tensor(name, shape, dt))

        def sig(name, per=0):
            return Signal(ctx.enter_context(nc.semaphore(name)), per)

        bank = [ctx.enter_context(nc.psum_tensor(f"b_bank{n}", [P, 512], F32)) for n in range(8)]
        gate_w, up_w = sb("gate_w", [P, PAIR, KT, INNER]), sb("up_w", [P, PAIR, KT, INNER])
        down_w = sb("down_w", [P, PAIR, IT, DIM])
        router = sb("router", [P, KT, EXPERTS])
        earlier = sb("earlier", [P, EXPERTS, EXPERTS])
        stats, mean_var = sb("b_stats", [P, N, 6]), sb("b_mean_var", [P, N, 2])
        eps, half_neg, var_eps, rstd = (sb("b_" + n, [P, N]) for n in ("eps", "half_neg", "var_eps", "rstd"))
        lnx, lnT = sb("b_lnx", [P, N, DIM]), sb("b_lnT", [P, KT, N * P])
        top, total = sb("r_top", [P, N]), sb("r_total", [P, N])
        prob, before = sb("prob", [P, N, EXPERTS]), sb("before", [P, N, EXPERTS])
        above, above_eq = sb("above", [P, N, EXPERTS, EXPERTS]), sb("above_eq", [P, N, EXPERTS, EXPERTS])
        weight = sb("weight", [P, EXPERTS, N])
        weight_e = sb("weight_e", [P, PAIR, N])
        g_tanh, g_silu = sb("b_g_tanh", [P, 2, HALF]), sb("b_g_silu", [P, 2, HALF])
        hidden = sb("hidden", [P, 2, IT, HALF])
        LUT, LUT_COLS = 16, 3 * 6 * DIM
        PER_PASS, SLICES = LUT // (EXPERTS // PAIR), 4
        lut_idx, lut_hit = sb("lut_idx", [P, LUT_COLS], I32), sb("lut_hit", [P, LUT_COLS // SLICES])
        lut_val, lut_key = sb("lut_val", [P, LUT]), sb("lut_key", [P, LUT])
        val_now, key_now = sb("val_now", [P, PER_PASS]), sb("key_now", [P, PER_PASS])
        lut_flat = lut_w["all"]

        const_in, set_ = sig("b_const_in"), sig("b_set")
        stats_ready, rstd_ready, ln_ready, lnT_psum, lnT_ready = (sig("b_" + n) for n in (
            "stats_ready", "rstd_ready", "ln_ready", "lnT_psum", "lnT_ready"))
        logit_psum, shifted, prob_exp, router_done = (sig(n) for n in ("logit_psum", "shifted", "prob_exp", "router_done"))
        pool_step, prologue_step = sig("b_pool_step"), sig("b_prologue_step")
        gate_in, up_in, down_in = ([sig(f"{n}_in{e}", 16) for e in range(PAIR)] for n in ("gate", "up", "down"))
        start = sig("b_start", 1)
        expert_done = sig("expert_done", PAIR)
        gate_psum, gate_tanh, gate_silu, hidden_ready = (sig("b_" + n, UNITS) for n in (
            "gate_psum", "gate_tanh", "gate_silu", "hidden_ready"))
        weight_ready = sig("weight_ready", PAIR)
        lut_now, lut_hit_ready, lut_added = sig("lut_now", 1), sig("lut_hit_ready", UNITS), sig("lut_added", UNITS)
        y_psum, y_added = sig("y_psum", UNITS // 2), sig("y_added", UNITS // 2)

        with nc.Block() as block:
            @block.sync
            def _(sp):
                sp.dma_start(router[:], d["routerT"].rearrange("(k p) e -> p k e", p=P)).then_inc(const_in.sem, 16)
                sp.dma_start(earlier[:], d["earlier"].partition_broadcast(P)).then_inc(const_in.sem, 16)
                sp.dma_start(lut_val[:], d["lut"].partition_broadcast(P)).then_inc(const_in.sem, 16)
                sp.dma_start(lut_key[:], d["lut_key"].partition_broadcast(P)).then_inc(const_in.sem, 16)
                for n, name in enumerate(("gate_idx", "up_idx")):
                    sp.dma_start(lut_idx[:, n * 6 * DIM:(n + 1) * 6 * DIM].rearrange("p (k n) -> p k n", k=KT),
                                 d[name].rearrange("(k p) n -> p k n", p=P)).then_inc(const_in.sem, 16)
                sp.dma_start(lut_idx[:, 12 * DIM:].rearrange("p (c n) -> p c n", c=6),
                             d["down_idx"].rearrange("(c p) n -> p c n", p=P)).then_inc(const_in.sem, 16)
                with sp.Fori(0, EXPERTS // PAIR) as i:
                    for e in range(PAIR):
                        if e == 0:
                            sp.wait_ge(*start(i, 1))
                        else:
                            sp.wait_ge(*start(i, 1))
                        sp.dma_start(gate_w[:, e], d["gateT"][i * PAIR + e].rearrange("(k p) n -> p k n", p=P)).then_inc(gate_in[e].sem, 16)
                        sp.dma_start(up_w[:, e], d["upT"][i * PAIR + e].rearrange("(k p) n -> p k n", p=P)).then_inc(up_in[e].sem, 16)
                        sp.dma_start(down_w[:, e], d["downT"][i * PAIR + e].rearrange("(k p) n -> p k n", p=P)).then_inc(down_in[e].sem, 16)

            @block.gpsimd
            def _(pool):
                pool.memset(eps[:], LN_EPS).then_inc(set_.sem, 1)
                pool.memset(half_neg[:], -0.5).then_inc(set_.sem, 1)
                pool.wait_ge(set_.sem, 2)
                pool.wait_ge(stats_ready.sem, 1)
                pool.tensor_tensor(var_eps[:], mean_var[:, :, 1], eps[:], ALU.add).then_inc(pool_step.sem, 1)
                pool.wait_ge(pool_step.sem, 1)
                pool.tensor_tensor(rstd[:], var_eps[:], half_neg[:], ALU.pow).then_inc(rstd_ready.sem, 1)

            @block.scalar
            def _(act):
                for n in range(4):
                    k, h = n // 2, n % 2
                    act.wait_ge(lnT_psum.sem, n + 1)
                    act.copy(lnT[:, k, h * HALF:(h + 1) * HALF], bank[n][:]).then_inc(lnT_ready.sem, 1)
                act.wait_ge(shifted.sem, 1)
                act.activation(prob[:], prob[:], ACT.Exp).then_inc(prob_exp.sem, 1)
                with act.Fori(0, EXPERTS // PAIR) as i:
                    for u in range(UNITS):
                        act.wait_ge(*gate_psum(i, u + 1))
                        if u >= 2:
                            act.wait_ge(*gate_silu(i, u - 1))
                        act.activation(g_tanh[:, u % 2], bank[u % 2][:], ACT.Tanh, scale=0.5).then_inc(gate_tanh.sem, 1)

            @block.vector
            def _(dve):
                n_ = [0]

                def step(ins):
                    n_[0] += 1
                    ins.then_inc(prologue_step.sem, 1)
                    dve.wait_ge(prologue_step.sem, n_[0])

                for n in range(N):
                    last = dve.bn_stats(stats[:, n, :], x_all[:, n, :])
                step(last)
                for n in range(N):
                    last = dve.bn_aggr(mean_var[:, n, :], stats[:, n, :])
                last.then_inc(stats_ready.sem, 1)
                dve.wait_ge(rstd_ready.sem, 1)
                for n in range(N):
                    dve.tensor_scalar(lnx[:, n, :], x_all[:, n, :], mean_var[:, n, 0:1], rstd[:, n:n + 1],
                                      ALU.subtract, ALU.mult).then_inc(ln_ready.sem, 1)
                dve.wait_ge(logit_psum.sem, 1)
                logits = bank[4][:, 0:N * EXPERTS].rearrange("p (n e) -> p n e", e=EXPERTS)
                step(dve.tensor_reduce(top[:], logits, AX.X, ALU.max))
                dve.tensor_tensor(prob[:], logits, top[:].unsqueeze(2).to_broadcast([P, N, EXPERTS]),
                                  ALU.subtract).then_inc(shifted.sem, 1)
                dve.wait_ge(prob_exp.sem, 1)
                step(dve.tensor_reduce(total[:], prob[:], AX.X, ALU.add))
                step(dve.reciprocal(total[:], total[:]))
                step(dve.tensor_tensor(prob[:], prob[:], total[:].unsqueeze(2).to_broadcast([P, N, EXPERTS]), ALU.mult))
                dve.wait_ge(const_in.sem, 112)
                for n in range(N):
                    pj = prob[:, n].unsqueeze(1).to_broadcast([P, EXPERTS, EXPERTS])
                    pe = prob[:, n].unsqueeze(2).to_broadcast([P, EXPERTS, EXPERTS])
                    dve.tensor_tensor(above[:, n], pj, pe, ALU.is_gt)
                    last = dve.tensor_tensor(above_eq[:, n], pj, pe, ALU.is_ge)
                step(last)
                for n in range(N):
                    last = dve.tensor_tensor(above_eq[:, n], above_eq[:, n], earlier[:], ALU.mult)
                step(last)
                step(dve.tensor_tensor(above[:].rearrange("p a b c -> p (a b c)"), above[:].rearrange("p a b c -> p (a b c)"),
                                       above_eq[:].rearrange("p a b c -> p (a b c)"), ALU.max))
                for n in range(N):
                    pj = prob[:, n].unsqueeze(1).to_broadcast([P, EXPERTS, EXPERTS])
                    last = dve.tensor_tensor(above[:, n], above[:, n], pj, ALU.mult)
                step(last)
                step(dve.tensor_reduce(before[:], above[:], AX.X, ALU.add))
                step(dve.memset(lut_flat[:], 0.0))
                step(dve.scalar_tensor_tensor(weight[:].rearrange("p e n -> p n e"), before[:], TOP_P, prob[:], ALU.is_le, ALU.mult))
                dve.sem_inc(start.sem, 1)
                with dve.Fori(0, EXPERTS // PAIR) as i:
                    def add_y(h):
                        for b in range(2):
                            dve.wait_ge(*y_psum(i, 2 * h + b + 1))
                            for t in range(2):
                                n = (h % 2) * 4 + b * 2 + t
                                last = dve.scalar_tensor_tensor(x_all[:, n, :], bank[4 + b][:, t * DIM:(t + 1) * DIM],
                                                                weight_e[:, h // 2, n:n + 1], x_all[:, n, :], ALU.mult, ALU.add)
                            last.then_inc(y_added.sem, 1)

                    dve.tensor_copy(weight_e[:], weight[:, bass.ds(i * PAIR, PAIR), :]).then_inc(weight_ready.sem, PAIR)
                    dve.tensor_copy(val_now[:], lut_val[:, bass.ds(i * PER_PASS, PER_PASS)])
                    dve.tensor_copy(key_now[:], lut_key[:, bass.ds(i * PER_PASS, PER_PASS)]).then_inc(lut_now.sem, 1)
                    dve.wait_ge(*weight_ready(i, PAIR))
                    dve.wait_ge(*lut_now(i, 1))
                    for u in range(UNITS):
                        h = u // IT
                        dve.wait_ge(*gate_tanh(i, u + 1))
                        dve.scalar_tensor_tensor(g_silu[:, u % 2], g_tanh[:, u % 2], 1.0, bank[u % 2][:], ALU.add,
                                                 ALU.mult).then_inc(gate_silu.sem, 1)
                        dve.wait_ge(*gate_silu(i, u + 1))
                        dve.scalar_tensor_tensor(hidden[:, h % 2, u % IT, :], g_silu[:, u % 2], 0.5, bank[2 + u % 2][:],
                                                 ALU.mult, ALU.mult).then_inc(hidden_ready.sem, 1)
                        v, part = u // SLICES, slice(u % SLICES * (LUT_COLS // SLICES), (u % SLICES + 1) * (LUT_COLS // SLICES))
                        dve.tensor_scalar(lut_hit[:], lut_idx[:, part], key_now[:, v:v + 1], val_now[:, v:v + 1],
                                          ALU.is_equal, ALU.mult).then_inc(lut_hit_ready.sem, 1)
                        if u % IT == 1 and h >= 1:
                            add_y(h - 1)
                        dve.wait_ge(*lut_hit_ready(i, u + 1))
                        dve.tensor_tensor(lut_flat[:, part], lut_flat[:, part], lut_hit[:], ALU.add).then_inc(lut_added.sem, 1)
                        dve.wait_ge(*lut_added(i, u + 1))
                    add_y(UNITS // IT - 1)
                    dve.wait_ge(*y_added(i, UNITS // 2))
                    dve.sem_inc(start.sem, 1)

            @block.tensor
            def _(pe):
                for n in range(4):
                    k, h = n // 2, n % 2
                    for t in range(4):
                        pe.wait_ge(ln_ready.sem, h * 4 + t + 1)
                        last = pe.transpose(bank[n][:, t * P:(t + 1) * P], lnx[:, h * 4 + t, k * P:(k + 1) * P], ident[:])
                    last.then_inc(lnT_psum.sem, 1)
                pe.wait_ge(lnT_ready.sem, 4)
                pe.wait_ge(const_in.sem, 112)
                for n in range(N):
                    for k in range(KT):
                        last = pe.matmul(bank[4][:, n * EXPERTS:(n + 1) * EXPERTS], lnT[:, k, n * P:(n + 1) * P], router[:, k, :],
                                         start=(k == 0), stop=(k == KT - 1))
                last.then_inc(logit_psum.sem, 1)
                pe.wait_ge(start.sem, 1)
                with pe.Fori(0, EXPERTS // PAIR) as i:
                    def down(h):
                        pe.wait_ge(*hidden_ready(i, IT * (h + 1)))
                        pe.wait_ge(*down_in[h // 2](i, 16))
                        for b in range(2):
                            if h >= 1:
                                pe.wait_ge(*y_added(i, 2 * (h - 1) + b + 1))
                            for t in range(2):
                                for c in range(IT):
                                    last = pe.matmul(bank[4 + b][:, t * DIM:(t + 1) * DIM],
                                                     hidden[:, h % 2, c, (b * 2 + t) * P:(b * 2 + t + 1) * P],
                                                     down_w[:, h // 2, c, :], start=(c == 0), stop=(c == IT - 1))
                            last.then_inc(y_psum.sem, 1)

                    pe.wait_ge(*start(i, 1))
                    for u in range(UNITS):
                        e, h, c = u // (2 * IT), (u // IT) % 2, u % IT
                        if c == 0 and h == 0:
                            pe.wait_ge(*gate_in[e](i, 16))
                            pe.wait_ge(*up_in[e](i, 16))
                        if u >= 2:
                            pe.wait_ge(*hidden_ready(i, u - 1))
                        for w, b in ((gate_w, 0), (up_w, 2)):
                            for k in range(KT):
                                last = pe.matmul(bank[b + u % 2][:], w[:, e, k, c * P:(c + 1) * P], lnT[:, k, h * HALF:(h + 1) * HALF],
                                                 start=(k == 0), stop=(k == KT - 1))
                        last.then_inc(gate_psum.sem, 1)
                        if c == 0 and u >= IT:
                            down(u // IT - 1)
                    down(UNITS // IT - 1)


def fast_weights_softmax_and_lut(nc, d, out, x_all, x_loaded, ident, lut_w):
    HEADS, HD = 16, 16
    QK_SCALE = 1.0 / HD ** 0.5
    FW_EPS, L2_EPS = 1e-6, 1e-5
    GROUP = 4
    GROUPS = HEADS // GROUP
    PARTS = 3
    TERMS = 6
    STACK = TERMS * HD
    DEEP = STACK + PARTS
    CHUNK = 512
    CHUNKS = -(-CTX // CHUNK)
    IT = 6
    INNER = 688

    def width(c):
        return min(CHUNK, CTX - c * CHUNK)

    with ExitStack() as ctx:
        def sb(name, shape, dt=F32):
            return ctx.enter_context(nc.sbuf_tensor(name, shape, dt))

        def sig(name, per=0):
            return Signal(ctx.enter_context(nc.semaphore(name)), per)

        def psum(name, banks=1):
            return ctx.enter_context(nc.psum_tensor(name, [P, banks * 512], F32))

        bank = {0: psum("c_bank0"), 1: psum("c_bank1")}
        wide_bank = [psum("c_bank23", 2), psum("c_bank45", 2)]
        bank.update({6: psum("c_bank6"), 7: psum("c_bank7")})
        for n in range(4):
            bank[2 + n] = wide_bank[n // 2][:, n % 2 * 512:(n % 2 + 1) * 512]

        k_dram = nc.dram_tensor("k_parts", (PARTS, DIM, CTX), BF16, kind="Internal").ap()
        q_dram = nc.dram_tensor("q_parts", (PARTS, DIM, SEQ), BF16, kind="Internal").ap()

        w = {n: sb("c_" + n, [P, KT, DIM]) for n in ("FWq", "FWo", "CWq", "CWk", "CWv")}
        w["CWo"] = sb("c_CWo", [P, GROUPS, DIM])
        fast = {n: sb("c_" + n, [P, KT, P]) for n in ("w0T", "w1T", "w2T")}
        w_s, b_s = sb("w_s", [P, KT, 2]), sb("b_s", [P, 2])
        fw_g, fw_b, bv, bo = sb("fw_g", [P, P]), sb("fw_b", [P, P]), sb("bv", [P, DIM]), sb("bo", [P, DIM])
        bq, bk = sb("bq", [P, KT]), sb("bk", [P, KT])
        sel = sb("sel", [P, P])
        ident_b = sb("ident_b", [P, P], BF16)
        ctxT = sb("c_ctxT", [P, KT, CTX])
        stats, mean_var = sb("c_stats", [P, 4, 6]), sb("c_mean_var", [P, 4, 2])
        var_eps, rstd, half_neg, half_pos = (sb("c_" + n, [P, 4]) for n in ("var_eps", "rstd", "half_neg", "half_pos"))
        eps, fw_eps, l2_eps = (sb("c_" + n, [P, 4]) for n in ("eps", "fw_eps", "l2_eps"))
        wait_pad = sb("c_wait_pad", [P, 1])
        lnx, lnT = sb("c_lnx", [P, TOK, DIM]), sb("c_lnT", [P, KT, SEQ])
        q_tanh, q_silu, q_sq = (sb("c_" + n, [P, 4, P]) for n in ("q_tanh", "q_silu", "q_sq"))
        q_norm = sb("q_norm", [P, 4])
        qT = sb("c_qT", [P, TOK, P, 2])
        f_tanh, f_silu, f_h = (sb("c_" + n, [P, 2 * SEQ]) for n in ("f_tanh", "f_silu", "f_h"))
        s_in, s_tanh = sb("s_in", [P, 4]), sb("s_tanh", [P, 4])
        fo, foT = sb("fo", [P, 4, P]), sb("foT", [P, KT, SEQ])
        x4, x5, x6 = (sb(n, [P, TOK, DIM]) for n in ("x4", "x5", "x6"))
        k_full = sb("k_full", [P, 2, CHUNK])
        k_part = sb("k_part", [P, 2, PARTS, CHUNK], BF16)
        q_full, q_part = sb("q_full", [P, KT, SEQ]), sb("q_part", [P, PARTS, KT, SEQ], BF16)
        v_sb = sb("c_v", [P, CTILES, HEADS, 32])
        k_stack = sb("k_stack", [P, 2, GROUP, CTX], BF16)
        q_stack = sb("q_stack", [P, HEADS, SEQ], BF16)
        chunk_max = sb("chunk_max", [P, 2 * GROUP, CHUNKS])
        neg_max = sb("neg_max", [P, 2 * GROUP])
        max_part = sb("max_part", [P, TOK, PARTS, GROUP], BF16)
        max_row = sb("max_row", [PARTS * GROUP, SEQ], BF16)
        probs = sb("probs", [P, 2, GROUP, 2, SEQ])
        u_sb, den = sb("u_sb", [P, SEQ]), sb("c_den", [P, SEQ])
        attT = sb("attT", [P, GROUPS, SEQ])
        gu = sb("gu", [P, IT, SEQ])

        const_in, weights_in, set_, ones_set = sig("c_const_in"), sig("c_weights_in"), sig("c_set"), sig("c_ones_set")
        VSTEPS, GSTEPS = 58, 5
        vstep, gstep = sig("c_vstep", VSTEPS), sig("c_gstep", GSTEPS)
        batch_done, stored = sig("c_batch_done", 1), sig("c_stored", 16)
        ctx_in = sig("c_ctx_in", 16)
        k_psum, k_full_ready, k_parts_ready = (sig("c_" + n, 2 * CHUNKS) for n in ("k_psum", "k_full_ready", "k_parts_ready"))
        k_written = [sig(f"k_written{n}", 16 * CHUNKS) for n in range(2)]
        v_psum, v_ready = sig("c_v_psum", 7), sig("c_v_ready", 7)
        stats_ready, rstd_ready, norm_ready = sig("c_stats_ready", 5), sig("c_rstd_ready", 5), sig("c_norm_ready", 3)
        lnT_psum, lnT_ready = sig("c_lnT_psum", 3), sig("c_lnT_ready", 3)
        fq_psum, fq_tanh, fq_ready, fqT_psum, fqT_ready = (sig(n, 1) for n in ("fq_psum", "fq_tanh", "fq_ready", "fqT_psum", "fqT_ready"))
        s_psum, s_in_ready, s_tanh_ready = (sig(n, 1) for n in ("s_psum", "s_in_ready", "s_tanh_ready"))
        fg_psum, fg_tanh, fh_ready, fo_psum, fo_ready = (sig(n, 1) for n in ("fg_psum", "fg_tanh", "fh_ready", "fo_psum", "fo_ready"))
        foT_psum, foT_ready, fwo_psum = (sig(n, 1) for n in ("foT_psum", "foT_ready", "fwo_psum"))
        q_psum, q_parts_ready = sig("c_q_psum", 1), sig("c_q_parts_ready", 1)
        q_written, q_stacked = sig("q_written", 32), sig("q_stacked", 16 * TERMS)
        k_stacked = [sig(f"k_stacked{n}", 2 * 16 * TERMS) for n in range(2)]
        max_psum, max_read = sig("max_psum", GROUPS * 2 * GROUP * CHUNKS), sig("max_read", GROUPS * 2 * GROUP * CHUNKS)
        max_part_ready, max_row_psum, max_row_ready = (sig(n, GROUPS) for n in ("max_part_ready", "max_row_psum", "max_row_ready"))
        max_stacked = sig("max_stacked", GROUPS * 48)
        STEPS = 13
        score_psum, prob_ready = sig("c_score_psum", GROUPS * STEPS), sig("c_prob_ready", GROUPS * STEPS)
        tiles_added = sig("tiles_added", GROUPS * 7)
        u_ready, den_psum, head_ready = sig("u_ready", GROUPS), sig("c_den_psum", GROUPS), sig("head_ready", GROUPS)
        co_psum = sig("co_psum", 1)
        gu_psum, gu_tanh, gu_ready = sig("gu_psum", IT // 2), sig("gu_tanh", IT // 2), sig("gu_ready", IT // 2)
        ffn_psum = sig("ffn_psum", 1)

        def wide(t):
            return t[:].rearrange("p a b -> p (a b)")

        consts_list = ([(fast[n], d[n].rearrange("g d e -> d g e")) for n in fast]
                       + [(w_s, d["w_s"].rearrange("(k p) n -> p k n", p=P)), (b_s, d["b_s"].partition_broadcast(P)),
                          (fw_g, d["fw_g"].partition_broadcast(P)), (fw_b, d["fw_b"].partition_broadcast(P)),
                          (bv, d["bv"].partition_broadcast(P)), (bo, d["bo"].partition_broadcast(P)),
                          (bq, d["bq"]), (bk, d["bk"]), (sel, d["sel"])])
        w_names = list(w)

        def last_tile_rows(t):
            return rows(t)

        with nc.Block() as block:
            @block.sync
            def _(sp):
                sp.dma_start(ctxT[:], d["ctxT"][0].rearrange("(k p) s -> p k s", p=P)).then_inc(ctx_in.sem, 16)
                for n in w_names:
                    sp.dma_start(w[n][:], d[n].rearrange("(k p) n -> p k n", p=P)).then_inc(weights_in.sem, 16)
                for t, src in consts_list:
                    sp.dma_start(t[:], src).then_inc(const_in.sem, 16)

                def stack_k(i, g):
                    row = 0
                    for part, times in ((0, 3), (1, 2), (2, 1)):
                        for _ in range(1):
                            src = k_dram[part, g * GROUP * HD:(g + 1) * GROUP * HD, :].rearrange("(h e) s -> e h s", e=HD)
                            for r in range(times):
                                sp.dma_start(k_stack[row:row + HD, g % 2], src).then_inc(k_stacked[g % 2].sem, 16)
                                row += HD

                sp.sem_inc(stored.sem, 16)
                with sp.Fori(0, BATCH) as i:
                    for u in range(2 * CHUNKS):
                        a, c = u // CHUNKS, u % CHUNKS
                        sp.wait_ge(*k_parts_ready(i, u + 1))
                        sp.dma_start(k_dram[:, a * P:(a + 1) * P, c * CHUNK:c * CHUNK + width(c)].rearrange("n p s -> p n s"),
                                     k_part[:, u % 2, :, 0:width(c)]).then_inc(k_written[u % 2].sem, 16)
                    for s in range(2):
                        sp.wait_ge(*k_written[s](i, 16 * CHUNKS))
                    stack_k(i, 0)
                    stack_k(i, 1)
                    sp.wait_ge(*v_psum(i, 7))
                    sp.dma_start(ctxT[:], d["ctxT"][(i + 1) % BATCH].rearrange("(k p) s -> p k s", p=P)).then_inc(ctx_in.sem, 16)
                    sp.wait_ge(*q_parts_ready(i, 1))
                    for k in range(KT):
                        sp.dma_start(q_dram[:, k * P:(k + 1) * P, :].rearrange("n p s -> p n s"), q_part[:, :, k, :]).then_inc(q_written.sem, 16)
                    sp.wait_ge(*q_written(i, 32))
                    row = 0
                    for parts in (3, 2, 1):
                        for part in range(parts):
                            sp.dma_start(q_stack[row:row + HD], q_dram[part].rearrange("(h e) s -> e h s", e=HD)).then_inc(q_stacked.sem, 16)
                            row += HD
                    for g in range(GROUPS):
                        sp.wait_ge(*max_row_ready(i, g + 1))
                        for n in range(PARTS):
                            sp.dma_start(q_stack[STACK + n:STACK + n + 1, g * GROUP:(g + 1) * GROUP, :],
                                         max_row[n * GROUP:(n + 1) * GROUP, :]).then_inc(max_stacked.sem, 16)
                        if 1 <= g <= GROUPS - 2:
                            sp.wait_ge(*tiles_added(i, 7 * g))
                            stack_k(i, g + 1)
                    sp.wait_ge(*batch_done(i, 2))
                    sp.dma_start(out[i].rearrange("(j p) c -> p j c", p=P), x6[:]).then_inc(stored.sem, 16)
                sp.wait_ge(stored.sem, 16 * (BATCH + 1))
                sp.wait_ge(ctx_in.sem, 16 * (BATCH + 1))

            @block.gpsimd
            def _(pool):
                for t, v in ((eps, LN_EPS), (fw_eps, FW_EPS), (l2_eps, 2 * L2_EPS), (half_neg, -0.5), (half_pos, 0.5),
                             (v_sb[:, :, :, HD:], 0.0)):
                    pool.memset(t if isinstance(t, bass.AP) else t[:], v).then_inc(set_.sem, 1)
                pool.wait_ge(set_.sem, 6)
                pool.memset(v_sb[:, :, :, HD:HD + 1], 1.0).then_inc(set_.sem, 1)
                pool.tensor_copy(ident_b[:], ident[:]).then_inc(set_.sem, 1)
                with pool.Fori(0, BATCH) as i:
                    n = [0]

                    def step(ins):
                        n[0] += 1
                        ins.then_inc(gstep.sem, 1)
                        pool.wait_ge(*gstep(i, n[0]))

                    def rsqrt_var(k, cols, e):
                        pool.wait_ge(*stats_ready(i, k))
                        step(pool.tensor_tensor(var_eps[:, 0:cols], mean_var[:, 0:cols, 1], e[:, 0:cols], ALU.add))
                        pool.tensor_tensor(rstd[:, 0:cols], var_eps[:, 0:cols], half_neg[:, 0:cols], ALU.pow).then_inc(rstd_ready.sem, 1)

                    rsqrt_var(1, TOK, eps)
                    pool.wait_ge(*stats_ready(i, 2))
                    step(pool.tensor_tensor(q_norm[:], q_norm[:], half_pos[:], ALU.pow))
                    pool.tensor_tensor(q_norm[:], q_norm[:], l2_eps[:], ALU.add).then_inc(rstd_ready.sem, 1)
                    rsqrt_var(3, 4, fw_eps)
                    rsqrt_var(4, TOK, eps)
                    rsqrt_var(5, TOK, eps)
                    assert n[0] == GSTEPS

            @block.scalar
            def _(act):
                act.wait_ge(const_in.sem, 16 * len(consts_list))
                act.wait_ge(set_.sem, 8)
                with act.Fori(0, BATCH) as i:
                    for u in range(2 * CHUNKS):
                        a, c, s = u // CHUNKS, u % CHUNKS, u % 2
                        m = width(c)
                        act.wait_ge(*k_psum(i, u + 1))
                        if u >= 2:
                            act.wait_ge(*k_written[s](i, 16 * (u // 2)))
                        act.activation(k_full[:, s, 0:m], bank[6 + s][:, 0:m], ACT.Identity, bias=bk[:, a:a + 1])
                        act.activation(k_part[:, s, 0, 0:m], bank[6 + s][:, 0:m], ACT.Identity,
                                       bias=bk[:, a:a + 1]).then_inc(k_full_ready.sem, 1)

                    def copy_T(k, b):
                        act.wait_ge(*lnT_psum(i, k))
                        act.copy(wide(lnT), bank[b][:]).then_inc(lnT_ready.sem, 1)

                    copy_T(1, 0)
                    act.wait_ge(*fq_psum(i, 1))
                    act.activation(wide(q_tanh), bank[1][:], ACT.Tanh, scale=0.5).then_inc(fq_tanh.sem, 1)
                    act.wait_ge(*s_in_ready(i, 1))
                    act.activation(s_tanh[:], s_in[:], ACT.Tanh, scale=0.5).then_inc(s_tanh_ready.sem, 1)
                    act.wait_ge(*fqT_psum(i, 1))
                    for j in range(TOK):
                        last = act.copy(qT[:, j].rearrange("p t h -> p h t"),
                                        bank[2][:, j * SEQ:(j + 1) * SEQ].rearrange("p (h t) -> p h t", h=2))
                    last.then_inc(fqT_ready.sem, 1)
                    act.wait_ge(*fg_psum(i, 1))
                    act.activation(f_tanh[:], bank[4][:], ACT.Tanh, scale=0.5).then_inc(fg_tanh.sem, 1)
                    act.wait_ge(*foT_psum(i, 1))
                    act.copy(wide(foT), bank[0][:]).then_inc(foT_ready.sem, 1)
                    copy_T(2, 2)
                    for g in range(GROUPS):
                        for t in range(STEPS):
                            n = g * STEPS + t
                            m = P if t < STEPS - 1 else rows(CTILES - 1)
                            act.wait_ge(*score_psum(i, n + 1))
                            if g * 7 + t // 2 >= 2:
                                act.wait_ge(*tiles_added(i, g * 7 + t // 2 - 1))
                            if t < STEPS - 1:
                                dst = probs[:, (g * 7 + t // 2) % 2, t % 2 * 2:t % 2 * 2 + 2].rearrange("p h t s -> p (h t s)")
                            else:
                                dst = probs[0:m, (g * 7 + 6) % 2, :, 0, :]
                            src = wide_bank[n % 2][0:m, :]
                            if t == STEPS - 1:
                                src = src.rearrange("p (h s) -> p h s", h=GROUP)
                            act.activation(dst, src, ACT.Exp).then_inc(prob_ready.sem, 1)
                        act.wait_ge(*tiles_added(i, 7 * (g + 1)))
                        if g >= 1:
                            act.wait_ge(*head_ready(i, g))
                        act.copy(u_sb[:], bank[6][:, 0:SEQ]).then_inc(u_ready.sem, 1)
                    copy_T(3, 0)
                    for p in range(IT // 2):
                        act.wait_ge(*gu_psum(i, p + 1))
                        if p >= 1:
                            act.wait_ge(*gu_ready(i, p))
                        act.activation(f_tanh[:], bank[2 + p][:], ACT.Tanh, scale=0.5).then_inc(gu_tanh.sem, 1)

            @block.vector
            def _(dve):
                dve.wait_ge(const_in.sem, 16 * len(consts_list))
                dve.memset(k_stack[STACK:P], 1.0).then_inc(ones_set.sem, 1)
                dve.wait_ge(ones_set.sem, 1)
                dve.wait_ge(set_.sem, 8)
                dve.sem_inc(batch_done.sem, 1)
                with dve.Fori(0, BATCH) as i:
                    n = [0]

                    def step(ins):
                        n[0] += 1
                        ins.then_inc(vstep.sem, 1)
                        dve.wait_ge(*vstep(i, n[0]))

                    def moments(src, count, k):
                        for j in range(count):
                            last = dve.bn_stats(stats[:, j, :], src(j))
                        step(last)
                        dve.memset(wait_pad[:], 0.0)
                        for j in range(count):
                            last = dve.bn_aggr(mean_var[:, j, :], stats[:, j, :])
                        last.then_inc(stats_ready.sem, 1)
                        dve.wait_ge(*rstd_ready(i, k))

                    def layer_norm(src, k, order):
                        moments(src, TOK, k)
                        for j in range(TOK):
                            last = dve.tensor_scalar(lnx[:, j, :], src(j), mean_var[:, j, 0:1], rstd[:, j:j + 1],
                                                     ALU.subtract, ALU.mult)
                        last.then_inc(norm_ready.sem, 1)

                    for u in range(2 * CHUNKS):
                        m, s = width(u % CHUNKS), u % 2
                        dve.wait_ge(*k_full_ready(i, u + 1))
                        step(dve.tensor_tensor(k_full[:, s, 0:m], k_full[:, s, 0:m], k_part[:, s, 0, 0:m], ALU.subtract))
                        step(dve.tensor_copy(k_part[:, s, 1, 0:m], k_full[:, s, 0:m]))
                        dve.tensor_tensor(k_part[:, s, 2, 0:m], k_full[:, s, 0:m], k_part[:, s, 1, 0:m],
                                          ALU.subtract).then_inc(k_parts_ready.sem, 1)
                    for b in range(7):
                        dve.wait_ge(*v_psum(i, b + 1))
                        for t in range(2 * b, min(2 * b + 2, CTILES)):
                            m = rows(t)
                            last = dve.tensor_tensor(v_sb[0:m, t, :, 0:HD],
                                                     bank[4 + b % 2][0:m, t % 2 * DIM:(t % 2 + 1) * DIM].rearrange("p (h e) -> p h e", e=HD),
                                                     bv[0:m].rearrange("p (h e) -> p h e", e=HD), ALU.add)
                        last.then_inc(v_ready.sem, 1)

                    layer_norm(lambda j: x_all[:, TOK * i + j, :], 1, 1)
                    dve.wait_ge(*fq_tanh(i, 1))
                    step(dve.scalar_tensor_tensor(wide(q_silu), wide(q_tanh), 1.0, bank[1][:], ALU.add, ALU.mult))
                    step(dve.tensor_tensor(q_sq[:], q_silu[:], q_silu[:], ALU.mult))
                    dve.tensor_reduce(q_norm[:], q_sq[:], AX.X, ALU.add).then_inc(stats_ready.sem, 1)
                    dve.wait_ge(*s_psum(i, 1))
                    dve.tensor_tensor(s_in[:].rearrange("p (j g) -> p j g", g=2), bank[6][:, 0:4].rearrange("p (j g) -> p j g", g=2),
                                      b_s[:].unsqueeze(1).to_broadcast([P, TOK, 2]), ALU.add).then_inc(s_in_ready.sem, 1)
                    dve.wait_ge(*rstd_ready(i, 2))
                    step(dve.reciprocal(q_norm[:], q_norm[:]))
                    dve.tensor_tensor(q_silu[:], q_silu[:], q_norm[:].unsqueeze(2).to_broadcast([P, 4, P]),
                                      ALU.mult).then_inc(fq_ready.sem, 1)
                    dve.wait_ge(*s_tanh_ready(i, 1))
                    step(dve.scalar_tensor_tensor(s_in[:], s_tanh[:], 1.0, s_in[:], ALU.add, ALU.mult))
                    dve.wait_ge(*fg_tanh(i, 1))
                    step(dve.scalar_tensor_tensor(f_silu[:], f_tanh[:], 1.0, bank[4][:], ALU.add, ALU.mult))
                    dve.scalar_tensor_tensor(f_h[:], f_silu[:], 0.5, bank[3][:], ALU.mult, ALU.mult).then_inc(fh_ready.sem, 1)
                    dve.wait_ge(*fo_psum(i, 1))
                    fo_p = bank[5][:].rearrange("p (a b) -> p a b", b=P)
                    moments(lambda j: fo_p[:, j, :], 4, 3)
                    for j in range(4):
                        last = dve.tensor_scalar(fo[:, j, :], fo_p[:, j, :], mean_var[:, j, 0:1], rstd[:, j:j + 1], ALU.subtract, ALU.mult)
                    step(last)
                    step(dve.tensor_tensor(fo[:], fo[:], fw_g[:].unsqueeze(1).to_broadcast([P, 4, P]), ALU.mult))
                    step(dve.tensor_tensor(fo[:], fo[:], fw_b[:].unsqueeze(1).to_broadcast([P, 4, P]), ALU.add))
                    dve.scalar_tensor_tensor(fo[:], fo[:], 0.5, s_in[:].unsqueeze(2).to_broadcast([P, 4, P]), ALU.mult,
                                             ALU.mult).then_inc(fo_ready.sem, 1)
                    dve.wait_ge(*fwo_psum(i, 1))
                    for j in range(TOK):
                        last = dve.tensor_tensor(x4[:, j, :], x_all[:, TOK * i + j, :], bank[1][:, j * DIM:(j + 1) * DIM], ALU.add)
                    step(last)

                    layer_norm(lambda j: x4[:, j, :], 4, 2)
                    dve.wait_ge(*q_psum(i, 1))
                    for k in range(KT):
                        last = dve.tensor_scalar(q_full[:, k, :], bank[3][:, k * SEQ:(k + 1) * SEQ], bq[:, k:k + 1], QK_SCALE,
                                                 ALU.add, ALU.mult)
                    step(last)
                    step(dve.tensor_copy(q_part[:, 0], q_full[:]))
                    step(dve.tensor_tensor(q_full[:], q_full[:], q_part[:, 0], ALU.subtract))
                    step(dve.tensor_copy(q_part[:, 1], q_full[:]))
                    dve.tensor_tensor(q_part[:, 2], q_full[:], q_part[:, 1], ALU.subtract).then_inc(q_parts_ready.sem, 1)

                    def row_max(g):
                        for u in range(2 * GROUP * CHUNKS):
                            c = u % CHUNKS
                            nn = g * 2 * GROUP * CHUNKS + u
                            dve.wait_ge(*max_psum(i, nn + 1))
                            last = dve.tensor_reduce(chunk_max[:, u // CHUNKS, c:c + 1], bank[nn % 2][:, 0:width(c)], AX.X,
                                                     ALU.max)
                            last.then_inc(max_read.sem, 1)
                        dve.wait_ge(*max_read(i, (g + 1) * 2 * GROUP * CHUNKS))
                        step(dve.tensor_reduce(neg_max[:], chunk_max[:], AX.X, ALU.max, negate=True))
                        view = neg_max[:].rearrange("p (h j) -> p j h", j=TOK)
                        if g >= 1:
                            dve.wait_ge(*max_row_psum(i, g))
                        step(dve.tensor_copy(max_part[:, :, 0, :], view))
                        step(dve.tensor_tensor(view, view, max_part[:, :, 0, :], ALU.subtract))
                        step(dve.tensor_copy(max_part[:, :, 1, :], view))
                        dve.tensor_tensor(max_part[:, :, 2, :], view, max_part[:, :, 1, :], ALU.subtract).then_inc(max_part_ready.sem, 1)
                        dve.wait_ge(*max_row_psum(i, g + 1))
                        if g >= 1:
                            dve.wait_ge(*max_stacked(i, 48 * g))
                        dve.tensor_copy(max_row[:], bank[7][0:PARTS * GROUP, 0:SEQ]).then_inc(max_row_ready.sem, 1)

                    row_max(0)
                    for g in range(GROUPS):
                        if g + 1 < GROUPS:
                            row_max(g + 1)
                        dve.wait_ge(*den_psum(i, g + 1))
                        step(dve.reciprocal(den[:], bank[7][:, SEQ:]))
                        dve.tensor_tensor(attT[:, g, :], u_sb[:], den[:], ALU.mult).then_inc(head_ready.sem, 1)
                    dve.wait_ge(*co_psum(i, 1))
                    for j in range(TOK):
                        last = dve.tensor_tensor(x5[:, j, :], x4[:, j, :], bank[1][:, j * DIM:(j + 1) * DIM], ALU.add)
                    step(last)
                    step(dve.tensor_tensor(x5[:], x5[:], bo[:].unsqueeze(1).to_broadcast([P, TOK, DIM]), ALU.add))

                    layer_norm(lambda j: x5[:, j, :], 5, 3)
                    for p in range(IT // 2):
                        dve.wait_ge(*gu_tanh(i, p + 1))
                        step(dve.scalar_tensor_tensor(f_silu[:], f_tanh[:], 1.0, bank[2 + p][:], ALU.add, ALU.mult))
                        dve.scalar_tensor_tensor(gu[:, 2 * p:2 * p + 2, :].rearrange("p a b -> p (a b)"), f_silu[:], 0.5,
                                                 bank[(5, 6, 7)[p]][:], ALU.mult, ALU.mult).then_inc(gu_ready.sem, 1)
                    dve.wait_ge(*ffn_psum(i, 1))
                    dve.wait_ge(*stored(i, 16))
                    for j in range(TOK):
                        last = dve.tensor_tensor(x6[:, j, :], x5[:, j, :], bank[1][:, j * DIM:(j + 1) * DIM], ALU.add)
                    last.then_inc(batch_done.sem, 1)
                    assert n[0] == VSTEPS

            @block.tensor
            def _(pe):
                def transposed(dst, src):
                    for a in range(KT):
                        for b in range(TOK):
                            last = pe.transpose(dst[:, a * SEQ + b * P:a * SEQ + (b + 1) * P], src[:, b, a * P:(a + 1) * P], ident[:])
                    return last

                def channels_out(dst, weight, act_t, a, first=0):
                    for k in range(KT):
                        last = pe.matmul(dst, weight[:, k, a * P:(a + 1) * P], act_t[:, k, :], start=(k == 0), stop=(k == KT - 1))
                    return last

                def tokens_out(dst, weight, act_t):
                    for j in range(TOK):
                        for k in range(KT):
                            last = pe.matmul(dst[:, j * DIM:(j + 1) * DIM], act_t[:, k, j * P:(j + 1) * P], weight[:, k, :],
                                             start=(k == 0), stop=(k == KT - 1))
                    return last

                pe.wait_ge(weights_in.sem, 16 * len(w_names))
                pe.wait_ge(const_in.sem, 16 * len(consts_list))
                pe.wait_ge(set_.sem, 8)
                pe.wait_ge(ones_set.sem, 1)
                with pe.Fori(0, BATCH) as i:
                    pe.wait_ge(*batch_done(i, 1))
                    pe.wait_ge(*ctx_in(i, 16))
                    for u in range(2 * CHUNKS):
                        a, c = u // CHUNKS, u % CHUNKS
                        if u >= 2:
                            pe.wait_ge(*k_full_ready(i, u - 1))
                        for k in range(KT):
                            last = pe.matmul(bank[6 + u % 2][:, 0:width(c)], w["CWk"][:, k, a * P:(a + 1) * P],
                                             ctxT[:, k, c * CHUNK:c * CHUNK + width(c)], start=(k == 0), stop=(k == KT - 1))
                        last.then_inc(k_psum.sem, 1)
                    for b in range(7):
                        if b >= 2:
                            pe.wait_ge(*v_ready(i, b - 1))
                        for t in range(2 * b, min(2 * b + 2, CTILES)):
                            m = rows(t)
                            for k in range(KT):
                                last = pe.matmul(bank[4 + b % 2][0:m, t % 2 * DIM:(t % 2 + 1) * DIM], ctxT[:, k, t * P:t * P + m],
                                                 w["CWv"][:, k, :], start=(k == 0), stop=(k == KT - 1))
                        last.then_inc(v_psum.sem, 1)

                    pe.wait_ge(*norm_ready(i, 1))
                    transposed(bank[0], lnx).then_inc(lnT_psum.sem, 1)
                    pe.wait_ge(*lnT_ready(i, 1))
                    tokens_out(bank[1], w["FWq"], lnT).then_inc(fq_psum.sem, 1)
                    pe.wait_ge(*k_full_ready(i, 2 * CHUNKS))
                    for j in range(TOK):
                        for k in range(KT):
                            last = pe.matmul(bank[6][:, 2 * j:2 * j + 2], lnT[:, k, j * P:(j + 1) * P], w_s[:, k, :],
                                             start=(k == 0), stop=(k == KT - 1))
                    last.then_inc(s_psum.sem, 1)
                    pe.wait_ge(*fq_ready(i, 1))
                    for n in range(4):
                        last = pe.transpose(bank[2][:, n * P:(n + 1) * P], q_silu[:, n, :], ident[:])
                    last.then_inc(fqT_psum.sem, 1)
                    pe.wait_ge(*fqT_ready(i, 1))
                    for b, name in ((3, "w2T"), (4, "w0T")):
                        for g in range(2):
                            last = pe.matmul(bank[b][:, g * SEQ:(g + 1) * SEQ], fast[name][:, g, :],
                                             qT[:, g].rearrange("p t h -> p (t h)"), start=True, stop=True)
                    last.then_inc(fg_psum.sem, 1)
                    pe.wait_ge(*fh_ready(i, 1))
                    for j in range(TOK):
                        for g in range(2):
                            last = pe.matmul(bank[5][:, (2 * j + g) * P:(2 * j + g + 1) * P], f_h[:, g * SEQ + j * P:g * SEQ + (j + 1) * P],
                                             fast["w1T"][:, g, :], start=True, stop=True)
                    last.then_inc(fo_psum.sem, 1)
                    pe.wait_ge(*fo_ready(i, 1))
                    transposed(bank[0], fo[:].rearrange("p (j g) e -> p j (g e)", g=2)).then_inc(foT_psum.sem, 1)
                    pe.wait_ge(*foT_ready(i, 1))
                    tokens_out(bank[1], w["FWo"], foT).then_inc(fwo_psum.sem, 1)

                    pe.wait_ge(*norm_ready(i, 2))
                    transposed(bank[2], lnx).then_inc(lnT_psum.sem, 1)
                    pe.wait_ge(*lnT_ready(i, 2))
                    for a in range(KT):
                        last = channels_out(bank[3][:, a * SEQ:(a + 1) * SEQ], w["CWq"], lnT, a)
                    last.then_inc(q_psum.sem, 1)

                    UNITS = 2 * GROUP * CHUNKS

                    def max_scores(g, u):
                        n, h, j, c = g * UNITS + u, u // (2 * CHUNKS), u // CHUNKS % 2, u % CHUNKS
                        if u == 0:
                            pe.wait_ge(*k_stacked[g % 2](i, 96 * (g // 2 + 1)))
                        if n >= 2:
                            pe.wait_ge(*max_read(i, n - 1))
                        pe.matmul(bank[n % 2][:, 0:width(c)], q_stack[0:STACK, g * GROUP + h, j * P:(j + 1) * P],
                                  k_stack[0:STACK, g % 2, h, c * CHUNK:c * CHUNK + width(c)], start=True,
                                  stop=True).then_inc(max_psum.sem, 1)

                    def max_rows(g):
                        pe.wait_ge(*max_part_ready(i, g + 1))
                        for j in range(TOK):
                            last = pe.matmul(bank[7][0:PARTS * GROUP, j * P:(j + 1) * P],
                                             max_part[:, j].rearrange("p n h -> p (n h)"), ident_b[:], start=True, stop=True)
                        last.then_inc(max_row_psum.sem, 1)

                    def scores(g, t):
                        n = g * STEPS + t
                        if t == 0:
                            pe.wait_ge(*max_stacked(i, 48 * (g + 1)))
                        if n >= 2:
                            pe.wait_ge(*prob_ready(i, n - 1))
                        for e in range(4):
                            if t < STEPS - 1:
                                h, tile = t % 2 * 2 + e // 2, t // 2 * 2 + e % 2
                            else:
                                h, tile = e, CTILES - 1
                            m = rows(tile)
                            last = pe.matmul(wide_bank[n % 2][0:m, e * SEQ:(e + 1) * SEQ], k_stack[0:DEEP, g % 2, h, tile * P:tile * P + m],
                                             q_stack[0:DEEP, g * GROUP + h, :], start=True, stop=True)
                        last.then_inc(score_psum.sem, 1)

                    def add_values(g, b):
                        pe.wait_ge(*prob_ready(i, g * STEPS + min(2 * b + 2, STEPS)))
                        if b == 0 and g >= 1:
                            pe.wait_ge(*u_ready(i, g))
                        for tile in range(2 * b, min(2 * b + 2, CTILES)):
                            m = rows(tile)
                            for h in range(GROUP):
                                last = pe.matmul(bank[6][32 * h:32 * h + 32, 0:SEQ], v_sb[0:m, tile, g * GROUP + h, :],
                                                 probs[0:m, (g * 7 + b) % 2, h, tile % 2, :], start=(tile == 0), stop=(tile == CTILES - 1))
                        last.then_inc(tiles_added.sem, 1)

                    pe.wait_ge(*q_stacked(i, 96))
                    pe.wait_ge(*v_ready(i, 7))
                    for u in range(UNITS):
                        max_scores(0, u)
                    max_rows(0)
                    for g in range(GROUPS):
                        done = 0
                        for t in range(STEPS):
                            scores(g, t)
                            if g + 1 < GROUPS:
                                while done < UNITS * (t + 1) // STEPS:
                                    max_scores(g + 1, done)
                                    done += 1
                            if t >= 2 and t % 2 == 0:
                                add_values(g, t // 2 - 1)
                        add_values(g, 6)
                        if g + 1 < GROUPS:
                            max_rows(g + 1)
                        pe.wait_ge(*u_ready(i, g + 1))
                        if g + 1 < GROUPS:
                            pe.wait_ge(*max_row_ready(i, g + 2))
                        pe.matmul(bank[7][:, SEQ:], sel[:], u_sb[:], start=True, stop=True).then_inc(den_psum.sem, 1)
                    pe.wait_ge(*head_ready(i, GROUPS))
                    for j in range(TOK):
                        for g in range(GROUPS):
                            last = pe.matmul(bank[1][:, j * DIM:(j + 1) * DIM], attT[:, g, j * P:(j + 1) * P], w["CWo"][:, g, :],
                                             start=(g == 0), stop=(g == GROUPS - 1))
                    last.then_inc(co_psum.sem, 1)

                    pe.wait_ge(*norm_ready(i, 3))
                    transposed(bank[0], lnx).then_inc(lnT_psum.sem, 1)
                    pe.wait_ge(*lnT_ready(i, 3))
                    for p in range(IT // 2):
                        for name, b in (("gate", 2 + p), ("up", (5, 6, 7)[p])):
                            for a in range(2):
                                last = channels_out(bank[b][:, a * SEQ:(a + 1) * SEQ], lut_w[name], lnT, 2 * p + a)
                        last.then_inc(gu_psum.sem, 1)
                    pe.wait_ge(*gu_ready(i, IT // 2))
                    for j in range(TOK):
                        for c in range(IT):
                            m = min(P, INNER - c * P)
                            last = pe.matmul(bank[1][:, j * DIM:(j + 1) * DIM], gu[0:m, c, j * P:(j + 1) * P], lut_w["down"][0:m, c, :],
                                             start=(c == 0), stop=(c == IT - 1))
                    last.then_inc(ffn_psum.sem, 1)


def build(nc, d, out, stop_after=9):
    with ExitStack() as ctx:
        x_all = ctx.enter_context(nc.sbuf_tensor("x_all", [P, BATCH * TOK, DIM], F32))
        ident = ctx.enter_context(nc.sbuf_tensor("ident", [P, P], F32))
        lut_all = ctx.enter_context(nc.sbuf_tensor("lut_all", [P, 3 * 6 * DIM], F32))
        lut_w = {"all": lut_all,
                 "gate": lut_all[:, 0:6 * DIM].rearrange("p (k n) -> p k n", k=KT),
                 "up": lut_all[:, 6 * DIM:12 * DIM].rearrange("p (k n) -> p k n", k=KT),
                 "down": lut_all[:, 12 * DIM:].rearrange("p (c n) -> p c n", c=6)}
        x_loaded = Signal(ctx.enter_context(nc.semaphore("x_loaded")))
        x_view = d["x"].rearrange("b (j p) c -> p (b j) c", p=P)
        with nc.Block() as block:
            @block.sync
            def _(sp):
                sp.dma_start(x_all[:], x_view).then_inc(x_loaded.sem, 16)
                sp.dma_start(ident[:], d["ident"]).then_inc(x_loaded.sem, 16)
        attention_and_context(nc, d, x_all, x_loaded, {"ident": ident, "ones": None})
        if stop_after >= 3:
            experts(nc, d, x_all, x_loaded, ident, lut_w)
        if stop_after >= 6:
            fast_weights_softmax_and_lut(nc, d, out, x_all, x_loaded, ident, lut_w)
            return
        with nc.semaphore("stored") as stored, nc.Block() as block:
            @block.sync
            def _(sp):
                sp.dma_start(out.rearrange("b (j p) c -> p (b j) c", p=P), x_all[:]).then_inc(stored, 16)
                sp.wait_ge(stored, 16)


def layout(inputs):
    import numpy as np

    def a(n):
        return np.asarray(inputs[n])

    def t(n):
        return np.ascontiguousarray(a(n).T)

    def col(n):
        return np.ascontiguousarray(a(n).reshape(KT, P).T)

    d = {"x": a("x"), "ctxT": np.ascontiguousarray(a("ctx_2048").transpose(0, 2, 1))}
    for n in ("r", "k", "v", "g", "o"):
        d[f"W{n}T"] = t(f"L0_attn_W{n}")
    for n in ("k", "v", "r", "g"):
        d["maa_" + n] = col("L0_attn_time_maa_" + n)
    d["time_decay"] = a("L0_attn_time_decay").reshape(-1)
    d["faaaa"] = a("L0_attn_time_faaaa").reshape(-1)
    d["gamma"], d["beta"] = a("L0_attn_gamma"), a("L0_attn_beta")
    for n in ("q", "g", "kv", "o"):
        d[f"XW{n}T"] = t(f"L0_xattn_W{n}")
    d["xbg"] = col("L0_xattn_bg")
    key = np.arange(P)[:, None]
    tok = np.concatenate([np.arange(SEQ), np.arange(P)])[None, :]
    d["delta"] = np.maximum(tok - key - 1, 0).astype(np.float32)
    d["strict"] = (tok > key).astype(np.float32)
    d["diag"] = (tok == key).astype(np.float32)
    d["headmask"] = (np.arange(P)[:, None] // 8 == np.arange(P // 8)[None, :]).astype(np.float32)
    d["blk16"] = (np.arange(P)[:, None] // 16 == np.arange(P)[None, :] // 16).astype(np.float32)
    d["routerT"] = t("L0_ffn_router_w")
    for n in ("gate", "up", "down"):
        d[n + "T"] = np.ascontiguousarray(a(f"L0_ffn_{n}_w").transpose(0, 2, 1))
    d["lut"], d["lut_key"] = a("L1_ffn_lut"), np.arange(16, dtype=np.float32)
    for n in ("gate", "up"):
        d[n + "_idx"] = np.ascontiguousarray(np.pad(a(f"L1_ffn_{n}_idx").T, ((0, 0), (0, 768 - 688))))
    d["down_idx"] = np.ascontiguousarray(np.pad(a("L1_ffn_down_idx").T, ((0, 768 - 688), (0, 0))))
    qkv = a("L1_attn_W_qkv")
    d["FWq"] = np.ascontiguousarray(np.concatenate([qkv[:, 0:P], qkv[:, 3 * P:4 * P]], axis=1))
    d["FWo"], d["w_s"], d["b_s"] = a("L1_attn_W_o"), a("L1_attn_W_s"), a("L1_attn_b_s")
    d["fw_g"], d["fw_b"] = a("L1_attn_ln_g"), a("L1_attn_ln_b")
    for n in range(3):
        d[f"w{n}T"] = np.ascontiguousarray(a(f"L1_attn_w{n}").transpose(0, 2, 1))
    for n in ("q", "k", "v"):
        d["CW" + n] = t("L1_xattn_W" + n)
    d["CWo"] = np.ascontiguousarray(np.pad(a("L1_xattn_Wo").T.reshape(16, 16, DIM), ((0, 0), (0, 16), (0, 0))).reshape(512, DIM))
    d["bq"], d["bk"], d["bv"], d["bo"] = col("L1_xattn_bq"), col("L1_xattn_bk"), a("L1_xattn_bv"), a("L1_xattn_bo")
    rows_, cols_ = np.arange(P)[:, None], np.arange(P)[None, :]
    d["sel"] = ((rows_ % 32 == 16) & (rows_ // 32 == cols_ // 32)).astype(np.float32)
    d["earlier"] = np.tril(np.ones((8, 8), np.float32), -1)
    d["ident"] = np.eye(P, dtype=np.float32)
    return d


def kernel(**inputs):
    import concourse.bacc as bacc
    from concourse.bass_utils import run_bass_kernel_spmd

    nc = bacc.Bacc("TRN2", target_bir_lowering=False, num_devices=1)
    arrays = {"in_" + k: v for k, v in layout(inputs).items()}
    d = {k[3:]: nc.dram_tensor(k, v.shape, mybir.dt.from_np(v.dtype), kind="ExternalInput").ap() for k, v in arrays.items()}
    out = nc.dram_tensor("out", (BATCH, SEQ, DIM), F32, kind="ExternalOutput").ap()
    build(nc, d, out)
    r = run_bass_kernel_spmd(nc, [arrays], core_ids=[0])
    return r.results[0]["out"]
```

```python
from contextlib import ExitStack

import concourse.bass as bass
import concourse.mybir as mybir

F32 = mybir.dt.float32
BF16 = mybir.dt.bfloat16
F32R = mybir.dt.float32r
I32 = mybir.dt.int32
ALU = mybir.AluOpType
ACT = mybir.ActivationFunctionType
AX = mybir.AxisListType

P = 128
BATCH, SEQ, DIM = 4, 256, 256
TOK = SEQ // P
KT = DIM // P
CTX = 1601
CTILES = -(-CTX // P)
LN_EPS = 1e-5


class Signal:

    def __init__(self, sem, per=0, before=0):
        self.sem, self.per, self.before = sem, per, before

    def __call__(self, i, k):
        return self.sem, i * self.per + (self.before + k)


def rows(t):
    return min(P, CTX - t * P)


def attention_and_context(nc, d, x_all, x_loaded, consts):
    HEADS, HD = 32, 8
    GROUP_EPS = 1e-5 * 144
    ZEPS = 1e-6
    SC = SEQ + P
    RING = 3
    ATTS = 8
    ident, ones = consts["ident"], consts["ones"]
    with ExitStack() as ctx:
        def sb(name, shape, dt=F32):
            return ctx.enter_context(nc.sbuf_tensor(name, shape, dt))

        def sig(name, per=0):
            return Signal(ctx.enter_context(nc.semaphore(name)), per)

        bank = [ctx.enter_context(nc.psum_tensor(f"a_bank{n}", [P, 512], F32)) for n in range(8)]

        w_names = ["WrT", "WkT", "WvT", "WgT", "WoT", "XWqT", "XWgT", "XWoT"]
        w = {n: sb("a_" + n, [P, KT, DIM]) for n in w_names}
        w["XWkvT"] = sb("a_XWkvT", [P, KT, 2 * DIM])
        cols = {n: sb("a_" + n, [P, KT]) for n in ["maa_k", "maa_v", "maa_r", "maa_g", "xbg"]}
        gamma, beta = sb("gamma", [P, DIM]), sb("beta", [P, DIM])
        delta, strict, diag = sb("delta", [P, SC]), sb("strict", [P, SC]), sb("diag", [P, SC])
        headmask, blk16 = sb("headmask", [P, P // HD]), sb("blk16", [P, P])
        logw, faaaa = sb("logw", [P, HEADS]), sb("faaaa", [P, HEADS])
        decay = sb("decay", [P, HEADS, SC])
        ctxT = sb("ctxT", [P, KT, CTX])
        mean_var, stats = sb("a_mean_var", [P, TOK, 2]), sb("a_stats", [P, TOK, 6])
        rstd, half_neg = sb("a_rstd", [P, TOK]), sb("a_half_neg", [P, TOK])
        var_eps, eps = sb("a_var_eps", [P, TOK]), sb("a_eps", [P, TOK])
        lnx = sb("a_lnx", [P, TOK, DIM])
        wait_pad = sb("a_wait_pad", [P, 1])
        lnT = sb("a_lnT", [P, KT, SEQ + 1])
        ln2T = sb("a_ln2T", [P, KT, SEQ])
        diff = sb("diff", [P, KT, SEQ])
        mix = {n: sb("mix_" + n, [P, KT, SEQ]) for n in "krvg"}
        r_sb, k_sb = sb("r_sb", [P, KT, SEQ]), sb("k_sb", [P, KT, SEQ])
        r_head = sb("r_head", [P, ATTS, SEQ])
        v_pad = sb("v_pad", [P, TOK, 8, 4 * 40])
        att = sb("att", [P, ATTS, SC])
        y_sb, g_tanh, g_silu = sb("y_sb", [P, KT, SEQ]), sb("g_tanh", [P, TOK, DIM]), sb("g_silu", [P, TOK, DIM])
        y_c, y_sq = sb("y_c", [P, TOK * HEADS, HD]), sb("y_sq", [P, TOK * HEADS, HD])
        g_mean, g_var, g_rstd = (sb(n, [P, TOK * HEADS]) for n in ("g_mean", "g_var", "g_rstd"))
        g_bits, g_square = sb("g_bits", [P, TOK * HEADS], I32), sb("g_square", [P, TOK * HEADS])
        zT = sb("zT", [P, KT, SEQ])
        x1 = sb("x1", [P, TOK, DIM])
        k_min, k_exp, k_feat = (sb(n, [P, 2, DIM]) for n in ("k_min", "k_exp", "k_feat"))
        v_ones = sb("v_ones", [P, 2, KT, P + 1])
        kv_m, ks_m = sb("kv_m", [P, KT, P]), sb("ks_m", [P, KT, P])
        ks_col = sb("ks_col", [P, KT])
        q_min, q_exp, q_feat = (sb(n, [P, KT, SEQ]) for n in ("q_min", "q_exp", "q_feat"))
        gate, den, aT = sb("gate", [P, KT, SEQ]), sb("den", [P, KT, SEQ]), sb("aT", [P, KT, SEQ])
        hbg = sb("hbg", [P, KT])

        const_in, weights_in = sig("a_const_in"), sig("a_weights_in")
        ctx_in = sig("ctx_in", 16)
        logw_exp, logw_ready, decay_exp, decay_ready = (sig(n) for n in ("logw_exp", "logw_ready", "decay_exp", "decay_ready"))
        zeroed, ones_set, hbg_ready = sig("zeroed"), sig("ones_set"), sig("hbg_ready")
        tri_masked, tri_copied = sig("tri_masked"), sig("tri_copied")
        batch_done = sig("a_batch_done", 1)
        NEWTON = 3
        VSTEPS, GSTEPS = 16 + 4 + 3 * NEWTON, 2
        vstep, gstep = sig("a_vstep", VSTEPS), sig("a_gstep", GSTEPS)
        stats_ready, rstd_ready, ln_ready = sig("a_stats_ready", 2), sig("a_rstd_ready", 2), sig("a_ln_ready", 2)
        lnT_psum, lnT_ready = sig("a_lnT_psum", 2), sig("a_lnT_ready", 2)
        ctx_psum, k_min_ready, k_exp_ready = sig("ctx_psum", CTILES), sig("k_min_ready", CTILES), sig("k_exp_ready", CTILES)
        k_feat_ready, v_ready, kv_added = sig("k_feat_ready", CTILES), sig("v_ready", CTILES), sig("kv_added", CTILES)
        kv_ready = sig("kv_ready", 1)
        mix_ready = sig("mix_ready", 4)
        proj_psum, proj_read = sig("proj_psum", 4), sig("proj_read", 4)
        g_ready = sig("g_ready", 1)
        r_head_ready = sig("r_head_ready", HEADS)
        score_psum, att_ready, group_added = sig("score_psum", HEADS), sig("att_ready", HEADS), sig("group_added", 8)
        y_ready, yt_psum = sig("y_ready", 1), sig("yt_psum", 1)
        z_ready = sig("z_ready", 1)
        zT_psum, zT_ready, o_psum = sig("zT_psum", 1), sig("zT_ready", 1), sig("o_psum", 1)
        q_psum, q_min_ready, q_exp_ready, q_feat_ready = (sig(n, 1) for n in ("q_psum", "q_min_ready", "q_exp_ready", "q_feat_ready"))
        gate_psum, gate_tanh, num_psum, den_psum = (sig(n, 1) for n in ("gate_psum", "gate_tanh", "num_psum", "den_psum"))
        aT_ready, xo_psum = sig("aT_ready", 1), sig("xo_psum", 1)

        ORDER = [(half, q * 4 + m) for half in range(KT) for m in range(4) for q in range(4)]

        MID = 5
        POINTS = CTILES + 2
        EIGHTH = HEADS // 4

        HEAD_POINTS = {7 * k - 1: MID + k for k in range(1, 5)}

        R_LEAD = 4

        def passes(eng, ahead, chain):
            ahead()
            with eng.Fori(0, BATCH - 1) as i:
                chain(i, True)
            chain(BATCH - 1, False)

        def wide(t):
            return t[:, :, :].rearrange("p a b -> p (a b)")

        consts_list = [(delta, d["delta"]), (strict, d["strict"]), (diag, d["diag"]), (headmask, d["headmask"]),
                       (blk16, d["blk16"]), (logw, d["time_decay"].partition_broadcast(P)),
                       (faaaa, d["faaaa"].partition_broadcast(P)), (gamma, d["gamma"].partition_broadcast(P)),
                       (beta, d["beta"].partition_broadcast(P))] + [(cols[n], d[n]) for n in cols]
        weights_list = [(w[n], d[n]) for n in ["XWkvT", "WkT", "WrT", "WvT", "WgT", "WoT", "XWqT", "XWgT", "XWoT"]]

        with nc.Block() as block:
            @block.sync
            def _(sp):
                sp.dma_start(ctxT[:], d["ctxT"][0].rearrange("(k p) s -> p k s", p=P)).then_inc(ctx_in.sem, 16)
                for t, src in consts_list:
                    sp.dma_start(t[:], src).then_inc(const_in.sem, 16)
                with sp.Fori(0, BATCH - 1) as i:
                    sp.wait_ge(*ctx_psum(i, CTILES))
                    sp.dma_start(ctxT[:], d["ctxT"][i + 1].rearrange("(k p) s -> p k s", p=P)).then_inc(ctx_in.sem, 16)

            @block.gpsimd
            def _(pool):
                pool.memset(v_pad[:], 0.0).then_inc(zeroed.sem, 1)
                pool.memset(lnT[:, :, 0:1], 0.0).then_inc(zeroed.sem, 1)
                pool.memset(half_neg[:], -0.5).then_inc(zeroed.sem, 1)
                pool.memset(eps[:], LN_EPS).then_inc(zeroed.sem, 1)
                pool.memset(v_ones[:, :, :, P:P + 1], 1.0).then_inc(zeroed.sem, 1)
                pool.wait_ge(zeroed.sem, 5)
                with pool.Fori(0, BATCH) as i:
                    n = [0]

                    def step(ins):
                        n[0] += 1
                        ins.then_inc(gstep.sem, 1)
                        pool.wait_ge(*gstep(i, n[0]))

                    def rsqrt_var(k):
                        pool.wait_ge(*stats_ready(i, k))
                        step(pool.tensor_tensor(var_eps[:], mean_var[:, :, 1], eps[:, 0:TOK], ALU.add))
                        pool.tensor_tensor(rstd[:], var_eps[:], half_neg[:, 0:TOK], ALU.pow).then_inc(rstd_ready.sem, 1)

                    rsqrt_var(1)
                    rsqrt_var(2)
                    assert n[0] == GSTEPS

            @block.scalar
            def _(act):
                for t, src in weights_list:
                    act.dma_start(t[:], src.rearrange("(k p) n -> p k n", p=P)).then_inc(weights_in.sem, 16)
                act.wait_ge(const_in.sem, 16 * len(consts_list))
                act.activation(logw[:], logw[:], ACT.Exp).then_inc(logw_exp.sem, 1)
                act.wait_ge(logw_ready.sem, 2)
                act.wait_ge(zeroed.sem, 5)

                def point(i, p):
                    if p >= CTILES:
                        return
                    m = rows(p)
                    act.wait_ge(*k_min_ready(i, p + 1))
                    if p >= 2:
                        act.wait_ge(*kv_added(i, p - 1))
                    act.copy(v_ones[0:m, p % 2, :, 0:P],
                             bank[5 + p % 2][0:m, DIM:].rearrange("p (a b) -> p a b", a=KT)).then_inc(v_ready.sem, 1)
                    act.activation(k_exp[0:m, p % 2, :], k_min[0:m, p % 2, :], ACT.Exp).then_inc(k_exp_ready.sem, 1)

                def copy_tri(e):
                    act.wait_ge(decay_ready.sem, e + 1)
                    act.copy(decay[:, e * EIGHTH:(e + 1) * EIGHTH, SEQ:], decay[:, e * EIGHTH:(e + 1) * EIGHTH, 0:P]).then_inc(tri_copied.sem, 1)

                def ahead():
                    for e in range(4):
                        for h in range(e * EIGHTH, (e + 1) * EIGHTH):
                            last = act.activation(decay[:, h, 0:SEQ], delta[:, 0:SEQ], ACT.Exp, scale=logw[:, h:h + 1])
                        last.then_inc(decay_exp.sem, 1)
                        point(0, e)
                        copy_tri(e)
                    point(0, 4)

                def chain(i, more):
                    def at(*points):
                        for p in points:
                            if p >= MID:
                                point(i, p)
                            elif more:
                                point(i + 1, p)

                    act.wait_ge(*lnT_psum(i, 1))
                    act.copy(lnT[:, :, 1:], bank[0][:].rearrange("p (a b) -> p a b", a=KT)).then_inc(lnT_ready.sem, 1)
                    act.wait_ge(*proj_psum(i, 1))
                    act.copy(wide(k_sb), bank[1][:]).then_inc(proj_read.sem, 1)
                    act.wait_ge(*proj_psum(i, 2))
                    act.copy(wide(r_sb), bank[2][:]).then_inc(proj_read.sem, 1)
                    act.wait_ge(*proj_psum(i, 3))
                    for j in range(TOK):
                        last = act.copy(v_pad[:, j].rearrange("p q (m e) -> p q m e", m=4)[:, :, :, 0:HD],
                                        bank[7][:, j * DIM:(j + 1) * DIM].rearrange("p (q m e) -> p q m e", q=8, m=4))
                    last.then_inc(proj_read.sem, 1)
                    act.wait_ge(*proj_psum(i, 4))
                    act.activation(wide(g_tanh), bank[0][:], ACT.Tanh, scale=0.5).then_inc(proj_read.sem, 1)
                    act.wait_ge(*proj_read(i, 4))
                    at(MID)
                    for n_, (half, h) in enumerate(ORDER):
                        if n_ >= ATTS:
                            act.wait_ge(*score_psum(i, n_ - ATTS + 1))
                        act.activation(r_head[:, n_ % ATTS, :], r_sb[:, half, :], ACT.Copy,
                                       scale=headmask[:, h:h + 1]).then_inc(r_head_ready.sem, 1)
                        if n_ - R_LEAD in HEAD_POINTS:
                            at(HEAD_POINTS[n_ - R_LEAD])
                    act.wait_ge(*group_added(i, 8))
                    act.copy(wide(y_sb), bank[0][:]).then_inc(y_ready.sem, 1)
                    at(10, 11)
                    act.wait_ge(*zT_psum(i, 1))
                    act.copy(wide(zT), bank[2][:]).then_inc(zT_ready.sem, 1)
                    at(12)
                    act.wait_ge(*lnT_psum(i, 2))
                    act.copy(wide(ln2T), bank[0][:]).then_inc(lnT_ready.sem, 1)
                    act.wait_ge(*q_min_ready(i, 1))
                    act.activation(wide(q_exp), wide(q_min), ACT.Exp).then_inc(q_exp_ready.sem, 1)
                    act.wait_ge(*gate_psum(i, 1))
                    for k in range(KT):
                        last = act.activation(gate[:, k, :], bank[2][:, k * SEQ:(k + 1) * SEQ], ACT.Tanh,
                                              bias=hbg[:, k:k + 1], scale=0.5)
                    last.then_inc(gate_tanh.sem, 1)
                    at(0, 1, 2, 3, 4)

                passes(act, ahead, chain)

            @block.vector
            def _(dve):
                dve.wait_ge(logw_exp.sem, 1)
                dve.tensor_scalar(logw[:], logw[:], -1.0, None, ALU.mult).then_inc(logw_ready.sem, 1)
                dve.tensor_scalar(hbg[:], cols["xbg"][:], 0.5, None, ALU.mult).then_inc(logw_ready.sem, 1)
                dve.wait_ge(zeroed.sem, 5)
                dve.wait_ge(x_loaded.sem, 16)
                dve.sem_inc(batch_done.sem, 1)

                def point(i, p):
                    if p < CTILES:
                        m, s = rows(p), p % 2
                        dve.wait_ge(*ctx_psum(i, p + 1))
                        dve.tensor_scalar(k_min[0:m, s, :], bank[5 + s][0:m, 0:DIM], 0.0, None,
                                          ALU.min).then_inc(k_min_ready.sem, 1)
                    if 1 <= p <= CTILES:
                        m, s = rows(p - 1), (p - 1) % 2
                        dve.wait_ge(*k_exp_ready(i, p))
                        if p >= 3:
                            dve.wait_ge(*kv_added(i, p - 2))
                        dve.scalar_tensor_tensor(k_feat[0:m, s, :], bank[5 + s][0:m, 0:DIM], 0.0, k_exp[0:m, s, :],
                                                 ALU.max, ALU.add).then_inc(k_feat_ready.sem, 1)

                def decay_part(e):
                    dve.wait_ge(decay_exp.sem, e + 1)
                    h0, h1 = e * EIGHTH, (e + 1) * EIGHTH
                    dve.tensor_tensor(decay[:, h0:h1, 0:P], decay[:, h0:h1, 0:P],
                                      strict[:, 0:P].unsqueeze(1).to_broadcast([P, EIGHTH, P]), ALU.mult).then_inc(tri_masked.sem, 1)
                    dve.wait_ge(tri_masked.sem, e + 1)
                    for h in range(h0, h1):
                        last = dve.scalar_tensor_tensor(decay[:, h, 0:P], diag[:, 0:P], faaaa[:, h:h + 1], decay[:, h, 0:P],
                                                        ALU.mult, ALU.add)
                    last.then_inc(decay_ready.sem, 1)

                def ahead():
                    for e in range(4):
                        decay_part(e)
                        point(0, e)
                    point(0, 4)
                    dve.wait_ge(tri_copied.sem, 4)

                def chain(i, more):
                    def at(*points):
                        for p in points:
                            if p >= MID:
                                point(i, p)
                            elif more:
                                point(i + 1, p)

                    n = [0]

                    def step(ins):
                        n[0] += 1
                        ins.then_inc(vstep.sem, 1)
                        dve.wait_ge(*vstep(i, n[0]))

                    def layer_norm(src, k):
                        for j in range(TOK):
                            last = dve.bn_stats(stats[:, j, :], src(j))
                        step(last)
                        dve.memset(wait_pad[:], 0.0)
                        for j in range(TOK):
                            last = dve.bn_aggr(mean_var[:, j, :], stats[:, j, :])
                        last.then_inc(stats_ready.sem, 1)
                        dve.wait_ge(*rstd_ready(i, k))
                        for j in range(TOK):
                            last = dve.tensor_scalar(lnx[:, j, :], src(j), mean_var[:, j, 0:1], rstd[:, j:j + 1],
                                                     ALU.subtract, ALU.mult)
                        last.then_inc(ln_ready.sem, 1)

                    layer_norm(lambda j: x_all[:, TOK * i + j, :], 1)
                    def keep_sums():
                        dve.wait_ge(*kv_added(i, CTILES))
                        for h in range(KT):
                            dve.tensor_tensor(kv_m[:, h, :], bank[3 + h][:, 0:P], blk16[:], ALU.mult)
                            last = dve.tensor_copy(ks_col[:, h:h + 1], bank[3 + h][:, P:P + 1])
                        step(last)
                        for h in range(KT):
                            last = dve.tensor_scalar(ks_m[:, h, :], blk16[:], ks_col[:, h:h + 1], None, ALU.mult)
                        last.then_inc(kv_ready.sem, 1)

                    dve.wait_ge(*lnT_ready(i, 1))
                    step(dve.tensor_tensor(diff[:], lnT[:, :, 0:SEQ], lnT[:, :, 1:], ALU.subtract))
                    for name in "krvg":
                        for k in range(KT):
                            last = dve.scalar_tensor_tensor(mix[name][:, k, :], diff[:, k, :], cols["maa_" + name][:, k:k + 1],
                                                            lnT[:, k, 1:], ALU.mult, ALU.add)
                        last.then_inc(mix_ready.sem, 1)
                    at(MID)
                    dve.wait_ge(*proj_read(i, 4))
                    dve.scalar_tensor_tensor(wide(g_silu), wide(g_tanh), 1.0, bank[0][:], ALU.add,
                                             ALU.mult).then_inc(g_ready.sem, 1)
                    for n_, (half, h) in enumerate(ORDER):
                        dve.wait_ge(*score_psum(i, n_ + 1))
                        if n_ >= ATTS:
                            dve.wait_ge(*group_added(i, (n_ - ATTS) // 4 + 1))
                        dve.tensor_tensor(att[:, n_ % ATTS, :], bank[(1, 2, 7)[n_ % RING]][:, 0:SC], decay[:, half * 16 + h, :],
                                          ALU.mult).then_inc(att_ready.sem, 1)
                        if n_ in HEAD_POINTS:
                            at(HEAD_POINTS[n_])
                    dve.wait_ge(*yt_psum(i, 1))
                    y4 = bank[1][:].rearrange("p (g e) -> p g e", e=HD)

                    def over(t):
                        return t[:].unsqueeze(2).to_broadcast([P, TOK * HEADS, HD])

                    step(dve.tensor_reduce(g_mean[:], y4, AX.X, ALU.add))
                    step(dve.tensor_scalar(g_mean[:], g_mean[:], 1.0 / HD, None, ALU.mult))
                    at(10)
                    step(dve.tensor_tensor(y_c[:], y4, over(g_mean), ALU.subtract))
                    step(dve.tensor_tensor(y_sq[:], y_c[:], y_c[:], ALU.mult))
                    step(dve.tensor_reduce(g_var[:], y_sq[:], AX.X, ALU.add))
                    at(11)
                    step(dve.tensor_scalar(g_var[:], g_var[:], GROUP_EPS * HD, None, ALU.add))
                    step(dve.tensor_scalar(g_bits[:], g_var[:].bitcast(I32), 1, None, ALU.logical_shift_right))
                    step(dve.tensor_scalar(g_rstd[:].bitcast(I32), g_bits[:], -1.0, float(0x5F3759DF), ALU.mult, ALU.add))
                    for _ in range(NEWTON):
                        step(dve.tensor_tensor(g_square[:], g_rstd[:], g_rstd[:], ALU.mult))
                        step(dve.scalar_tensor_tensor(g_square[:], g_square[:], -0.5, g_var[:], ALU.mult, ALU.mult))
                        step(dve.scalar_tensor_tensor(g_rstd[:], g_square[:], 1.5, g_rstd[:], ALU.add, ALU.mult))
                    step(dve.tensor_tensor(y_c[:], y_c[:], over(g_rstd), ALU.mult))
                    y2 = y_c[:].rearrange("p (j h) e -> p j (h e)", j=TOK)
                    step(dve.scalar_tensor_tensor(y2, y2, HD ** 0.5, gamma[:].unsqueeze(1).to_broadcast([P, TOK, DIM]),
                                                  ALU.mult, ALU.mult))
                    step(dve.tensor_tensor(y2, y2, beta[:].unsqueeze(1).to_broadcast([P, TOK, DIM]), ALU.add))
                    dve.wait_ge(*g_ready(i, 1))
                    dve.scalar_tensor_tensor(y2, y2, 0.5, g_silu[:], ALU.mult, ALU.mult).then_inc(z_ready.sem, 1)
                    at(12, 13)
                    dve.wait_ge(*o_psum(i, 1))
                    for j in range(TOK):
                        last = dve.tensor_tensor(x1[:, j, :], x_all[:, TOK * i + j, :], bank[7][:, j * DIM:(j + 1) * DIM], ALU.add)
                    step(last)

                    layer_norm(lambda j: x1[:, j, :], 2)
                    keep_sums()
                    dve.wait_ge(*q_psum(i, 1))
                    dve.tensor_scalar(wide(q_min), bank[1][:], 0.0, None, ALU.min).then_inc(q_min_ready.sem, 1)
                    dve.wait_ge(*q_exp_ready(i, 1))
                    dve.scalar_tensor_tensor(wide(q_feat), bank[1][:], 0.0, wide(q_exp), ALU.max,
                                             ALU.add).then_inc(q_feat_ready.sem, 1)
                    at(0, 1)
                    dve.wait_ge(*den_psum(i, 1))
                    step(dve.tensor_scalar(wide(den), bank[0][:], ZEPS, None, ALU.add))
                    step(dve.reciprocal(wide(den), wide(den)))
                    dve.wait_ge(*num_psum(i, 1))
                    step(dve.tensor_tensor(wide(den), wide(den), bank[7][:], ALU.mult))
                    dve.wait_ge(*gate_tanh(i, 1))
                    step(dve.tensor_scalar(wide(gate), wide(gate), 0.5, 0.5, ALU.mult, ALU.add))
                    dve.tensor_tensor(wide(aT), wide(den), wide(gate), ALU.mult).then_inc(aT_ready.sem, 1)
                    at(2, 3, 4)
                    dve.wait_ge(*xo_psum(i, 1))
                    for j in range(TOK):
                        last = dve.tensor_tensor(x_all[:, TOK * i + j, :], x1[:, j, :], bank[0][:, j * DIM:(j + 1) * DIM], ALU.add)
                    last.then_inc(batch_done.sem, 1)
                    assert n[0] == VSTEPS

                passes(dve, ahead, chain)

            @block.tensor
            def _(pe):
                def transposed(dst, src, part):
                    for a in range(KT):
                        for b in range(TOK):
                            last = pe.transpose(dst[:, a * SEQ + b * P:a * SEQ + (b + 1) * P], src[:, b, a * P:(a + 1) * P], ident[:])
                    return last

                def channels_out(dst, weight, act_t):
                    for a in range(KT):
                        for k in range(KT):
                            last = pe.matmul(dst[:, a * SEQ:(a + 1) * SEQ], weight[:, k, a * P:(a + 1) * P], act_t[:, k, :],
                                             start=(k == 0), stop=(k == KT - 1))
                    return last

                def tokens_out(dst, weight, act_t):
                    for j in range(TOK):
                        for k in range(KT):
                            last = pe.matmul(dst[:, j * DIM:(j + 1) * DIM], act_t[:, k, j * P:(j + 1) * P], weight[:, k, :],
                                             start=(k == 0), stop=(k == KT - 1))
                    return last

                pe.wait_ge(x_loaded.sem, 16 * 2)
                pe.wait_ge(weights_in.sem, 16 * len(weights_list))
                def point(i, p):
                    if p >= 2:
                        t = p - 2
                        m, s = rows(t), t % 2
                        pe.wait_ge(*k_feat_ready(i, t + 1))
                        pe.wait_ge(*v_ready(i, t + 1))
                        for h in range(KT):
                            last = pe.matmul(bank[3 + h][:, 0:P + 1], k_feat[0:m, s, h * P:(h + 1) * P], v_ones[0:m, s, h, :],
                                             start=(t == 0), stop=(t == CTILES - 1))
                        last.then_inc(kv_added.sem, 1)
                    if p < CTILES:
                        m = rows(p)
                        for k in range(KT):
                            last = pe.matmul(bank[5 + p % 2][0:m, :], ctxT[:, k, p * P:p * P + m], w["XWkvT"][:, k, :],
                                             start=(k == 0), stop=(k == KT - 1))
                        last.then_inc(ctx_psum.sem, 1)

                def ahead():
                    pe.wait_ge(*ctx_in(0, 16))
                    for p in range(MID):
                        point(0, p)

                def chain(i, more):
                    def at(*points):
                        for p in points:
                            if p >= MID:
                                point(i, p)
                            elif more:
                                if p == 0:
                                    pe.wait_ge(*ctx_in(i + 1, 16))
                                    pe.wait_ge(*kv_ready(i, 1))
                                point(i + 1, p)

                    pe.wait_ge(*batch_done(i, 1))
                    pe.wait_ge(*ln_ready(i, 1))
                    transposed(bank[0], lnx, 0).then_inc(lnT_psum.sem, 1)
                    for n_, (name, dst) in enumerate((("k", 1), ("r", 2))):
                        pe.wait_ge(*mix_ready(i, n_ + 1))
                        channels_out(bank[dst], w[f"W{name}T"], mix[name]).then_inc(proj_psum.sem, 1)
                    for n_, (name, dst) in enumerate((("v", 7), ("g", 0))):
                        pe.wait_ge(*mix_ready(i, n_ + 3))
                        tokens_out(bank[dst], w[f"W{name}T"], mix[name]).then_inc(proj_psum.sem, 1)

                    def add_group(n_):
                        pe.wait_ge(*att_ready(i, n_ + 4))
                        half, m = ORDER[n_][0], ORDER[n_][1] % 4
                        for j in range(TOK):
                            for q in range(4):
                                a = att[:, (n_ + q) % ATTS, j * SEQ:j * SEQ + SEQ - j * P]
                                last = pe.matmul(bank[0][32 * q:32 * q + 32, half * SEQ + j * P:(half + 1) * SEQ],
                                                 v_pad[:, j, half * 4 + q, 32 * m:32 * m + 32], a,
                                                 start=(m == 0 and j == 0), stop=(m == 3 and j == TOK - 1))
                        last.then_inc(group_added.sem, 1)

                    at(MID)
                    pe.wait_ge(*proj_read(i, 3))
                    for n_, (half, h) in enumerate(ORDER):
                        pe.wait_ge(*r_head_ready(i, n_ + 1))
                        if n_ >= RING:
                            pe.wait_ge(*att_ready(i, n_ - RING + 1))
                        b, r = bank[(1, 2, 7)[n_ % RING]], r_head[:, n_ % ATTS, :]
                        pe.matmul(b[:, 0:SEQ], k_sb[:, half, 0:P], r, start=True, stop=True)
                        pe.matmul(b[:, SEQ:SC], k_sb[:, half, P:SEQ], r[:, P:SEQ], start=True,
                                  stop=True).then_inc(score_psum.sem, 1)
                        if n_ >= 5 and (n_ - 5) % 4 == 0:
                            add_group(n_ - 5)
                        if n_ in HEAD_POINTS:
                            at(HEAD_POINTS[n_])
                    add_group(28)
                    pe.wait_ge(*y_ready(i, 1))
                    for j in range(TOK):
                        for a in range(KT):
                            last = pe.transpose(bank[1][:, j * DIM + a * P:j * DIM + (a + 1) * P], y_sb[:, a, j * P:(j + 1) * P], ident[:])
                    last.then_inc(yt_psum.sem, 1)
                    at(10, 11, 12)
                    pe.wait_ge(*z_ready(i, 1))
                    transposed(bank[2], y_c[:].rearrange("p (j h) e -> p j (h e)", j=TOK), 1).then_inc(zT_psum.sem, 1)
                    at(13)
                    pe.wait_ge(*zT_ready(i, 1))
                    tokens_out(bank[7], w["WoT"], zT).then_inc(o_psum.sem, 1)
                    at(14)

                    pe.wait_ge(*ln_ready(i, 2))
                    transposed(bank[0], lnx, 2).then_inc(lnT_psum.sem, 1)
                    pe.wait_ge(*lnT_ready(i, 2))
                    channels_out(bank[1], w["XWqT"], ln2T).then_inc(q_psum.sem, 1)
                    channels_out(bank[2], w["XWgT"], ln2T).then_inc(gate_psum.sem, 1)
                    at(0, 1)
                    pe.wait_ge(*q_feat_ready(i, 1))
                    for h in range(KT):
                        last = pe.matmul(bank[0][:, h * SEQ:(h + 1) * SEQ], ks_m[:, h, :], q_feat[:, h, :], start=True, stop=True)
                    last.then_inc(den_psum.sem, 1)
                    for h in range(KT):
                        last = pe.matmul(bank[7][:, h * SEQ:(h + 1) * SEQ], kv_m[:, h, :], q_feat[:, h, :], start=True, stop=True)
                    last.then_inc(num_psum.sem, 1)
                    at(2, 3, 4)
                    pe.wait_ge(*aT_ready(i, 1))
                    tokens_out(bank[0], w["XWoT"], aT).then_inc(xo_psum.sem, 1)

                passes(pe, ahead, chain)




def experts(nc, d, x_all, x_loaded, ident, lut_w):
    EXPERTS, INNER, TOP_P = 8, 512, 0.9
    N = BATCH * TOK
    IT = INNER // P
    PAIR = 2
    HALF = N * P // 2
    UNITS = PAIR * 2 * IT
    with ExitStack() as ctx:
        def sb(name, shape, dt=F32):
            return ctx.enter_context(nc.sbuf_tensor(name, shape, dt))

        def sig(name, per=0):
            return Signal(ctx.enter_context(nc.semaphore(name)), per)

        bank = [ctx.enter_context(nc.psum_tensor(f"b_bank{n}", [P, 512], F32)) for n in range(8)]
        SIZE = KT * INNER
        w_in = sb("w_in", [P, PAIR, 3, SIZE])
        w_hi, w_lo = sb("w_hi", [P, PAIR, 3, SIZE], F32R), sb("w_lo", [P, PAIR, 3, SIZE], F32R)
        router = sb("router", [P, KT, EXPERTS])
        earlier = sb("earlier", [P, EXPERTS, EXPERTS])
        stats, mean_var = sb("b_stats", [P, N, 6]), sb("b_mean_var", [P, N, 2])
        eps, half_neg, var_eps, rstd = (sb("b_" + n, [P, N]) for n in ("eps", "half_neg", "var_eps", "rstd"))
        lnx, lnT = sb("b_lnx", [P, N, DIM]), sb("b_lnT", [P, KT, N * P])
        lnT_hi, lnT_lo = sb("lnT_hi", [P, KT, N * P], F32R), sb("lnT_lo", [P, KT, N * P], F32R)
        top, total = sb("r_top", [P, N]), sb("r_total", [P, N])
        prob, before = sb("prob", [P, N, EXPERTS]), sb("before", [P, N, EXPERTS])
        above, above_eq = sb("above", [P, N, EXPERTS, EXPERTS]), sb("above_eq", [P, N, EXPERTS, EXPERTS])
        weight = sb("weight", [P, EXPERTS, N])
        weight_e = sb("weight_e", [P, PAIR, N])
        g_tanh, g_silu = sb("b_g_tanh", [P, 2, HALF]), sb("b_g_silu", [P, 2, HALF])
        h_full = sb("h_full", [P, 2, HALF])
        h_hi, h_lo = sb("h_hi", [P, 2, IT, HALF], F32R), sb("h_lo", [P, 2, IT, HALF], F32R)
        LUT, LUT_COLS = 16, 3 * 6 * DIM
        PER_PASS, SLICES = LUT // (EXPERTS // PAIR), 4
        lut_idx, lut_hit = sb("lut_idx", [P, LUT_COLS], I32), sb("lut_hit", [P, LUT_COLS // SLICES])
        lut_val, lut_key = sb("lut_val", [P, LUT]), sb("lut_key", [P, LUT])
        val_now, key_now = sb("val_now", [P, PER_PASS]), sb("key_now", [P, PER_PASS])
        lut_flat = lut_w["all"]

        const_in, set_ = sig("b_const_in"), sig("b_set")
        stats_ready, rstd_ready, ln_ready, lnT_psum, lnT_ready = (sig("b_" + n) for n in (
            "stats_ready", "rstd_ready", "ln_ready", "lnT_psum", "lnT_ready"))
        logit_psum, shifted, prob_exp, router_done = (sig(n) for n in ("logit_psum", "shifted", "prob_exp", "router_done"))
        pool_step, prologue_step = sig("b_pool_step"), sig("b_prologue_step")
        weights_in, w_hi_ready, w_lo_ready = ([sig(f"b_{n}{e}", k) for e in range(PAIR)] for n, k in (
            ("weights_in", 48), ("w_hi_ready", 3), ("w_lo_ready", 3)))
        lnT_hi_ready, lnT_lo_ready = sig("lnT_hi_ready"), sig("lnT_lo_ready")
        gate_psum, gate_tanh, gate_silu, h_full_ready, h_hi_ready, h_lo_ready = (sig("b_" + n, UNITS) for n in (
            "gate_psum", "gate_tanh", "gate_silu", "h_full_ready", "h_hi_ready", "h_lo_ready"))
        weight_ready = sig("weight_ready", 1)
        lut_now, lut_hit_ready, lut_added = sig("lut_now", 1), sig("lut_hit_ready", UNITS), sig("lut_added", UNITS)
        y_psum, y_added = sig("y_psum", UNITS // 2), sig("y_added", UNITS // 2)
        HALVES = UNITS // IT
        PASSES = EXPERTS // PAIR
        SPLIT_AT = {2 + 2 * n: (1, n) for n in range(3)}
        SPLIT_AT.update({10 + 2 * n: (0, n) for n in range(3)})

        def passes(eng, body):
            body(0, True, True)
            with eng.Fori(1, PASSES - 1) as i:
                body(i, False, True)
            body(PASSES - 1, False, False)

        def split_of(i, u, more):
            if u not in SPLIT_AT or (SPLIT_AT[u][0] == 0 and not more):
                return None
            place, n = SPLIT_AT[u]
            return (i if place else i + 1), place, n

        def three(pe, dst, hi, lo, moving_hi, moving_lo, first, last):
            pe.matmul(dst, hi, moving_hi, start=first, stop=False)
            pe.matmul(dst, hi, moving_lo, start=False, stop=False)
            return pe.matmul(dst, lo, moving_hi, start=False, stop=last)

        with nc.Block() as block:
            @block.sync
            def _(sp):
                def load(i, e):
                    for n, (name, tiles) in enumerate((("gateT", KT), ("upT", KT), ("downT", IT))):
                        sp.dma_start(w_in[:, e, n].rearrange("p (k n) -> p k n", k=tiles),
                                     d[name][i * PAIR + e].rearrange("(k p) n -> p k n", p=P)).then_inc(weights_in[e].sem, 16)

                for e in range(PAIR):
                    load(0, e)
                sp.dma_start(router[:], d["routerT"].rearrange("(k p) e -> p k e", p=P)).then_inc(const_in.sem, 16)
                sp.dma_start(earlier[:], d["earlier"].partition_broadcast(P)).then_inc(const_in.sem, 16)
                sp.dma_start(lut_val[:], d["lut"].partition_broadcast(P)).then_inc(const_in.sem, 16)
                sp.dma_start(lut_key[:], d["lut_key"].partition_broadcast(P)).then_inc(const_in.sem, 16)
                for n, name in enumerate(("gate_idx", "up_idx")):
                    sp.dma_start(lut_idx[:, n * 6 * DIM:(n + 1) * 6 * DIM].rearrange("p (k n) -> p k n", k=KT),
                                 d[name].rearrange("(k p) n -> p k n", p=P)).then_inc(const_in.sem, 16)
                sp.dma_start(lut_idx[:, 12 * DIM:].rearrange("p (c n) -> p c n", c=6),
                             d["down_idx"].rearrange("(c p) n -> p c n", p=P)).then_inc(const_in.sem, 16)

                with sp.Fori(0, PASSES - 1) as i:
                    for e in range(PAIR):
                        sp.wait_ge(*w_lo_ready[e](i, 3))
                        load(i + 1, e)

            @block.gpsimd
            def _(pool):
                pool.memset(eps[:], LN_EPS).then_inc(set_.sem, 1)
                pool.memset(half_neg[:], -0.5).then_inc(set_.sem, 1)
                pool.wait_ge(set_.sem, 2)
                pool.wait_ge(stats_ready.sem, 1)
                pool.tensor_tensor(var_eps[:], mean_var[:, :, 1], eps[:], ALU.add).then_inc(pool_step.sem, 1)
                pool.wait_ge(pool_step.sem, 1)
                pool.tensor_tensor(rstd[:], var_eps[:], half_neg[:], ALU.pow).then_inc(rstd_ready.sem, 1)

                def split(i, e, n):
                    pool.wait_ge(*w_hi_ready[e](i, n + 1))
                    pool.tensor_tensor(w_lo[:, e, n], w_in[:, e, n], w_hi[:, e, n].bitcast(F32), ALU.subtract).then_inc(w_lo_ready[e].sem, 1)

                def body(i, first, more):
                    for u in range(UNITS):
                        s = split_of(i, u, more)
                        if s:
                            split(*s)
                        h, c = u // IT, u % IT
                        pool.wait_ge(*h_hi_ready(i, u + 1))
                        pool.tensor_tensor(h_lo[:, h % 2, c], h_full[:, u % 2], h_hi[:, h % 2, c].bitcast(F32),
                                           ALU.subtract).then_inc(h_lo_ready.sem, 1)

                for n in range(3):
                    split(0, 0, n)
                passes(pool, body)

            @block.scalar
            def _(act):
                for n in range(4):
                    k, h = n // 2, n % 2
                    act.wait_ge(lnT_psum.sem, n + 1)
                    act.copy(lnT[:, k, h * HALF:(h + 1) * HALF], bank[n][:]).then_inc(lnT_ready.sem, 1)
                    act.wait_ge(lnT_ready.sem, n + 1)
                    act.copy(lnT_hi[:, k, h * HALF:(h + 1) * HALF], lnT[:, k, h * HALF:(h + 1) * HALF]).then_inc(lnT_hi_ready.sem, 1)

                def split(i, e, n):
                    act.wait_ge(*weights_in[e](i, 48))
                    act.copy(w_hi[:, e, n], w_in[:, e, n]).then_inc(w_hi_ready[e].sem, 1)

                for n in range(3):
                    split(0, 0, n)
                act.wait_ge(shifted.sem, 1)
                act.activation(prob[:], prob[:], ACT.Exp).then_inc(prob_exp.sem, 1)

                def body(i, first, more):
                    for u in range(UNITS):
                        h, c = u // IT, u % IT
                        act.wait_ge(*gate_psum(i, u + 1))
                        if u >= 2 or not first:
                            act.wait_ge(*gate_silu(i, u - 1))
                        act.activation(g_tanh[:, u % 2], bank[u % 2][:], ACT.Tanh, scale=0.5).then_inc(gate_tanh.sem, 1)
                        s = split_of(i, u, more)
                        if s:
                            split(*s)
                        act.wait_ge(*h_full_ready(i, u + 1))
                        act.copy(h_hi[:, h % 2, c], h_full[:, u % 2]).then_inc(h_hi_ready.sem, 1)

                passes(act, body)

            @block.vector
            def _(dve):
                n_ = [0]

                def step(ins):
                    n_[0] += 1
                    ins.then_inc(prologue_step.sem, 1)
                    dve.wait_ge(prologue_step.sem, n_[0])

                for n in range(N):
                    last = dve.bn_stats(stats[:, n, :], x_all[:, n, :])
                step(last)
                for n in range(N):
                    last = dve.bn_aggr(mean_var[:, n, :], stats[:, n, :])
                last.then_inc(stats_ready.sem, 1)
                dve.wait_ge(rstd_ready.sem, 1)
                for n in range(N):
                    dve.tensor_scalar(lnx[:, n, :], x_all[:, n, :], mean_var[:, n, 0:1], rstd[:, n:n + 1],
                                      ALU.subtract, ALU.mult).then_inc(ln_ready.sem, 1)
                for n in range(4):
                    k, h = n // 2, n % 2
                    cols = slice(h * HALF, (h + 1) * HALF)
                    dve.wait_ge(lnT_hi_ready.sem, n + 1)
                    dve.tensor_tensor(lnT_lo[:, k, cols], lnT[:, k, cols], lnT_hi[:, k, cols].bitcast(F32),
                                      ALU.subtract).then_inc(lnT_lo_ready.sem, 1)
                dve.wait_ge(logit_psum.sem, 1)
                logits = bank[4][:, 0:N * EXPERTS].rearrange("p (n e) -> p n e", e=EXPERTS)
                step(dve.tensor_reduce(top[:], logits, AX.X, ALU.max))
                dve.tensor_tensor(prob[:], logits, top[:].unsqueeze(2).to_broadcast([P, N, EXPERTS]),
                                  ALU.subtract).then_inc(shifted.sem, 1)
                dve.wait_ge(prob_exp.sem, 1)
                step(dve.tensor_reduce(total[:], prob[:], AX.X, ALU.add))
                step(dve.reciprocal(total[:], total[:]))
                step(dve.tensor_tensor(prob[:], prob[:], total[:].unsqueeze(2).to_broadcast([P, N, EXPERTS]), ALU.mult))
                dve.wait_ge(const_in.sem, 112)
                for n in range(N):
                    pj = prob[:, n].unsqueeze(1).to_broadcast([P, EXPERTS, EXPERTS])
                    pe = prob[:, n].unsqueeze(2).to_broadcast([P, EXPERTS, EXPERTS])
                    dve.tensor_tensor(above[:, n], pj, pe, ALU.is_gt)
                    last = dve.tensor_tensor(above_eq[:, n], pj, pe, ALU.is_ge)
                step(last)
                for n in range(N):
                    last = dve.tensor_tensor(above_eq[:, n], above_eq[:, n], earlier[:], ALU.mult)
                step(last)
                step(dve.tensor_tensor(above[:].rearrange("p a b c -> p (a b c)"), above[:].rearrange("p a b c -> p (a b c)"),
                                       above_eq[:].rearrange("p a b c -> p (a b c)"), ALU.max))
                for n in range(N):
                    pj = prob[:, n].unsqueeze(1).to_broadcast([P, EXPERTS, EXPERTS])
                    last = dve.tensor_tensor(above[:, n], above[:, n], pj, ALU.mult)
                step(last)
                step(dve.tensor_reduce(before[:], above[:], AX.X, ALU.add))
                step(dve.memset(lut_flat[:], 0.0))
                step(dve.scalar_tensor_tensor(weight[:].rearrange("p e n -> p n e"), before[:], TOP_P, prob[:], ALU.is_le, ALU.mult))
                dve.wait_ge(prologue_step.sem, n_[0])

                def add_y(i, h):
                    for b in range(2):
                        dve.wait_ge(*y_psum(i, 2 * h + b + 1))
                        for t in range(2):
                            n = (h % 2) * 4 + b * 2 + t
                            last = dve.scalar_tensor_tensor(x_all[:, n, :], bank[4 + h % 2 * 2 + b][:, t * DIM:(t + 1) * DIM],
                                                            weight_e[:, h // 2, n:n + 1], x_all[:, n, :], ALU.mult, ALU.add)
                        last.then_inc(y_added.sem, 1)

                def body(i, first, more):
                    dve.tensor_copy(val_now[:], lut_val[:, bass.ds(i * PER_PASS, PER_PASS)])
                    dve.tensor_copy(key_now[:], lut_key[:, bass.ds(i * PER_PASS, PER_PASS)]).then_inc(lut_now.sem, 1)
                    dve.wait_ge(*lut_now(i, 1))
                    for u in range(UNITS):
                        h = u // IT
                        dve.wait_ge(*gate_tanh(i, u + 1))
                        dve.scalar_tensor_tensor(g_silu[:, u % 2], g_tanh[:, u % 2], 1.0, bank[u % 2][:], ALU.add,
                                                 ALU.mult).then_inc(gate_silu.sem, 1)
                        if u >= 2 or not first:
                            dve.wait_ge(*h_lo_ready(i, u - 1))
                        dve.wait_ge(*gate_silu(i, u + 1))
                        dve.scalar_tensor_tensor(h_full[:, u % 2], g_silu[:, u % 2], 0.5, bank[2 + u % 2][:],
                                                 ALU.mult, ALU.mult).then_inc(h_full_ready.sem, 1)
                        v, part = u // SLICES, slice(u % SLICES * (LUT_COLS // SLICES), (u % SLICES + 1) * (LUT_COLS // SLICES))
                        dve.tensor_scalar(lut_hit[:], lut_idx[:, part], key_now[:, v:v + 1], val_now[:, v:v + 1],
                                          ALU.is_equal, ALU.mult).then_inc(lut_hit_ready.sem, 1)
                        if u % IT == 2 and h >= 1:
                            add_y(i, h - 1)
                        elif u == 2:
                            if not first:
                                add_y(i - 1, HALVES - 1)
                                dve.wait_ge(*y_added(i, 0))
                            dve.tensor_copy(weight_e[:], weight[:, bass.ds(i * PAIR, PAIR), :]).then_inc(weight_ready.sem, 1)
                            dve.wait_ge(*weight_ready(i, 1))
                        dve.wait_ge(*lut_hit_ready(i, u + 1))
                        dve.tensor_tensor(lut_flat[:, part], lut_flat[:, part], lut_hit[:], ALU.add).then_inc(lut_added.sem, 1)
                        dve.wait_ge(*lut_added(i, u + 1))

                passes(dve, body)
                add_y(PASSES - 1, HALVES - 1)
                dve.wait_ge(*y_added(PASSES - 1, UNITS // 2))

            @block.tensor
            def _(pe):
                for n in range(4):
                    k, h = n // 2, n % 2
                    for t in range(4):
                        pe.wait_ge(ln_ready.sem, h * 4 + t + 1)
                        last = pe.transpose(bank[n][:, t * P:(t + 1) * P], lnx[:, h * 4 + t, k * P:(k + 1) * P], ident[:])
                    last.then_inc(lnT_psum.sem, 1)
                pe.wait_ge(lnT_ready.sem, 4)
                pe.wait_ge(const_in.sem, 112)
                for n in range(N):
                    for k in range(KT):
                        last = pe.matmul(bank[4][:, n * EXPERTS:(n + 1) * EXPERTS], lnT[:, k, n * P:(n + 1) * P], router[:, k, :],
                                         start=(k == 0), stop=(k == KT - 1))
                last.then_inc(logit_psum.sem, 1)
                pe.wait_ge(lnT_lo_ready.sem, 4)

                def down(i, h):
                    e, half = h // 2, h % 2
                    pe.wait_ge(*h_lo_ready(i, IT * (h + 1)))
                    pe.wait_ge(*w_lo_ready[e](i, 3))
                    for b in range(2):
                        if h >= 2 or not (isinstance(i, int) and i == 0):
                            pe.wait_ge(*y_added(i, 2 * (h - 2) + b + 1))
                        for t in range(2):
                            for c in range(IT):
                                tokens = slice((b * 2 + t) * P, (b * 2 + t + 1) * P)
                                cols = slice(c * DIM, (c + 1) * DIM)
                                last = three(pe, bank[4 + half * 2 + b][:, t * DIM:(t + 1) * DIM],
                                             h_hi[:, half, c, tokens], h_lo[:, half, c, tokens],
                                             w_hi[:, e, 2, cols], w_lo[:, e, 2, cols], c == 0, c == IT - 1)
                        last.then_inc(y_psum.sem, 1)

                def body(i, first, more):
                    for u in range(UNITS):
                        e, h, c = u // (2 * IT), (u // IT) % 2, u % IT
                        if c == 0 and h == 0:
                            pe.wait_ge(*w_lo_ready[e](i, 2))
                        if u >= 2 or not first:
                            pe.wait_ge(*h_full_ready(i, u - 1))
                        tokens = slice(h * HALF, (h + 1) * HALF)
                        for n, b in ((0, 0), (1, 2)):
                            for k in range(KT):
                                cols = slice(k * INNER + c * P, k * INNER + (c + 1) * P)
                                last = three(pe, bank[b + u % 2][:], w_hi[:, e, n, cols], w_lo[:, e, n, cols],
                                             lnT_hi[:, k, tokens], lnT_lo[:, k, tokens], k == 0, k == KT - 1)
                        last.then_inc(gate_psum.sem, 1)
                        if c == 1 and u >= IT:
                            down(i, u // IT - 1)
                        elif c == 1 and not first:
                            down(i - 1, HALVES - 1)

                passes(pe, body)
                down(PASSES - 1, HALVES - 1)


def fast_weights_softmax_and_lut(nc, d, out, x_all, x_loaded, ident, lut_w):
    HEADS, HD = 16, 16
    QK_SCALE = 1.0 / HD ** 0.5
    FW_EPS, L2_EPS = 1e-6, 1e-5
    GROUP = 4
    GROUPS = HEADS // GROUP
    PARTS = 3
    TERMS = 6
    STACK = TERMS * HD
    DEEP = STACK + PARTS
    CHUNK = 512
    CHUNKS = -(-CTX // CHUNK)
    K_SLOTS = 4
    IT = 6
    INNER = 688

    def width(c):
        return min(CHUNK, CTX - c * CHUNK)

    with ExitStack() as ctx:
        def sb(name, shape, dt=F32):
            return ctx.enter_context(nc.sbuf_tensor(name, shape, dt))

        def sig(name, per=0):
            return Signal(ctx.enter_context(nc.semaphore(name)), per)

        def stages(name, n):
            sem = ctx.enter_context(nc.semaphore(name))
            return [Signal(sem, n, k) for k in range(n)]

        def psum(name, banks=1):
            return ctx.enter_context(nc.psum_tensor(name, [P, banks * 512], F32))

        bank = [psum(f"c_bank{n}") for n in range(8)]

        k_dram = nc.dram_tensor("k_parts", (BATCH, PARTS, DIM, CTX), BF16, kind="Internal").ap()
        q_dram = nc.dram_tensor("q_parts", (BATCH, PARTS, DIM, SEQ), BF16, kind="Internal").ap()

        w = {n: sb("c_" + n, [P, KT, DIM]) for n in ("FWq", "FWo", "CWq", "CWk", "CWv")}
        w["CWo"] = sb("c_CWo", [P, GROUPS, DIM])
        fast = {n: sb("c_" + n, [P, KT, P]) for n in ("w0T", "w1T", "w2T")}
        w_s, b_s = sb("w_s", [P, KT, 2]), sb("b_s", [P, 2])
        fw_g, fw_b, bv, bo = sb("fw_g", [P, P]), sb("fw_b", [P, P]), sb("bv", [P, DIM]), sb("bo", [P, DIM])
        bq, bk = sb("bq", [P, KT]), sb("bk", [P, KT])
        sel = sb("sel", [P, P])
        ident_b = sb("ident_b", [P, P], BF16)
        ctxT = sb("c_ctxT", [P, KT, CTX])
        stats, mean_var = sb("c_stats", [P, 4, 6]), sb("c_mean_var", [P, 4, 2])
        var_eps, rstd, half_neg, half_pos = (sb("c_" + n, [P, 4]) for n in ("var_eps", "rstd", "half_neg", "half_pos"))
        eps, fw_eps, l2_eps = (sb("c_" + n, [P, 4]) for n in ("eps", "fw_eps", "l2_eps"))
        wait_pad = sb("c_wait_pad", [P, 1])
        lnx, lnT = sb("c_lnx", [P, TOK, DIM]), sb("c_lnT", [P, KT, SEQ])
        q_tanh, q_silu, q_sq = (sb("c_" + n, [P, 4, P]) for n in ("q_tanh", "q_silu", "q_sq"))
        q_norm = sb("q_norm", [P, 4])
        qT = sb("c_qT", [P, TOK, P, 2])
        f_tanh, f_silu, f_h = (sb("c_" + n, [P, 2 * SEQ]) for n in ("f_tanh", "f_silu", "f_h"))
        s_in, s_tanh = sb("s_in", [P, 4]), sb("s_tanh", [P, 4])
        fo, foT = sb("fo", [P, 4, P]), sb("foT", [P, KT, SEQ])
        x4_ahead, x4, x5, x6 = (sb(n, [P, TOK, DIM]) for n in ("x4_ahead", "x4", "x5", "x6"))
        v_ahead = sb("v_ahead", [P, CTILES, DIM])
        k_full = sb("k_full", [P, K_SLOTS, CHUNK])
        k_part = sb("k_part", [P, K_SLOTS, PARTS, CHUNK], BF16)
        q_full, q_part = sb("q_full", [P, KT, SEQ]), sb("q_part", [P, PARTS, KT, SEQ], BF16)
        v_all = sb("c_v", [P, CTILES, HEADS * (HD + 1) + 32 - HD - 1])
        v_sb = v_all[:, :, 0:HEADS * (HD + 1)].rearrange("p t (h e) -> p t h e", e=HD + 1)
        k_stack = sb("k_stack", [P, 2, GROUP, CTX], BF16)
        q_stack = sb("q_stack", [P, HEADS, SEQ], BF16)
        chunk_max = sb("chunk_max", [P, 2 * GROUP, CHUNKS])
        neg_max = sb("neg_max", [P, 2 * GROUP])
        max_part = sb("max_part", [P, TOK, PARTS, GROUP], BF16)
        max_row = sb("max_row", [PARTS * GROUP, SEQ], BF16)
        probs = sb("probs", [P, 2, GROUP, 2, SEQ])
        u_sb, den = sb("u_sb", [P, SEQ]), sb("c_den", [P, SEQ])
        attT = sb("attT", [P, GROUPS, SEQ])
        gu = sb("gu", [P, IT, SEQ])

        const_in, weights_in, set_, ones_set = sig("c_const_in"), sig("c_weights_in"), sig("c_set"), sig("c_ones_set")
        ahead_step, behind_step, max_step = sig("ahead_step", 15), sig("behind_step", 5), sig("max_step", 4 * GROUPS)
        pool_ahead, pool_behind = sig("pool_ahead", 4), sig("pool_behind", 1)
        behind_done, stored = sig("behind_done", 1), sig("c_stored", 16)
        ctx_in = sig("c_ctx_in", 16)
        k_psum, k_full_ready, k_rest_ready, k_part1_ready, k_parts_ready = (sig("c_" + n, 2 * CHUNKS) for n in (
            "k_psum", "k_full_ready", "k_rest_ready", "k_part1_ready", "k_parts_ready"))
        k_written = [sig(f"k_written{n}", 16 * 2 * CHUNKS // K_SLOTS) for n in range(K_SLOTS)]
        v_psum, v_ready, v_copied = sig("c_v_psum", 7), sig("c_v_ready", 7), sig("v_copied", 2)
        stats_ready, rstd_ready = sig("c_stats_ready", 3), sig("c_rstd_ready", 4)
        norm_ready, lnT_psum, lnT_ready = (sig("c_" + n, 2) for n in ("norm_ready", "lnT_psum", "lnT_ready"))
        b_stats_ready, b_rstd_ready, b_norm_ready, b_lnT_psum, b_lnT_ready = (sig("behind_" + n, 1) for n in (
            "stats_ready", "rstd_ready", "norm_ready", "lnT_psum", "lnT_ready"))
        fq_psum, s_psum, fqT_psum, fg_psum, fo_psum, foT_psum, fwo_psum, q_psum = stages("fast_psum", 8)
        fq_tanh, s_tanh_ready, fqT_ready, fg_tanh, foT_ready = stages("fast_act", 5)
        s_in_ready, fq_squares, fq_ready, fh_ready, fo_ready, x4_ready, q_parts_ready = stages("fast_dve", 7)
        q_written, q_stacked = sig("q_written", 32), [sig(f"q_stacked{g}", 16 * TERMS) for g in range(GROUPS)]
        k_stacked = [[sig(f"k_stacked{n}{half}", 2 * 16 * TERMS) for half in "ab"] for n in range(2)]
        MAXES = 2 * GROUP * CHUNKS
        max_psum, max_read = sig("max_psum", GROUPS * MAXES), sig("max_read", GROUPS * MAXES)
        max_part_ready, max_row_psum, max_row_ready = (sig(n, GROUPS) for n in ("max_part_ready", "max_row_psum", "max_row_ready"))
        max_stacked = sig("max_stacked", GROUPS * 48)
        HALF = 2 * CHUNK
        HALF_STEPS = HALF // P // 2 * GROUP
        PAIRS = 7
        STEPS = 26
        MAX_BY = 20
        score_psum, prob_ready = sig("c_score_psum", GROUPS * STEPS), sig("c_prob_ready", GROUPS * STEPS)
        tiles_added = sig("tiles_added", GROUPS * PAIRS)
        u_ready, den_psum, den_inverse, head_ready = (sig(n, GROUPS) for n in ("u_ready", "c_den_psum", "den_inverse", "head_ready"))
        x4_kept = sig("x4_kept", 1)
        co_psum, x5_ready = sig("co_psum", 1), sig("x5_ready", 1)
        gu_psum, gu_tanh, gu_ready = sig("gu_psum", IT // 2), sig("gu_tanh", IT // 2), sig("gu_ready", IT // 2)
        ffn_psum = sig("ffn_psum", 1)

        K_AT = [46 + 5 * u // 2 for u in range(2 * CHUNKS)]
        V_AT = [65 + t for t in range(CTILES)]
        GU_AT = [84 + 5 * p for p in range(IT // 2)]
        KV_STEPS = range(46, 82)

        vector_load = {5: 2, 8: 1, 16: 4, 18: 1.5, 25: 2, 28: 2, 30: 4, 36: 2.5, 38: 1, 43: 2, 44: 2.5, 10: 2, 11: 1, 78: 2, 80: 1,
                       86: 2, 91: 2, 96: 2, 103: 1}
        vector_load.update({7 + g * STEPS: 3 for g in range(GROUPS)})
        vector_load.update({V_AT[2 * b] + 2: 1 for b in range(PAIRS)})

        def maxes_schedule(g):
            load = [vector_load.get(g * STEPS + t, 0) for t in range(MAX_BY)]
            share = (sum(load) + MAXES) / MAX_BY
            begun = [0]
            for t in range(MAX_BY):
                begun.append(min(MAXES, max(begun[-1], round(share * (t + 1) - sum(load[:t + 1])))))
            begun[-1] = MAXES
            return begun

        def maxes_before(g, t, ahead):
            if (g == GROUPS - 1 and not ahead) or t >= MAX_BY:
                return range(0)
            begun = maxes_schedule(g)
            return range(begun[t], begun[t + 1])

        def following(i, g):
            return (i, g + 1) if g + 1 < GROUPS else (i + 1, 0)

        def preceding(i, g):
            return (i, g - 1) if g else (i - 1, GROUPS - 1)

        def alone(i):
            return isinstance(i, int) and i == 0

        def kv_bank(i, n):
            return bank[(2 if alone(i) else 4) + n % 2]

        steps_alone = sorted(range(GROUPS * STEPS), key=lambda s: s - KV_STEPS.start if s in KV_STEPS else s)

        def passes(eng, ahead_of, body, behind_of):
            ahead_of(0)
            body(0, True, True)
            with eng.Fori(1, BATCH - 1) as i:
                body(i, False, True)
            body(BATCH - 1, False, False)
            behind_of(BATCH - 1)

        def wide(t):
            return t[:].rearrange("p a b -> p (a b)")

        consts_list = ([(fast[n], d[n].rearrange("g d e -> d g e")) for n in fast]
                       + [(w_s, d["w_s"].rearrange("(k p) n -> p k n", p=P)), (b_s, d["b_s"].partition_broadcast(P)),
                          (fw_g, d["fw_g"].partition_broadcast(P)), (fw_b, d["fw_b"].partition_broadcast(P)),
                          (bv, d["bv"].partition_broadcast(P)), (bo, d["bo"].partition_broadcast(P)),
                          (bq, d["bq"]), (bk, d["bk"]), (sel, d["sel"])])
        w_names = list(w)

        with nc.Block() as block:
            @block.sync
            def _(sp):
                sp.dma_start(ctxT[:], d["ctxT"][0].rearrange("(k p) s -> p k s", p=P)).then_inc(ctx_in.sem, 16)
                for n in w_names:
                    sp.dma_start(w[n][:], d[n].rearrange("(k p) n -> p k n", p=P)).then_inc(weights_in.sem, 16)
                for t, src in consts_list:
                    sp.dma_start(t[:], src).then_inc(const_in.sem, 16)
                sp.sem_inc(stored.sem, 16)

                def write_k(i, u):
                    a, c = u // CHUNKS, u % CHUNKS
                    sp.wait_ge(*k_parts_ready(i, u + 1))
                    sp.dma_start(k_dram[i, :, a * P:(a + 1) * P, c * CHUNK:c * CHUNK + width(c)].rearrange("n p s -> p n s"),
                                 k_part[:, u % K_SLOTS, :, 0:width(c)]).then_inc(k_written[u % K_SLOTS].sem, 16)

                def stack_k(i, g, half):
                    c0, c1 = ((0, HALF), (HALF, CTX))[half]
                    row = 0
                    for part, times in ((0, 3), (1, 2), (2, 1)):
                        src = k_dram[i, part, g * GROUP * HD:(g + 1) * GROUP * HD, c0:c1].rearrange("(h e) s -> e h s", e=HD)
                        for r in range(times):
                            sp.dma_start(k_stack[row:row + HD, g % 2, :, c0:c1], src).then_inc(k_stacked[g % 2][half].sem, 16)
                            row += HD

                def write_q(i):
                    sp.wait_ge(*q_parts_ready(i, 1))
                    for k in range(KT):
                        sp.dma_start(q_dram[i, :, k * P:(k + 1) * P, :].rearrange("n p s -> p n s"), q_part[:, :, k, :]).then_inc(q_written.sem, 16)
                    sp.wait_ge(*q_written(i, 32))

                def stack_q(i, g, waits=()):
                    row = 0
                    for parts in (3, 2, 1):
                        for part in range(parts):
                            src = q_dram[i, part, g * GROUP * HD:(g + 1) * GROUP * HD, :].rearrange("(h e) s -> e h s", e=HD)
                            if row // HD < len(waits):
                                sp.wait_ge(*waits[row // HD])
                            sp.dma_start(q_stack[row:row + HD, g * GROUP:(g + 1) * GROUP], src).then_inc(q_stacked[g].sem, 16)
                            row += HD

                def stack_max(i, g):
                    sp.wait_ge(*max_row_ready(i, g + 1))
                    for n in range(PARTS):
                        sp.dma_start(q_stack[STACK + n:STACK + n + 1, g * GROUP:(g + 1) * GROUP, :],
                                     max_row[n * GROUP:(n + 1) * GROUP, :]).then_inc(max_stacked.sem, 16)

                def load_ctx(i):
                    sp.wait_ge(*v_psum(i - 1, 7))
                    sp.dma_start(ctxT[:], d["ctxT"][i % BATCH].rearrange("(k p) s -> p k s", p=P)).then_inc(ctx_in.sem, 16)

                def store(i):
                    sp.wait_ge(*behind_done(i, 1))
                    sp.dma_start(out[i].rearrange("(j p) c -> p j c", p=P), x6[:]).then_inc(stored.sem, 16)

                def ahead(i):
                    for u in range(2 * CHUNKS):
                        write_k(i, u)
                    for k in k_written:
                        sp.wait_ge(*k(i, k.per))
                    for g in range(2):
                        for half in range(2):
                            stack_k(i, g, half)
                    write_q(i)
                    stack_q(i, 0)
                    for g in range(1, GROUPS):
                        stack_q(i, g)
                    load_ctx(i + 1)
                    stack_max(i, 0)

                def body(i, first, more):
                    for g in range(GROUPS):
                        ni, ng = (i, g + 2) if g + 2 < GROUPS else (i + 1, g + 2 - GROUPS)
                        if g + 2 < GROUPS or more:
                            sp.wait_ge(*score_psum(i, g * STEPS + HALF_STEPS))
                            stack_k(ni, ng, 0)
                        if g + 1 < GROUPS or more:
                            stack_max(*following(i, g))
                        if g + 2 < GROUPS or more:
                            sp.wait_ge(*score_psum(i, (g + 1) * STEPS))
                            stack_k(ni, ng, 1)
                        if more and g == 0:
                            write_q(i + 1)
                            stack_q(i + 1, 0)
                        elif more and g == 1:
                            for u in range(2 * CHUNKS):
                                write_k(i + 1, u)
                            stack_q(i + 1, 1, [k(i + 1, k.per) for k in k_written])
                        elif more and g == 2:
                            stack_q(i + 1, 2)
                        elif more and g == 3:
                            stack_q(i + 1, 3)
                            load_ctx(i + 2)
                    if not first:
                        store(i - 1)

                passes(sp, ahead, body, store)
                sp.wait_ge(stored.sem, 16 * (BATCH + 1))
                sp.wait_ge(ctx_in.sem, 16 * (BATCH + 1))

            @block.gpsimd
            def _(pool):
                for t, v in ((eps, LN_EPS), (fw_eps, FW_EPS), (l2_eps, 2 * L2_EPS), (half_neg, -0.5), (half_pos, 0.5)):
                    pool.memset(t[:], v).then_inc(set_.sem, 1)
                pool.memset(v_all[:], 0.0).then_inc(set_.sem, 1)
                pool.wait_ge(set_.sem, 6)
                pool.memset(v_sb[:, :, :, HD:HD + 1], 1.0).then_inc(set_.sem, 1)
                pool.tensor_copy(ident_b[:], ident[:]).then_inc(set_.sem, 1)

                def root_of_var(i, wait, done, k, cols, e, step, n):
                    pool.wait_ge(*wait(i, k))
                    pool.tensor_tensor(var_eps[:, 0:cols], mean_var[:, 0:cols, 1], e[:, 0:cols], ALU.add).then_inc(step.sem, 1)
                    pool.wait_ge(*step(i, n))
                    pool.tensor_tensor(rstd[:, 0:cols], var_eps[:, 0:cols], half_neg[:, 0:cols], ALU.pow).then_inc(done.sem, 1)

                def ahead_step_at(i, s):
                    if s == 6:
                        root_of_var(i, stats_ready, rstd_ready, 1, TOK, eps, pool_ahead, 1)
                    elif s == 17:
                        pool.wait_ge(*fq_squares(i, 1))
                        pool.tensor_tensor(q_norm[:], q_norm[:], half_pos[:], ALU.pow).then_inc(pool_ahead.sem, 1)
                        pool.wait_ge(*pool_ahead(i, 2))
                        pool.tensor_tensor(q_norm[:], q_norm[:], l2_eps[:], ALU.add).then_inc(rstd_ready.sem, 1)
                    elif s == 29:
                        root_of_var(i, stats_ready, rstd_ready, 2, 4, fw_eps, pool_ahead, 3)
                    elif s == 37:
                        root_of_var(i, stats_ready, rstd_ready, 3, TOK, eps, pool_ahead, 4)
                    if s - 6 in K_AT:
                        u = K_AT.index(s - 6)
                        m, sl = width(u % CHUNKS), u % K_SLOTS
                        pool.wait_ge(*k_part1_ready(i, u + 1))
                        pool.tensor_tensor(k_part[:, sl, 2, 0:m], k_full[:, sl, 0:m], k_part[:, sl, 1, 0:m],
                                           ALU.subtract).then_inc(k_parts_ready.sem, 1)
                    if s - 3 in K_AT:
                        u = K_AT.index(s - 3)
                        m, sl = width(u % CHUNKS), u % K_SLOTS
                        pool.wait_ge(*k_full_ready(i, u + 1))
                        pool.tensor_tensor(k_full[:, sl, 0:m], k_full[:, sl, 0:m], k_part[:, sl, 0, 0:m],
                                           ALU.subtract).then_inc(k_rest_ready.sem, 1)

                def ahead(i):
                    for s in steps_alone:
                        ahead_step_at(i, s)

                def behind(i):
                    root_of_var(i, b_stats_ready, b_rstd_ready, 1, TOK, eps, pool_behind, 1)

                def body(i, first, more):
                    if more:
                        for s in range(GROUPS * STEPS):
                            ahead_step_at(i + 1, s)
                    if not first:
                        behind(i - 1)

                passes(pool, ahead, body, behind)

            @block.scalar
            def _(act):
                act.wait_ge(const_in.sem, 16 * len(consts_list))
                act.wait_ge(set_.sem, 8)

                def ahead_step_at(i, s):
                    if s in (11, 40):
                        k = 1 if s == 11 else 2
                        act.wait_ge(*lnT_psum(i, k))
                        act.copy(wide(lnT), bank[5][:]).then_inc(lnT_ready.sem, 1)
                    elif s == 15:
                        act.wait_ge(*fq_psum(i, 1))
                        act.activation(wide(q_tanh), bank[4][:], ACT.Tanh, scale=0.5).then_inc(fq_tanh.sem, 1)
                    elif s == 17:
                        act.wait_ge(*s_in_ready(i, 1))
                        act.activation(s_tanh[:], s_in[:], ACT.Tanh, scale=0.5).then_inc(s_tanh_ready.sem, 1)
                    elif s == 20:
                        act.wait_ge(*fqT_psum(i, 1))
                        for j in range(TOK):
                            last = act.copy(qT[:, j].rearrange("p t h -> p h t"),
                                            bank[5][:, j * SEQ:(j + 1) * SEQ].rearrange("p (h t) -> p h t", h=2))
                        last.then_inc(fqT_ready.sem, 1)
                    elif s == 24:
                        act.wait_ge(*fg_psum(i, 1))
                        act.activation(f_tanh[:], bank[5][:], ACT.Tanh, scale=0.5).then_inc(fg_tanh.sem, 1)
                    elif s == 33:
                        act.wait_ge(*foT_psum(i, 1))
                        act.copy(wide(foT), bank[5][:]).then_inc(foT_ready.sem, 1)
                    if s - 2 in K_AT:
                        u = K_AT.index(s - 2)
                        a, sl = u // CHUNKS, u % K_SLOTS
                        m = width(u % CHUNKS)
                        act.wait_ge(*k_psum(i, u + 1))
                        if u >= K_SLOTS:
                            act.wait_ge(*k_written[sl](i, 16 * (u // K_SLOTS)))
                        act.activation(k_full[:, sl, 0:m], kv_bank(i, u)[:, 0:m], ACT.Identity, bias=bk[:, a:a + 1])
                        act.activation(k_part[:, sl, 0, 0:m], kv_bank(i, u)[:, 0:m], ACT.Identity,
                                       bias=bk[:, a:a + 1]).then_inc(k_full_ready.sem, 1)
                    if s - 5 in K_AT:
                        u = K_AT.index(s - 5)
                        m, sl = width(u % CHUNKS), u % K_SLOTS
                        act.wait_ge(*k_rest_ready(i, u + 1))
                        act.copy(k_part[:, sl, 1, 0:m], k_full[:, sl, 0:m]).then_inc(k_part1_ready.sem, 1)

                def copy_v(i, g0, g1):
                    act.wait_ge(*v_ready(i, 7))
                    act.copy(v_sb[:, :, g0 * GROUP:g1 * GROUP, 0:HD],
                             v_ahead[:, :, g0 * GROUP * HD:g1 * GROUP * HD].rearrange("p t (h e) -> p t h e", e=HD)).then_inc(v_copied.sem, 1)

                def behind_step_at(i, s):
                    if s == 83:
                        act.wait_ge(*b_lnT_psum(i, 1))
                        act.copy(wide(lnT), bank[5][:]).then_inc(b_lnT_ready.sem, 1)
                    elif s - 1 in GU_AT:
                        p = GU_AT.index(s - 1)
                        act.wait_ge(*gu_psum(i, p + 1))
                        if p >= 1:
                            act.wait_ge(*gu_ready(i, p))
                        act.activation(f_tanh[:], bank[4][:], ACT.Tanh, scale=0.5).then_inc(gu_tanh.sem, 1)

                def copy_u(i, g):
                    act.wait_ge(*tiles_added(i, PAIRS * (g + 1)))
                    if g >= 1 or not isinstance(i, int) or i >= 1:
                        act.wait_ge(*head_ready(i, g))
                    act.copy(u_sb[:], bank[6][:, 0:SEQ]).then_inc(u_ready.sem, 1)

                def body(i, first, more):
                    for g in range(GROUPS):
                        for t in range(STEPS):
                            n, b, s = g * STEPS + t, min(t // 4, PAIRS - 1), g * STEPS + t
                            act.wait_ge(*score_psum(i, n + 1))
                            if not first or g * PAIRS + b >= 2:
                                act.wait_ge(*tiles_added(i, g * PAIRS + b - 1))
                            if t < STEPS - 2:
                                act.activation(probs[:, (g * PAIRS + b) % 2, t % 4].rearrange("p t s -> p (t s)"), bank[2 + n % 2][:],
                                               ACT.Exp).then_inc(prob_ready.sem, 1)
                            else:
                                m = rows(CTILES - 1)
                                act.activation(probs[0:m, (g * PAIRS + b) % 2, t % 2 * 2:t % 2 * 2 + 2, 0, :],
                                               bank[2 + n % 2][0:m, :].rearrange("p (h s) -> p h s", h=2),
                                               ACT.Exp).then_inc(prob_ready.sem, 1)
                            if t == 3 and not (first and g == 0):
                                copy_u(*preceding(i, g))
                            if s == 4 and not first:
                                copy_v(i, 3, 4)
                            if more:
                                ahead_step_at(i + 1, s)
                            if s == 81 and more:
                                act.wait_ge(*tiles_added(i, 3 * PAIRS))
                                copy_v(i + 1, 0, 3)
                            if not first:
                                behind_step_at(i - 1, s)
                    
                def ahead(i):
                    for s in steps_alone:
                        ahead_step_at(i, s)
                    copy_v(i, 0, 3)
                    copy_v(i, 3, 4)

                def behind(i):
                    copy_u(i, GROUPS - 1)
                    for s in range(GROUPS * STEPS):
                        behind_step_at(i, s)

                passes(act, ahead, body, behind)

            @block.vector
            def _(dve):
                dve.memset(k_stack[STACK:P], 1.0).then_inc(ones_set.sem, 1)
                dve.memset(v_ahead[:, CTILES - 1, :], 0.0).then_inc(ones_set.sem, 1)
                dve.wait_ge(const_in.sem, 16 * len(consts_list))
                dve.wait_ge(ones_set.sem, 2)
                dve.wait_ge(set_.sem, 8)

                def moments(i, src, count, step, n, ready):
                    for j in range(count):
                        last = dve.bn_stats(stats[:, j, :], src(j))
                    last.then_inc(step.sem, 1)
                    dve.wait_ge(*step(i, n))
                    dve.memset(wait_pad[:], 0.0)
                    for j in range(count):
                        last = dve.bn_aggr(mean_var[:, j, :], stats[:, j, :])
                    last.then_inc(ready.sem, 1)

                def normalize(src, ready):
                    for j in range(TOK):
                        last = dve.tensor_scalar(lnx[:, j, :], src(j), mean_var[:, j, 0:1], rstd[:, j:j + 1],
                                                 ALU.subtract, ALU.mult)
                    last.then_inc(ready.sem, 1)

                def ahead_step_at(i, s):
                    def step(ins, n):
                        ins.then_inc(ahead_step.sem, 1)
                        dve.wait_ge(*ahead_step(i, n))

                    def x3(j):
                        return x_all[:, TOK * i + j, :]

                    fo_p = bank[4][:].rearrange("p (a b) -> p a b", b=P)
                    if s == 5:
                        moments(i, x3, TOK, ahead_step, 1, stats_ready)
                    elif s == 8:
                        dve.wait_ge(*rstd_ready(i, 1))
                        normalize(x3, norm_ready)
                    elif s == 16:
                        dve.wait_ge(*s_psum(i, 1))
                        dve.tensor_tensor(s_in[:].rearrange("p (j g) -> p j g", g=2), bank[5][:, 0:4].rearrange("p (j g) -> p j g", g=2),
                                          b_s[:].unsqueeze(1).to_broadcast([P, TOK, 2]), ALU.add).then_inc(s_in_ready.sem, 1)
                        dve.wait_ge(*fq_tanh(i, 1))
                        step(dve.scalar_tensor_tensor(wide(q_silu), wide(q_tanh), 1.0, bank[4][:], ALU.add, ALU.mult), 2)
                        step(dve.tensor_tensor(q_sq[:], q_silu[:], q_silu[:], ALU.mult), 3)
                        dve.tensor_reduce(q_norm[:], q_sq[:], AX.X, ALU.add).then_inc(fq_squares.sem, 1)
                    elif s == 18:
                        dve.wait_ge(*rstd_ready(i, 2))
                        step(dve.reciprocal(q_norm[:], q_norm[:]), 4)
                        dve.tensor_tensor(q_silu[:], q_silu[:], q_norm[:].unsqueeze(2).to_broadcast([P, 4, P]),
                                          ALU.mult).then_inc(fq_ready.sem, 1)
                    elif s == 21:
                        dve.wait_ge(*s_tanh_ready(i, 1))
                        step(dve.scalar_tensor_tensor(s_in[:], s_tanh[:], 1.0, s_in[:], ALU.add, ALU.mult), 5)
                    elif s == 25:
                        dve.wait_ge(*fg_tanh(i, 1))
                        step(dve.scalar_tensor_tensor(f_silu[:], f_tanh[:], 1.0, bank[5][:], ALU.add, ALU.mult), 6)
                        dve.scalar_tensor_tensor(f_h[:], f_silu[:], 0.5, bank[4][:], ALU.mult, ALU.mult).then_inc(fh_ready.sem, 1)
                    elif s == 28:
                        dve.wait_ge(*fo_psum(i, 1))
                        moments(i, lambda j: fo_p[:, j, :], 4, ahead_step, 7, stats_ready)
                    elif s == 30:
                        dve.wait_ge(*rstd_ready(i, 3))
                        for j in range(4):
                            last = dve.tensor_scalar(fo[:, j, :], fo_p[:, j, :], mean_var[:, j, 0:1], rstd[:, j:j + 1], ALU.subtract, ALU.mult)
                        step(last, 8)
                        step(dve.tensor_tensor(fo[:], fo[:], fw_g[:].unsqueeze(1).to_broadcast([P, 4, P]), ALU.mult), 9)
                        step(dve.tensor_tensor(fo[:], fo[:], fw_b[:].unsqueeze(1).to_broadcast([P, 4, P]), ALU.add), 10)
                        dve.scalar_tensor_tensor(fo[:], fo[:], 0.5, s_in[:].unsqueeze(2).to_broadcast([P, 4, P]), ALU.mult,
                                                 ALU.mult).then_inc(fo_ready.sem, 1)
                    elif s == 36:
                        dve.wait_ge(*fwo_psum(i, 1))
                        for j in range(TOK):
                            last = dve.tensor_tensor(x4_ahead[:, j, :], x3(j), bank[4][:, j * DIM:(j + 1) * DIM], ALU.add)
                        last.then_inc(x4_ready.sem, 1)
                        dve.wait_ge(*x4_ready(i, 1))
                        moments(i, lambda j: x4_ahead[:, j, :], TOK, ahead_step, 11, stats_ready)
                    elif s == 38:
                        dve.wait_ge(*rstd_ready(i, 4))
                        normalize(lambda j: x4_ahead[:, j, :], norm_ready)
                    elif s == 43:
                        dve.wait_ge(*q_psum(i, 1))
                        for k in range(KT):
                            last = dve.tensor_scalar(q_full[:, k, :], bank[4][:, k * SEQ:(k + 1) * SEQ], bq[:, k:k + 1], QK_SCALE,
                                                     ALU.add, ALU.mult)
                        step(last, 12)
                        dve.tensor_copy(q_part[:, 0], q_full[:]).then_inc(ahead_step.sem, 1)
                    elif s == 44:
                        dve.wait_ge(*ahead_step(i, 13))
                        step(dve.tensor_tensor(q_full[:], q_full[:], q_part[:, 0], ALU.subtract), 14)
                        step(dve.tensor_copy(q_part[:, 1], q_full[:]), 15)
                        dve.tensor_tensor(q_part[:, 2], q_full[:], q_part[:, 1], ALU.subtract).then_inc(q_parts_ready.sem, 1)
                    if s - 2 in V_AT[::2]:
                        b = V_AT[::2].index(s - 2)
                        if b == 0 and (not isinstance(i, int) or i >= 1):
                            dve.wait_ge(*v_copied(i, 0))
                        dve.wait_ge(*v_psum(i, b + 1))
                        for t in range(2 * b, min(2 * b + 2, CTILES)):
                            m = rows(t)
                            last = dve.tensor_tensor(v_ahead[0:m, t, :], kv_bank(i, b)[0:m, t % 2 * DIM:(t % 2 + 1) * DIM], bv[0:m], ALU.add)
                        last.then_inc(v_ready.sem, 1)

                def behind_step_at(i, s):
                    def step(ins, n):
                        ins.then_inc(behind_step.sem, 1)
                        dve.wait_ge(*behind_step(i, n))

                    if s == 10:
                        dve.wait_ge(*co_psum(i, 1))
                        for j in range(TOK):
                            last = dve.tensor_tensor(x5[:, j, :], x4[:, j, :], bank[4][:, j * DIM:(j + 1) * DIM], ALU.add)
                        step(last, 1)
                        dve.tensor_tensor(x5[:], x5[:], bo[:].unsqueeze(1).to_broadcast([P, TOK, DIM]), ALU.add).then_inc(x5_ready.sem, 1)
                    elif s == 78:
                        dve.wait_ge(*x5_ready(i, 1))
                        moments(i, lambda j: x5[:, j, :], TOK, behind_step, 2, b_stats_ready)
                    elif s == 80:
                        dve.wait_ge(*b_rstd_ready(i, 1))
                        normalize(lambda j: x5[:, j, :], b_norm_ready)
                    elif s - 2 in GU_AT:
                        p = GU_AT.index(s - 2)
                        dve.wait_ge(*gu_tanh(i, p + 1))
                        step(dve.scalar_tensor_tensor(f_silu[:], f_tanh[:], 1.0, bank[4][:], ALU.add, ALU.mult), 3 + p)
                        dve.scalar_tensor_tensor(gu[:, 2 * p:2 * p + 2, :].rearrange("p a b -> p (a b)"), f_silu[:], 0.5,
                                                 bank[5][:], ALU.mult, ALU.mult).then_inc(gu_ready.sem, 1)
                    elif s == 103:
                        dve.wait_ge(*ffn_psum(i, 1))
                        dve.wait_ge(*stored(i, 16))
                        for j in range(TOK):
                            last = dve.tensor_tensor(x6[:, j, :], x5[:, j, :], bank[4][:, j * DIM:(j + 1) * DIM], ALU.add)
                        last.then_inc(behind_done.sem, 1)

                def chunk_maxes(i, g, units):
                    for u in units:
                        c, n = u // (2 * GROUP), g * MAXES + u
                        dve.wait_ge(*max_psum(i, n + 1))
                        dve.tensor_reduce(chunk_max[:, u % (2 * GROUP), c:c + 1], bank[n % 2][:, 0:width(c)], AX.X,
                                          ALU.max).then_inc(max_read.sem, 1)

                def max_parts(i, g):
                    def step(ins, n):
                        ins.then_inc(max_step.sem, 1)
                        dve.wait_ge(*max_step(i, 4 * g + n))

                    dve.wait_ge(*max_read(i, (g + 1) * MAXES))
                    step(dve.tensor_reduce(neg_max[:], chunk_max[:], AX.X, ALU.max, negate=True), 1)
                    view = neg_max[:].rearrange("p (h j) -> p j h", j=TOK)
                    step(dve.tensor_copy(max_part[:, :, 0, :], view), 2)
                    step(dve.tensor_tensor(view, view, max_part[:, :, 0, :], ALU.subtract), 3)
                    step(dve.tensor_copy(max_part[:, :, 1, :], view), 4)
                    dve.tensor_tensor(max_part[:, :, 2, :], view, max_part[:, :, 1, :], ALU.subtract).then_inc(max_part_ready.sem, 1)

                def max_row_copy(i, g):
                    dve.wait_ge(*max_row_psum(i, g + 1))
                    if g >= 1 or not isinstance(i, int) or i >= 1:
                        dve.wait_ge(*max_stacked(i, 48 * g))
                    dve.tensor_copy(max_row[:], bank[7][0:PARTS * GROUP, 0:SEQ]).then_inc(max_row_ready.sem, 1)

                def finish_group(i, g):
                    dve.wait_ge(*den_psum(i, g + 1))
                    dve.reciprocal(den[:], bank[7][:, SEQ:]).then_inc(den_inverse.sem, 1)
                    dve.wait_ge(*den_inverse(i, g + 1))
                    dve.tensor_tensor(attT[:, g, :], u_sb[:], den[:], ALU.mult).then_inc(head_ready.sem, 1)

                def keep_x4(i):
                    dve.wait_ge(*x4_ready(i, 1))
                    if not isinstance(i, int) or i >= 1:
                        dve.wait_ge(*x5_ready(i, 0))
                    dve.tensor_copy(x4[:], x4_ahead[:]).then_inc(x4_kept.sem, 1)
                    dve.wait_ge(*x4_kept(i, 1))

                def body(i, first, more):
                    for g in range(GROUPS):
                        for t in range(STEPS):
                            s = g * STEPS + t
                            ni, ng = following(i, g)
                            chunk_maxes(ni, ng, maxes_before(g, t, more))
                            if t == MAX_BY and (g < GROUPS - 1 or more):
                                max_parts(ni, ng)
                            if t == MAX_BY + 2 and (g < GROUPS - 1 or more):
                                max_row_copy(ni, ng)
                            if t == 7 and not (first and g == 0):
                                finish_group(*preceding(i, g))
                            if not first:
                                behind_step_at(i - 1, s)
                            if s == 11:
                                keep_x4(i)
                            if more:
                                ahead_step_at(i + 1, s)

                def ahead(i):
                    for s in steps_alone:
                        ahead_step_at(i, s)
                    chunk_maxes(i, 0, range(MAXES))
                    max_parts(i, 0)
                    max_row_copy(i, 0)

                def behind(i):
                    finish_group(i, GROUPS - 1)
                    for s in range(GROUPS * STEPS):
                        behind_step_at(i, s)

                passes(dve, ahead, body, behind)

            @block.tensor
            def _(pe):
                def transposed(dst, src):
                    for a in range(KT):
                        for b in range(TOK):
                            last = pe.transpose(dst[:, a * SEQ + b * P:a * SEQ + (b + 1) * P], src[:, b, a * P:(a + 1) * P], ident[:])
                    return last

                def channels_out(dst, weight, act_t, a):
                    for k in range(KT):
                        last = pe.matmul(dst, weight[:, k, a * P:(a + 1) * P], act_t[:, k, :], start=(k == 0), stop=(k == KT - 1))
                    return last

                def tokens_out(dst, weight, act_t, tiles=range(TOK)):
                    for j in tiles:
                        for k in range(KT):
                            last = pe.matmul(dst[:, j * DIM:(j + 1) * DIM], act_t[:, k, j * P:(j + 1) * P], weight[:, k, :],
                                             start=(k == 0), stop=(k == KT - 1))
                    return last

                pe.wait_ge(weights_in.sem, 16 * len(w_names))
                pe.wait_ge(const_in.sem, 16 * len(consts_list))
                pe.wait_ge(set_.sem, 8)
                pe.wait_ge(ones_set.sem, 2)

                def ahead_step_at(i, s):
                    if s == 10:
                        pe.wait_ge(*norm_ready(i, 1))
                        transposed(bank[5], lnx).then_inc(lnT_psum.sem, 1)
                    elif s == 13:
                        pe.wait_ge(*lnT_ready(i, 1))
                        if not isinstance(i, int):
                            pe.wait_ge(*x5_ready(i - 1, 0))
                        tokens_out(bank[4], w["FWq"], lnT, (0,))
                    elif s == 14:
                        tokens_out(bank[4], w["FWq"], lnT, (1,)).then_inc(fq_psum.sem, 1)
                    elif s == 15:
                        for j in range(TOK):
                            for k in range(KT):
                                last = pe.matmul(bank[5][:, 2 * j:2 * j + 2], lnT[:, k, j * P:(j + 1) * P], w_s[:, k, :],
                                                 start=(k == 0), stop=(k == KT - 1))
                        last.then_inc(s_psum.sem, 1)
                    elif s == 19:
                        pe.wait_ge(*s_in_ready(i, 1))
                        pe.wait_ge(*fq_ready(i, 1))
                        for n in range(4):
                            last = pe.transpose(bank[5][:, n * P:(n + 1) * P], q_silu[:, n, :], ident[:])
                        last.then_inc(fqT_psum.sem, 1)
                    elif s in (22, 23):
                        if s == 22:
                            pe.wait_ge(*fqT_ready(i, 1))
                        b, name = (4, "w2T") if s == 22 else (5, "w0T")
                        for g in range(2):
                            last = pe.matmul(bank[b][:, g * SEQ:(g + 1) * SEQ], fast[name][:, g, :],
                                             qT[:, g].rearrange("p t h -> p (t h)"), start=True, stop=True)
                        if s == 23:
                            last.then_inc(fg_psum.sem, 1)
                    elif s == 27:
                        pe.wait_ge(*fh_ready(i, 1))
                        for j in range(TOK):
                            for g in range(2):
                                last = pe.matmul(bank[4][:, (2 * j + g) * P:(2 * j + g + 1) * P], f_h[:, g * SEQ + j * P:g * SEQ + (j + 1) * P],
                                                 fast["w1T"][:, g, :], start=True, stop=True)
                        last.then_inc(fo_psum.sem, 1)
                    elif s == 32:
                        pe.wait_ge(*fo_ready(i, 1))
                        transposed(bank[5], fo[:].rearrange("p (j g) e -> p j (g e)", g=2)).then_inc(foT_psum.sem, 1)
                    elif s == 34:
                        pe.wait_ge(*foT_ready(i, 1))
                        tokens_out(bank[4], w["FWo"], foT, (0,))
                    elif s == 35:
                        tokens_out(bank[4], w["FWo"], foT, (1,)).then_inc(fwo_psum.sem, 1)
                    elif s == 39:
                        pe.wait_ge(*norm_ready(i, 2))
                        transposed(bank[5], lnx).then_inc(lnT_psum.sem, 1)
                    elif s == 41:
                        pe.wait_ge(*lnT_ready(i, 2))
                        channels_out(bank[4][:, 0:SEQ], w["CWq"], lnT, 0)
                    elif s == 42:
                        channels_out(bank[4][:, SEQ:], w["CWq"], lnT, 1).then_inc(q_psum.sem, 1)
                    if s in K_AT:
                        u = K_AT.index(s)
                        a, c = u // CHUNKS, u % CHUNKS
                        if u == 0:
                            pe.wait_ge(*ctx_in(i, 16))
                        if u == 0 and not alone(i):
                            pe.wait_ge(*q_parts_ready(i, 1))
                        if u >= 2:
                            pe.wait_ge(*k_full_ready(i, u - 1))
                    for k in range(KT):
                        if s - k in K_AT:
                            u = K_AT.index(s - k)
                            a, c = u // CHUNKS, u % CHUNKS
                            last = pe.matmul(kv_bank(i, u)[:, 0:width(c)], w["CWk"][:, k, a * P:(a + 1) * P],
                                             ctxT[:, k, c * CHUNK:c * CHUNK + width(c)], start=(k == 0), stop=(k == KT - 1))
                            if k == KT - 1:
                                last.then_inc(k_psum.sem, 1)
                    if s in V_AT:
                        t = V_AT.index(s)
                        b, m = t // 2, rows(t)
                        if t in (0, 2):
                            pe.wait_ge(*k_full_ready(i, 2 * CHUNKS - 1 + b))
                        elif t % 2 == 0:
                            pe.wait_ge(*v_ready(i, b - 1))
                        for k in range(KT):
                            last = pe.matmul(kv_bank(i, b)[0:m, t % 2 * DIM:(t % 2 + 1) * DIM], ctxT[:, k, t * P:t * P + m],
                                             w["CWv"][:, k, :], start=(k == 0), stop=(k == KT - 1))
                        if t % 2 == 1 or t == CTILES - 1:
                            last.then_inc(v_psum.sem, 1)

                def behind_step_at(i, s, alone=False):
                    if s == 8:
                        pe.wait_ge(*head_ready(i, GROUPS))
                        for j in range(TOK):
                            for g in range(GROUPS):
                                last = pe.matmul(bank[4][:, j * DIM:(j + 1) * DIM], attT[:, g, j * P:(j + 1) * P], w["CWo"][:, g, :],
                                                 start=(g == 0), stop=(g == GROUPS - 1))
                        last.then_inc(co_psum.sem, 1)
                    elif s == 82:
                        pe.wait_ge(*b_norm_ready(i, 1))
                        transposed(bank[5], lnx).then_inc(b_lnT_psum.sem, 1)
                    elif s in GU_AT:
                        p = GU_AT.index(s)
                        if p == 0:
                            pe.wait_ge(*b_lnT_ready(i, 1))
                        else:
                            pe.wait_ge(*gu_ready(i, p))
                        for a in range(2):
                            channels_out(bank[4][:, a * SEQ:(a + 1) * SEQ], lut_w["gate"], lnT, 2 * p + a)
                    elif s - 1 in GU_AT:
                        p = GU_AT.index(s - 1)
                        for a in range(2):
                            last = channels_out(bank[5][:, a * SEQ:(a + 1) * SEQ], lut_w["up"], lnT, 2 * p + a)
                        last.then_inc(gu_psum.sem, 1)
                    elif s >= 98:
                        j, c0 = (s - 98) // 3, (s - 98) % 3 * 2
                        if s == 98:
                            pe.wait_ge(*gu_ready(i, IT // 2))
                        for c in (c0, c0 + 1):
                            m = min(P, INNER - c * P)
                            last = pe.matmul(bank[4][:, j * DIM:(j + 1) * DIM], gu[0:m, c, j * P:(j + 1) * P], lut_w["down"][0:m, c, :],
                                             start=(c == 0), stop=(c == IT - 1))
                        if s == 103:
                            last.then_inc(ffn_psum.sem, 1)

                def max_scores(i, g, units, first=False):
                    for u in units:
                        n, h, j, c = g * MAXES + u, u // 2 % GROUP, u % 2, u // (2 * GROUP)
                        if u == 0:
                            pe.wait_ge(*q_stacked[g](i, 96))
                        if u in (0, MAXES // 2):
                            pe.wait_ge(*k_stacked[g % 2][u * 2 // MAXES](i, 96 * (g // 2 + 1)))
                        if n >= 2 or not first:
                            pe.wait_ge(*max_read(i, n - 1))
                        pe.matmul(bank[n % 2][:, 0:width(c)], q_stack[0:STACK, g * GROUP + h, j * P:(j + 1) * P],
                                  k_stack[0:STACK, g % 2, h, c * CHUNK:c * CHUNK + width(c)], start=True,
                                  stop=True).then_inc(max_psum.sem, 1)

                def max_rows(i, g):
                    pe.wait_ge(*max_part_ready(i, g + 1))
                    for j in range(TOK):
                        last = pe.matmul(bank[7][0:PARTS * GROUP, j * P:(j + 1) * P],
                                         max_part[:, j].rearrange("p n h -> p (n h)"), ident_b[:], start=True, stop=True)
                    last.then_inc(max_row_psum.sem, 1)

                def scores(i, g, t, first):
                    n = g * STEPS + t
                    if t == 0:
                        pe.wait_ge(*max_stacked(i, 48 * (g + 1)))
                    if n >= 2 or not first:
                        pe.wait_ge(*prob_ready(i, n - 1))
                    for e in range(2):
                        h, tile = (t % 4, t // 4 * 2 + e) if t < STEPS - 2 else (t % 2 * 2 + e, CTILES - 1)
                        m = rows(tile)
                        last = pe.matmul(bank[2 + n % 2][0:m, e * SEQ:(e + 1) * SEQ], k_stack[0:DEEP, g % 2, h, tile * P:tile * P + m],
                                         q_stack[0:DEEP, g * GROUP + h, :], start=True, stop=True)
                    last.then_inc(score_psum.sem, 1)

                def add_values(i, g, tile, first):
                    b, m = tile // 2, rows(tile)
                    if tile % 2 == 0:
                        pe.wait_ge(*prob_ready(i, g * STEPS + min(4 * b + 4, STEPS)))
                    if tile == 0 and (g >= 1 or not first):
                        pe.wait_ge(*u_ready(i, g))
                    if tile == 0 and g in (0, GROUPS - 1):
                        pe.wait_ge(*v_copied(i, 1 if g == 0 else 2))
                    for h in range(GROUP):
                        last = pe.matmul(bank[6][32 * h:32 * h + 32, 0:SEQ], v_all[0:m, tile, (g * GROUP + h) * (HD + 1):(g * GROUP + h) * (HD + 1) + 32],
                                         probs[0:m, (g * PAIRS + b) % 2, h, tile % 2, :], start=(tile == 0), stop=(tile == CTILES - 1))
                    if tile % 2 == 1 or tile == CTILES - 1:
                        last.then_inc(tiles_added.sem, 1)

                def sum_rows(i, g):
                    pe.wait_ge(*u_ready(i, g + 1))
                    pe.matmul(bank[7][:, SEQ:], sel[:], u_sb[:], start=True, stop=True).then_inc(den_psum.sem, 1)

                def body(i, first, more):
                    for g in range(GROUPS):
                        for t in range(STEPS):
                            s = g * STEPS + t
                            ni, ng = following(i, g)
                            pi, pg = preceding(i, g)
                            scores(i, g, t, first)
                            units = maxes_before(g, t, more)
                            max_scores(ni, ng, units[:1])
                            if t == MAX_BY + 2 and (g < GROUPS - 1 or more):
                                max_rows(ni, ng)
                            if t < 2 and not (first and g == 0):
                                add_values(pi, pg, CTILES - 2 + t, first)
                            if t >= 5 and t % 4 < 3 and t % 4 > 0:
                                add_values(i, g, t // 4 * 2 - 2 + (t % 4 - 1), first)
                            if t == 5 and not (first and g == 0):
                                sum_rows(pi, pg)
                            if not first:
                                behind_step_at(i - 1, s)
                            if more:
                                ahead_step_at(i + 1, s)
                            max_scores(ni, ng, units[1:])

                def ahead(i):
                    for s in steps_alone:
                        ahead_step_at(i, s)
                    max_scores(i, 0, range(MAXES), True)
                    max_rows(i, 0)

                def behind(i):
                    add_values(i, GROUPS - 1, CTILES - 2, False)
                    add_values(i, GROUPS - 1, CTILES - 1, False)
                    sum_rows(i, GROUPS - 1)
                    for s in range(GROUPS * STEPS):
                        behind_step_at(i, s)

                passes(pe, ahead, body, behind)


def build(nc, d, out, stop_after=9):
    with ExitStack() as ctx:
        x_all = ctx.enter_context(nc.sbuf_tensor("x_all", [P, BATCH * TOK, DIM], F32))
        ident = ctx.enter_context(nc.sbuf_tensor("ident", [P, P], F32))
        lut_all = ctx.enter_context(nc.sbuf_tensor("lut_all", [P, 3 * 6 * DIM], F32))
        lut_w = {"all": lut_all,
                 "gate": lut_all[:, 0:6 * DIM].rearrange("p (k n) -> p k n", k=KT),
                 "up": lut_all[:, 6 * DIM:12 * DIM].rearrange("p (k n) -> p k n", k=KT),
                 "down": lut_all[:, 12 * DIM:].rearrange("p (c n) -> p c n", c=6)}
        x_loaded = Signal(ctx.enter_context(nc.semaphore("x_loaded")))
        x_view = d["x"].rearrange("b (j p) c -> p (b j) c", p=P)
        with nc.Block() as block:
            @block.sync
            def _(sp):
                sp.dma_start(x_all[:], x_view).then_inc(x_loaded.sem, 16)
                sp.dma_start(ident[:], d["ident"]).then_inc(x_loaded.sem, 16)
        attention_and_context(nc, d, x_all, x_loaded, {"ident": ident, "ones": None})
        if stop_after >= 3:
            experts(nc, d, x_all, x_loaded, ident, lut_w)
        if stop_after >= 6:
            fast_weights_softmax_and_lut(nc, d, out, x_all, x_loaded, ident, lut_w)
            return
        with nc.semaphore("stored") as stored, nc.Block() as block:
            @block.sync
            def _(sp):
                sp.dma_start(out.rearrange("b (j p) c -> p (b j) c", p=P), x_all[:]).then_inc(stored, 16)
                sp.wait_ge(stored, 16)


def layout(inputs):
    import numpy as np

    def a(n):
        return np.asarray(inputs[n])

    def t(n):
        return np.ascontiguousarray(a(n).T)

    def col(n):
        return np.ascontiguousarray(a(n).reshape(KT, P).T)

    d = {"x": a("x"), "ctxT": np.ascontiguousarray(a("ctx_2048").transpose(0, 2, 1))}
    for n in ("r", "k", "v", "g", "o"):
        d[f"W{n}T"] = t(f"L0_attn_W{n}")
    for n in ("k", "v", "r", "g"):
        d["maa_" + n] = col("L0_attn_time_maa_" + n)
    d["time_decay"] = a("L0_attn_time_decay").reshape(-1)
    d["faaaa"] = a("L0_attn_time_faaaa").reshape(-1)
    d["gamma"], d["beta"] = a("L0_attn_gamma"), a("L0_attn_beta")
    for n in ("q", "g", "kv", "o"):
        d[f"XW{n}T"] = t(f"L0_xattn_W{n}")
    d["xbg"] = col("L0_xattn_bg")
    key = np.arange(P)[:, None]
    tok = np.concatenate([np.arange(SEQ), np.arange(P)])[None, :]
    d["delta"] = np.maximum(tok - key - 1, 0).astype(np.float32)
    d["strict"] = (tok > key).astype(np.float32)
    d["diag"] = (tok == key).astype(np.float32)
    d["headmask"] = (np.arange(P)[:, None] // 8 == np.arange(P // 8)[None, :]).astype(np.float32)
    d["blk16"] = (np.arange(P)[:, None] // 16 == np.arange(P)[None, :] // 16).astype(np.float32)
    d["routerT"] = t("L0_ffn_router_w")
    for n in ("gate", "up", "down"):
        d[n + "T"] = np.ascontiguousarray(a(f"L0_ffn_{n}_w").transpose(0, 2, 1))
    d["lut"], d["lut_key"] = a("L1_ffn_lut"), np.arange(16, dtype=np.float32)
    for n in ("gate", "up"):
        d[n + "_idx"] = np.ascontiguousarray(np.pad(a(f"L1_ffn_{n}_idx").T, ((0, 0), (0, 768 - 688))))
    d["down_idx"] = np.ascontiguousarray(np.pad(a("L1_ffn_down_idx").T, ((0, 768 - 688), (0, 0))))
    qkv = a("L1_attn_W_qkv")
    d["FWq"] = np.ascontiguousarray(np.concatenate([qkv[:, 0:P], qkv[:, 3 * P:4 * P]], axis=1))
    d["FWo"], d["w_s"], d["b_s"] = a("L1_attn_W_o"), a("L1_attn_W_s"), a("L1_attn_b_s")
    d["fw_g"], d["fw_b"] = a("L1_attn_ln_g"), a("L1_attn_ln_b")
    for n in range(3):
        d[f"w{n}T"] = np.ascontiguousarray(a(f"L1_attn_w{n}").transpose(0, 2, 1))
    for n in ("q", "k", "v"):
        d["CW" + n] = t("L1_xattn_W" + n)
    d["CWo"] = np.ascontiguousarray(np.pad(a("L1_xattn_Wo").T.reshape(16, 16, DIM), ((0, 0), (0, 16), (0, 0))).reshape(512, DIM))
    d["bq"], d["bk"], d["bv"], d["bo"] = col("L1_xattn_bq"), col("L1_xattn_bk"), a("L1_xattn_bv"), a("L1_xattn_bo")
    rows_, cols_ = np.arange(P)[:, None], np.arange(P)[None, :]
    d["sel"] = ((rows_ % 32 == 16) & (rows_ // 32 == cols_ // 32)).astype(np.float32)
    d["earlier"] = np.tril(np.ones((8, 8), np.float32), -1)
    d["ident"] = np.eye(P, dtype=np.float32)
    return d


def kernel(**inputs):
    import concourse.bacc as bacc
    from concourse.bass_utils import run_bass_kernel_spmd

    nc = bacc.Bacc("TRN2", target_bir_lowering=False, num_devices=1)
    arrays = {"in_" + k: v for k, v in layout(inputs).items()}
    d = {k[3:]: nc.dram_tensor(k, v.shape, mybir.dt.from_np(v.dtype), kind="ExternalInput").ap() for k, v in arrays.items()}
    out = nc.dram_tensor("out", (BATCH, SEQ, DIM), F32, kind="ExternalOutput").ap()
    build(nc, d, out)
    r = run_bass_kernel_spmd(nc, [arrays], core_ids=[0])
    return r.results[0]["out"]
```

```python
from contextlib import ExitStack

import concourse.bass as bass
import concourse.mybir as mybir

F32 = mybir.dt.float32
BF16 = mybir.dt.bfloat16
F32R = mybir.dt.float32r
I32 = mybir.dt.int32
ALU = mybir.AluOpType
ACT = mybir.ActivationFunctionType
AX = mybir.AxisListType

P = 128
BATCH, SEQ, DIM = 4, 256, 256
TOK = SEQ // P
KT = DIM // P
CTX = 1601
CTILES = -(-CTX // P)
LN_EPS = 1e-5


class Signal:

    def __init__(self, sem, per=0, before=0):
        self.sem, self.per, self.before = sem, per, before

    def __call__(self, i, k):
        return self.sem, i * self.per + (self.before + k)


def rows(t):
    return min(P, CTX - t * P)


def attention_and_context(nc, d, x_all, ident):
    HEADS, HD = 32, 8
    GROUP_EPS = 1e-5 * 144
    ZEPS = 1e-6
    SC = SEQ + P
    RING = 3
    ATTS = 8
    with ExitStack() as ctx:
        def sb(name, shape, dt=F32):
            return ctx.enter_context(nc.sbuf_tensor(name, shape, dt))

        def sig(name, per=0):
            return Signal(ctx.enter_context(nc.semaphore(name)), per)

        bank = [ctx.enter_context(nc.psum_tensor(f"a_bank{n}", [P, 512], F32)) for n in range(8)]

        w_names = ["WrT", "WkT", "WvT", "WgT", "WoT", "XWqT", "XWgT", "XWoT"]
        w = {n: sb("a_" + n, [P, KT, DIM]) for n in w_names}
        w["XWkvT"] = sb("a_XWkvT", [P, KT, 2 * DIM])
        cols = {n: sb("a_" + n, [P, KT]) for n in ["maa_k", "maa_v", "maa_r", "maa_g", "xbg"]}
        gamma, beta = sb("gamma", [P, DIM]), sb("beta", [P, DIM])
        delta, strict, diag = sb("delta", [P, SC]), sb("strict", [P, SC]), sb("diag", [P, SC])
        headmask, blk16 = sb("headmask", [P, P // HD]), sb("blk16", [P, P])
        logw, faaaa = sb("logw", [P, HEADS]), sb("faaaa", [P, HEADS])
        decay = sb("decay", [P, HEADS, SC])
        ctxT = sb("ctxT", [P, KT, CTX])
        mean_var, stats = sb("a_mean_var", [P, TOK, 2]), sb("a_stats", [P, TOK, 6])
        rstd, half_neg = sb("a_rstd", [P, TOK]), sb("a_half_neg", [P, TOK])
        var_eps, eps = sb("a_var_eps", [P, TOK]), sb("a_eps", [P, TOK])
        lnx = sb("a_lnx", [P, TOK, DIM])
        wait_pad = sb("a_wait_pad", [P, 1])
        lnT = sb("a_lnT", [P, KT, SEQ + 1])
        ln2T = sb("a_ln2T", [P, KT, SEQ])
        diff = sb("diff", [P, KT, SEQ])
        mix = {n: sb("mix_" + n, [P, KT, SEQ]) for n in "krvg"}
        r_sb, k_sb = sb("r_sb", [P, KT, SEQ]), sb("k_sb", [P, KT, SEQ])
        r_head = sb("r_head", [P, ATTS, SEQ])
        v_pad = sb("v_pad", [P, TOK, 8, 4 * 40])
        att = sb("att", [P, ATTS, SC])
        y_sb, g_tanh, g_silu = sb("y_sb", [P, KT, SEQ]), sb("g_tanh", [P, TOK, DIM]), sb("g_silu", [P, TOK, DIM])
        y_c, y_sq = sb("y_c", [P, TOK * HEADS, HD]), sb("y_sq", [P, TOK * HEADS, HD])
        g_mean, g_var, g_rstd = (sb(n, [P, TOK * HEADS]) for n in ("g_mean", "g_var", "g_rstd"))
        g_bits, g_square = sb("g_bits", [P, TOK * HEADS], I32), sb("g_square", [P, TOK * HEADS])
        zT = sb("zT", [P, KT, SEQ])
        x1 = sb("x1", [P, TOK, DIM])
        k_min, k_exp, k_feat = (sb(n, [P, 2, DIM]) for n in ("k_min", "k_exp", "k_feat"))
        v_ones = sb("v_ones", [P, 2, KT, P + 1])
        kv_m, ks_m = sb("kv_m", [P, KT, P]), sb("ks_m", [P, KT, P])
        ks_col = sb("ks_col", [P, KT])
        q_min, q_exp, q_feat = (sb(n, [P, KT, SEQ]) for n in ("q_min", "q_exp", "q_feat"))
        gate, den, aT = sb("gate", [P, KT, SEQ]), sb("den", [P, KT, SEQ]), sb("aT", [P, KT, SEQ])
        hbg = sb("hbg", [P, KT])

        x_loaded = sig("x_loaded")
        const_in, weights_in, kv_weights_in = sig("a_const_in"), sig("a_weights_in"), sig("kv_weights_in")
        ctx_in = sig("ctx_in", 16)
        logw_exp, logw_ready, decay_exp, decay_ready = (sig(n) for n in ("logw_exp", "logw_ready", "decay_exp", "decay_ready"))
        zeroed = sig("zeroed")
        tri_masked, tri_copied = sig("tri_masked"), sig("tri_copied")
        batch_done = sig("a_batch_done", 1)
        NEWTON = 3
        VSTEPS, GSTEPS = 16 + 3 + 3 * NEWTON, 2
        vstep, gstep = sig("a_vstep", VSTEPS), sig("a_gstep", GSTEPS)
        stats_ready, rstd_ready, ln_ready = sig("a_stats_ready", 2), sig("a_rstd_ready", 2), sig("a_ln_ready", 2)
        lnT_psum, lnT_ready = sig("a_lnT_psum", 2), sig("a_lnT_ready", 2)
        ctx_psum, k_min_ready, k_exp_ready = sig("ctx_psum", CTILES), sig("k_min_ready", CTILES), sig("k_exp_ready", CTILES)
        k_feat_ready, v_ready, kv_added = sig("k_feat_ready", CTILES), sig("v_ready", CTILES), sig("kv_added", CTILES)
        kv_ready = sig("kv_ready", 1)
        mix_ready = sig("mix_ready", 4)
        proj_psum, proj_read = sig("proj_psum", 4), sig("proj_read", 4)
        g_ready = sig("g_ready", 1)
        r_head_ready = sig("r_head_ready", HEADS)
        score_psum, att_ready, group_added = sig("score_psum", HEADS), sig("att_ready", HEADS), sig("group_added", 8)
        yt_psum, first_stats = sig("yt_psum", 1), sig("first_stats", 1)
        z_ready = sig("z_ready", 1)
        zT_psum, o_psum = sig("zT_psum", 1), sig("o_psum", 1)
        y_copies = sig("y_copies").sem
        y_ready, zT_ready = Signal(y_copies, 2), Signal(y_copies, 2, 1)
        q_psum, q_min_ready, q_exp_ready, q_feat_ready = (sig(n, 1) for n in ("q_psum", "q_min_ready", "q_exp_ready", "q_feat_ready"))
        gate_psum, gate_tanh, num_psum, den_psum = (sig(n, 1) for n in ("gate_psum", "gate_tanh", "num_psum", "den_psum"))
        aT_ready, xo_psum = sig("aT_ready", 1), sig("xo_psum", 1)

        ORDER = [(half, q * 4 + m) for half in range(KT) for m in range(4) for q in range(4)]

        MID = 5
        QUARTER = HEADS // 4

        HEAD_POINTS = {7 * k - 1: MID + k for k in range(1, 5)}
        R_LEAD = 4

        def passes(eng, ahead, chain):
            ahead()
            with eng.Fori(0, BATCH - 1) as i:
                chain(i, True)
            chain(BATCH - 1, False)

        def wide(t):
            return t[:, :, :].rearrange("p a b -> p (a b)")

        consts_list = [(delta, d["delta"]), (strict, d["strict"]), (diag, d["diag"]), (headmask, d["headmask"]),
                       (blk16, d["blk16"]), (logw, d["time_decay"].partition_broadcast(P)),
                       (faaaa, d["faaaa"].partition_broadcast(P)), (gamma, d["gamma"].partition_broadcast(P)),
                       (beta, d["beta"].partition_broadcast(P))] + [(cols[n], d[n]) for n in cols]
        weights_list = [(w[n], d[n]) for n in ["WkT", "WrT", "WvT", "WgT", "WoT", "XWqT", "XWgT", "XWoT"]]

        with nc.Block() as block:
            @block.sync
            def _(sp):
                for t, src in consts_list:
                    sp.dma_start(t[:], src).then_inc(const_in.sem, 16)
                sp.dma_start(x_all[:], d["x"].rearrange("b (j p) c -> p (b j) c", p=P)).then_inc(x_loaded.sem, 16)
                sp.dma_start(ident[:], d["ident"]).then_inc(x_loaded.sem, 16)
                with sp.Fori(0, BATCH - 1) as i:
                    sp.wait_ge(*ctx_psum(i, CTILES))
                    sp.dma_start(ctxT[:], d["ctxT"][i + 1].rearrange("(k p) s -> p k s", p=P)).then_inc(ctx_in.sem, 16)

            @block.gpsimd
            def _(pool):
                pool.memset(v_pad[:], 0.0).then_inc(zeroed.sem, 1)
                pool.memset(lnT[:, :, 0:1], 0.0).then_inc(zeroed.sem, 1)
                pool.memset(half_neg[:], -0.5).then_inc(zeroed.sem, 1)
                pool.memset(eps[:], LN_EPS).then_inc(zeroed.sem, 1)
                pool.memset(v_ones[:, :, :, P:P + 1], 1.0).then_inc(zeroed.sem, 1)
                pool.wait_ge(zeroed.sem, 5)
                with pool.Fori(0, BATCH) as i:
                    n = [0]

                    def step(ins):
                        n[0] += 1
                        ins.then_inc(gstep.sem, 1)
                        pool.wait_ge(*gstep(i, n[0]))

                    def rsqrt_var(k):
                        pool.wait_ge(*stats_ready(i, k))
                        step(pool.tensor_tensor(var_eps[:], mean_var[:, :, 1], eps[:, 0:TOK], ALU.add))
                        pool.tensor_tensor(rstd[:], var_eps[:], half_neg[:, 0:TOK], ALU.pow).then_inc(rstd_ready.sem, 1)

                    rsqrt_var(1)
                    rsqrt_var(2)
                    assert n[0] == GSTEPS

            @block.scalar
            def _(act):
                act.dma_start(w["XWkvT"][:], d["XWkvT"].rearrange("(k p) n -> p k n", p=P)).then_inc(kv_weights_in.sem, 16)
                act.dma_start(ctxT[:], d["ctxT"][0].rearrange("(k p) s -> p k s", p=P)).then_inc(ctx_in.sem, 16)
                for t, src in weights_list:
                    act.dma_start(t[:], src.rearrange("(k p) n -> p k n", p=P)).then_inc(weights_in.sem, 16)
                act.wait_ge(const_in.sem, 16 * len(consts_list))
                act.activation(logw[:], logw[:], ACT.Exp).then_inc(logw_exp.sem, 1)
                act.wait_ge(logw_ready.sem, 2)
                act.wait_ge(zeroed.sem, 5)

                def point(i, p):
                    if p >= CTILES:
                        return
                    m = rows(p)
                    act.wait_ge(*k_min_ready(i, p + 1))
                    if p >= 2:
                        act.wait_ge(*kv_added(i, p - 1))
                    act.copy(v_ones[0:m, p % 2, :, 0:P],
                             bank[5 + p % 2][0:m, DIM:].rearrange("p (a b) -> p a b", a=KT)).then_inc(v_ready.sem, 1)
                    act.activation(k_exp[0:m, p % 2, :], k_min[0:m, p % 2, :], ACT.Exp).then_inc(k_exp_ready.sem, 1)

                def copy_tri(e):
                    act.wait_ge(decay_ready.sem, e + 1)
                    act.copy(decay[:, e * QUARTER:(e + 1) * QUARTER, SEQ:], decay[:, e * QUARTER:(e + 1) * QUARTER, 0:P]).then_inc(tri_copied.sem, 1)

                def ahead():
                    for e in range(4):
                        for h in range(e * QUARTER, (e + 1) * QUARTER):
                            last = act.activation(decay[:, h, 0:SEQ], delta[:, 0:SEQ], ACT.Exp, scale=logw[:, h:h + 1])
                        last.then_inc(decay_exp.sem, 1)
                        if e >= 1:
                            point(0, e - 1)
                            copy_tri(e - 1)
                    point(0, 3)
                    copy_tri(3)
                    point(0, 4)

                def chain(i, more):
                    def at(*points):
                        for p in points:
                            if p >= MID:
                                point(i, p)
                            elif more:
                                point(i + 1, p)

                    act.wait_ge(*lnT_psum(i, 1))
                    act.copy(lnT[:, :, 1:], bank[0][:].rearrange("p (a b) -> p a b", a=KT)).then_inc(lnT_ready.sem, 1)
                    act.wait_ge(*proj_psum(i, 1))
                    act.copy(wide(k_sb), bank[1][:]).then_inc(proj_read.sem, 1)
                    act.wait_ge(*proj_psum(i, 2))
                    act.copy(wide(r_sb), bank[2][:]).then_inc(proj_read.sem, 1)
                    act.wait_ge(*proj_psum(i, 3))
                    for j in range(TOK):
                        last = act.copy(v_pad[:, j].rearrange("p q (m e) -> p q m e", m=4)[:, :, :, 0:HD],
                                        bank[7][:, j * DIM:(j + 1) * DIM].rearrange("p (q m e) -> p q m e", q=8, m=4))
                    last.then_inc(proj_read.sem, 1)
                    act.wait_ge(*proj_psum(i, 4))
                    act.activation(wide(g_tanh), bank[0][:], ACT.Tanh, scale=0.5).then_inc(proj_read.sem, 1)
                    act.wait_ge(*proj_read(i, 4))
                    at(MID)
                    for n_, (half, h) in enumerate(ORDER):
                        if n_ >= ATTS:
                            act.wait_ge(*score_psum(i, n_ - ATTS + 1))
                        act.activation(r_head[:, n_ % ATTS, :], r_sb[:, half, :], ACT.Copy,
                                       scale=headmask[:, h:h + 1]).then_inc(r_head_ready.sem, 1)
                        if n_ - R_LEAD in HEAD_POINTS:
                            at(HEAD_POINTS[n_ - R_LEAD])
                    act.wait_ge(*group_added(i, 8))
                    act.copy(wide(y_sb), bank[0][:]).then_inc(y_ready.sem, 1)
                    at(10, 11)
                    act.wait_ge(*zT_psum(i, 1))
                    act.copy(wide(zT), bank[2][:]).then_inc(zT_ready.sem, 1)
                    at(12)
                    act.wait_ge(*lnT_psum(i, 2))
                    act.copy(wide(ln2T), bank[0][:]).then_inc(lnT_ready.sem, 1)
                    at(0)
                    act.wait_ge(*q_min_ready(i, 1))
                    act.activation(wide(q_exp), wide(q_min), ACT.Exp).then_inc(q_exp_ready.sem, 1)
                    act.wait_ge(*gate_psum(i, 1))
                    for k in range(KT):
                        last = act.activation(gate[:, k, :], bank[2][:, k * SEQ:(k + 1) * SEQ], ACT.Tanh,
                                              bias=hbg[:, k:k + 1], scale=0.5)
                    last.then_inc(gate_tanh.sem, 1)
                    at(1, 2, 3, 4)

                passes(act, ahead, chain)

            @block.vector
            def _(dve):
                dve.wait_ge(logw_exp.sem, 1)
                dve.tensor_scalar(logw[:], logw[:], -1.0, None, ALU.mult).then_inc(logw_ready.sem, 1)
                dve.tensor_scalar(hbg[:], cols["xbg"][:], 0.5, None, ALU.mult).then_inc(logw_ready.sem, 1)
                dve.wait_ge(zeroed.sem, 5)
                dve.wait_ge(x_loaded.sem, 16 * 2)
                dve.sem_inc(batch_done.sem, 1)

                def point(i, p):
                    if p < CTILES:
                        m, s = rows(p), p % 2
                        dve.wait_ge(*ctx_psum(i, p + 1))
                        dve.tensor_scalar(k_min[0:m, s, :], bank[5 + s][0:m, 0:DIM], 0.0, None,
                                          ALU.min).then_inc(k_min_ready.sem, 1)
                    if 1 <= p <= CTILES:
                        m, s = rows(p - 1), (p - 1) % 2
                        dve.wait_ge(*k_exp_ready(i, p))
                        if p >= 3:
                            dve.wait_ge(*kv_added(i, p - 2))
                        dve.scalar_tensor_tensor(k_feat[0:m, s, :], bank[5 + s][0:m, 0:DIM], 0.0, k_exp[0:m, s, :],
                                                 ALU.max, ALU.add).then_inc(k_feat_ready.sem, 1)

                def decay_part(e):
                    dve.wait_ge(decay_exp.sem, e + 1)
                    h0, h1 = e * QUARTER, (e + 1) * QUARTER
                    dve.tensor_tensor(decay[:, h0:h1, 0:P], decay[:, h0:h1, 0:P],
                                      strict[:, 0:P].unsqueeze(1).to_broadcast([P, QUARTER, P]), ALU.mult).then_inc(tri_masked.sem, 1)
                    dve.wait_ge(tri_masked.sem, e + 1)
                    for h in range(h0, h1):
                        last = dve.scalar_tensor_tensor(decay[:, h, 0:P], diag[:, 0:P], faaaa[:, h:h + 1], decay[:, h, 0:P],
                                                        ALU.mult, ALU.add)
                    last.then_inc(decay_ready.sem, 1)

                def ahead():
                    for e in range(4):
                        decay_part(e)
                        point(0, e)
                    point(0, 4)
                    dve.wait_ge(tri_copied.sem, 4)

                def first_norm(i):
                    for j in range(TOK):
                        last = dve.bn_stats(stats[:, j, :], x_all[:, TOK * i + j, :])
                    last.then_inc(first_stats.sem, 1)
                    dve.wait_ge(*first_stats(i, 1))
                    dve.memset(wait_pad[:], 0.0)
                    for j in range(TOK):
                        last = dve.bn_aggr(mean_var[:, j, :], stats[:, j, :])
                    last.then_inc(stats_ready.sem, 1)
                    dve.wait_ge(*rstd_ready(i, 1))
                    for j in range(TOK):
                        last = dve.tensor_scalar(lnx[:, j, :], x_all[:, TOK * i + j, :], mean_var[:, j, 0:1], rstd[:, j:j + 1],
                                                 ALU.subtract, ALU.mult)
                    last.then_inc(ln_ready.sem, 1)

                def chain(i, more):
                    def at(*points):
                        for p in points:
                            if p >= MID:
                                point(i, p)
                            elif more:
                                point(i + 1, p)

                    n = [0]

                    def step(ins):
                        n[0] += 1
                        ins.then_inc(vstep.sem, 1)
                        dve.wait_ge(*vstep(i, n[0]))

                    def layer_norm(src, k):
                        for j in range(TOK):
                            last = dve.bn_stats(stats[:, j, :], src(j))
                        step(last)
                        dve.memset(wait_pad[:], 0.0)
                        for j in range(TOK):
                            last = dve.bn_aggr(mean_var[:, j, :], stats[:, j, :])
                        last.then_inc(stats_ready.sem, 1)
                        dve.wait_ge(*rstd_ready(i, k))
                        for j in range(TOK):
                            last = dve.tensor_scalar(lnx[:, j, :], src(j), mean_var[:, j, 0:1], rstd[:, j:j + 1],
                                                     ALU.subtract, ALU.mult)
                        last.then_inc(ln_ready.sem, 1)

                    def keep_sums():
                        dve.wait_ge(*kv_added(i, CTILES))
                        for h in range(KT):
                            dve.tensor_tensor(kv_m[:, h, :], bank[3 + h][:, 0:P], blk16[:], ALU.mult)
                            last = dve.tensor_copy(ks_col[:, h:h + 1], bank[3 + h][:, P:P + 1])
                        step(last)
                        for h in range(KT):
                            last = dve.tensor_scalar(ks_m[:, h, :], blk16[:], ks_col[:, h:h + 1], None, ALU.mult)
                        last.then_inc(kv_ready.sem, 1)

                    dve.wait_ge(*lnT_ready(i, 1))
                    step(dve.tensor_tensor(diff[:], lnT[:, :, 0:SEQ], lnT[:, :, 1:], ALU.subtract))
                    for name in "krvg":
                        for k in range(KT):
                            last = dve.scalar_tensor_tensor(mix[name][:, k, :], diff[:, k, :], cols["maa_" + name][:, k:k + 1],
                                                            lnT[:, k, 1:], ALU.mult, ALU.add)
                        last.then_inc(mix_ready.sem, 1)
                    at(MID)
                    dve.wait_ge(*proj_read(i, 4))
                    dve.scalar_tensor_tensor(wide(g_silu), wide(g_tanh), 1.0, bank[0][:], ALU.add,
                                             ALU.mult).then_inc(g_ready.sem, 1)
                    for n_, (half, h) in enumerate(ORDER):
                        dve.wait_ge(*score_psum(i, n_ + 1))
                        if n_ >= ATTS:
                            dve.wait_ge(*group_added(i, (n_ - ATTS) // 4 + 1))
                        dve.tensor_tensor(att[:, n_ % ATTS, :], bank[(1, 2, 7)[n_ % RING]][:, 0:SC], decay[:, half * 16 + h, :],
                                          ALU.mult).then_inc(att_ready.sem, 1)
                        if n_ in HEAD_POINTS:
                            at(HEAD_POINTS[n_])
                    dve.wait_ge(*yt_psum(i, 1))
                    y4 = bank[1][:].rearrange("p (g e) -> p g e", e=HD)

                    def over(t):
                        return t[:].unsqueeze(2).to_broadcast([P, TOK * HEADS, HD])

                    step(dve.tensor_reduce(g_mean[:], y4, AX.X, ALU.add))
                    step(dve.tensor_scalar(g_mean[:], g_mean[:], 1.0 / HD, None, ALU.mult))
                    at(10)
                    step(dve.tensor_tensor(y_c[:], y4, over(g_mean), ALU.subtract))
                    step(dve.tensor_tensor(y_sq[:], y_c[:], y_c[:], ALU.mult))
                    step(dve.tensor_reduce(g_var[:], y_sq[:], AX.X, ALU.add))
                    at(11)
                    step(dve.tensor_scalar(g_var[:], g_var[:], GROUP_EPS * HD, None, ALU.add))
                    step(dve.tensor_scalar(g_bits[:], g_var[:].bitcast(I32), 1, None, ALU.logical_shift_right))
                    step(dve.tensor_scalar(g_rstd[:].bitcast(I32), g_bits[:], -1.0, float(0x5F3759DF), ALU.mult, ALU.add))
                    for _ in range(NEWTON):
                        step(dve.tensor_tensor(g_square[:], g_rstd[:], g_rstd[:], ALU.mult))
                        step(dve.scalar_tensor_tensor(g_square[:], g_square[:], -0.5, g_var[:], ALU.mult, ALU.mult))
                        step(dve.scalar_tensor_tensor(g_rstd[:], g_square[:], 1.5, g_rstd[:], ALU.add, ALU.mult))
                    step(dve.tensor_tensor(y_c[:], y_c[:], over(g_rstd), ALU.mult))
                    y2 = y_c[:].rearrange("p (j h) e -> p j (h e)", j=TOK)
                    step(dve.scalar_tensor_tensor(y2, y2, HD ** 0.5, gamma[:].unsqueeze(1).to_broadcast([P, TOK, DIM]),
                                                  ALU.mult, ALU.mult))
                    step(dve.tensor_tensor(y2, y2, beta[:].unsqueeze(1).to_broadcast([P, TOK, DIM]), ALU.add))
                    dve.wait_ge(*g_ready(i, 1))
                    dve.scalar_tensor_tensor(y2, y2, 0.5, g_silu[:], ALU.mult, ALU.mult).then_inc(z_ready.sem, 1)
                    at(12, 13)
                    dve.wait_ge(*o_psum(i, 1))
                    for j in range(TOK):
                        last = dve.tensor_tensor(x1[:, j, :], x_all[:, TOK * i + j, :], bank[7][:, j * DIM:(j + 1) * DIM], ALU.add)
                    step(last)

                    layer_norm(lambda j: x1[:, j, :], 2)
                    keep_sums()
                    at(0)
                    dve.wait_ge(*q_psum(i, 1))
                    dve.tensor_scalar(wide(q_min), bank[1][:], 0.0, None, ALU.min).then_inc(q_min_ready.sem, 1)
                    dve.wait_ge(*q_exp_ready(i, 1))
                    dve.scalar_tensor_tensor(wide(q_feat), bank[1][:], 0.0, wide(q_exp), ALU.max,
                                             ALU.add).then_inc(q_feat_ready.sem, 1)
                    at(1)
                    dve.wait_ge(*den_psum(i, 1))
                    step(dve.tensor_scalar(wide(den), bank[0][:], ZEPS, None, ALU.add))
                    step(dve.reciprocal(wide(den), wide(den)))
                    dve.wait_ge(*num_psum(i, 1))
                    step(dve.tensor_tensor(wide(den), wide(den), bank[7][:], ALU.mult))
                    dve.wait_ge(*gate_tanh(i, 1))
                    step(dve.tensor_scalar(wide(gate), wide(gate), 0.5, 0.5, ALU.mult, ALU.add))
                    dve.tensor_tensor(wide(aT), wide(den), wide(gate), ALU.mult).then_inc(aT_ready.sem, 1)
                    if more:
                        dve.wait_ge(*lnT_psum(i, 2))
                        first_norm(i + 1)
                    at(2, 3)
                    dve.wait_ge(*xo_psum(i, 1))
                    for j in range(TOK):
                        last = dve.tensor_tensor(x_all[:, TOK * i + j, :], x1[:, j, :], bank[0][:, j * DIM:(j + 1) * DIM], ALU.add)
                    last.then_inc(batch_done.sem, 1)
                    at(4)
                    assert n[0] == VSTEPS

                def before_all():
                    ahead()
                    first_norm(0)

                passes(dve, before_all, chain)

            @block.tensor
            def _(pe):
                def transposed(dst, src):
                    for a in range(KT):
                        for b in range(TOK):
                            last = pe.transpose(dst[:, a * SEQ + b * P:a * SEQ + (b + 1) * P], src[:, b, a * P:(a + 1) * P], ident[:])
                    return last

                def channels_out(dst, weight, act_t):
                    for a in range(KT):
                        for k in range(KT):
                            last = pe.matmul(dst[:, a * SEQ:(a + 1) * SEQ], weight[:, k, a * P:(a + 1) * P], act_t[:, k, :],
                                             start=(k == 0), stop=(k == KT - 1))
                    return last

                def tokens_out(dst, weight, act_t):
                    for j in range(TOK):
                        for k in range(KT):
                            last = pe.matmul(dst[:, j * DIM:(j + 1) * DIM], act_t[:, k, j * P:(j + 1) * P], weight[:, k, :],
                                             start=(k == 0), stop=(k == KT - 1))
                    return last

                pe.wait_ge(kv_weights_in.sem, 16)
                def point(i, p):
                    if p >= 2:
                        t = p - 2
                        m, s = rows(t), t % 2
                        pe.wait_ge(*k_feat_ready(i, t + 1))
                        pe.wait_ge(*v_ready(i, t + 1))
                        for h in range(KT):
                            last = pe.matmul(bank[3 + h][:, 0:P + 1], k_feat[0:m, s, h * P:(h + 1) * P], v_ones[0:m, s, h, :],
                                             start=(t == 0), stop=(t == CTILES - 1))
                        last.then_inc(kv_added.sem, 1)
                    if p < CTILES:
                        m = rows(p)
                        for k in range(KT):
                            last = pe.matmul(bank[5 + p % 2][0:m, :], ctxT[:, k, p * P:p * P + m], w["XWkvT"][:, k, :],
                                             start=(k == 0), stop=(k == KT - 1))
                        last.then_inc(ctx_psum.sem, 1)

                def ahead():
                    pe.wait_ge(*ctx_in(0, 16))
                    for p in range(MID):
                        point(0, p)
                    pe.wait_ge(x_loaded.sem, 16 * 2)
                    pe.wait_ge(weights_in.sem, 16 * len(weights_list))

                def chain(i, more):
                    def at(*points):
                        for p in points:
                            if p >= MID:
                                point(i, p)
                            elif more:
                                if p == 0:
                                    pe.wait_ge(*ctx_in(i + 1, 16))
                                    pe.wait_ge(*kv_ready(i, 1))
                                point(i + 1, p)

                    pe.wait_ge(*batch_done(i, 1))
                    pe.wait_ge(*ln_ready(i, 1))
                    transposed(bank[0], lnx).then_inc(lnT_psum.sem, 1)
                    for n_, (name, dst) in enumerate((("k", 1), ("r", 2))):
                        pe.wait_ge(*mix_ready(i, n_ + 1))
                        channels_out(bank[dst], w[f"W{name}T"], mix[name]).then_inc(proj_psum.sem, 1)
                    for n_, (name, dst) in enumerate((("v", 7), ("g", 0))):
                        pe.wait_ge(*mix_ready(i, n_ + 3))
                        tokens_out(bank[dst], w[f"W{name}T"], mix[name]).then_inc(proj_psum.sem, 1)

                    def add_group(n_):
                        pe.wait_ge(*att_ready(i, n_ + 4))
                        half, m = ORDER[n_][0], ORDER[n_][1] % 4
                        for j in range(TOK):
                            for q in range(4):
                                a = att[:, (n_ + q) % ATTS, j * SEQ:j * SEQ + SEQ - j * P]
                                last = pe.matmul(bank[0][32 * q:32 * q + 32, half * SEQ + j * P:(half + 1) * SEQ],
                                                 v_pad[:, j, half * 4 + q, 32 * m:32 * m + 32], a,
                                                 start=(m == 0 and j == 0), stop=(m == 3 and j == TOK - 1))
                        last.then_inc(group_added.sem, 1)

                    at(MID)
                    pe.wait_ge(*proj_read(i, 3))
                    for n_, (half, h) in enumerate(ORDER):
                        pe.wait_ge(*r_head_ready(i, n_ + 1))
                        if n_ >= RING:
                            pe.wait_ge(*att_ready(i, n_ - RING + 1))
                        b, r = bank[(1, 2, 7)[n_ % RING]], r_head[:, n_ % ATTS, :]
                        pe.matmul(b[:, 0:SEQ], k_sb[:, half, 0:P], r, start=True, stop=True)
                        pe.matmul(b[:, SEQ:SC], k_sb[:, half, P:SEQ], r[:, P:SEQ], start=True,
                                  stop=True).then_inc(score_psum.sem, 1)
                        if n_ >= 5 and (n_ - 5) % 4 == 0:
                            add_group(n_ - 5)
                        if n_ in HEAD_POINTS:
                            at(HEAD_POINTS[n_])
                    add_group(28)
                    pe.wait_ge(*y_ready(i, 1))
                    for j in range(TOK):
                        for a in range(KT):
                            last = pe.transpose(bank[1][:, j * DIM + a * P:j * DIM + (a + 1) * P], y_sb[:, a, j * P:(j + 1) * P], ident[:])
                    last.then_inc(yt_psum.sem, 1)
                    at(10, 11, 12)
                    pe.wait_ge(*z_ready(i, 1))
                    transposed(bank[2], y_c[:].rearrange("p (j h) e -> p j (h e)", j=TOK)).then_inc(zT_psum.sem, 1)
                    at(13)
                    pe.wait_ge(*zT_ready(i, 1))
                    tokens_out(bank[7], w["WoT"], zT).then_inc(o_psum.sem, 1)
                    at(14)

                    pe.wait_ge(*ln_ready(i, 2))
                    transposed(bank[0], lnx).then_inc(lnT_psum.sem, 1)
                    at(0)
                    pe.wait_ge(*lnT_ready(i, 2))
                    channels_out(bank[1], w["XWqT"], ln2T).then_inc(q_psum.sem, 1)
                    channels_out(bank[2], w["XWgT"], ln2T).then_inc(gate_psum.sem, 1)
                    at(1)
                    pe.wait_ge(*q_feat_ready(i, 1))
                    for h in range(KT):
                        last = pe.matmul(bank[0][:, h * SEQ:(h + 1) * SEQ], ks_m[:, h, :], q_feat[:, h, :], start=True, stop=True)
                    last.then_inc(den_psum.sem, 1)
                    for h in range(KT):
                        last = pe.matmul(bank[7][:, h * SEQ:(h + 1) * SEQ], kv_m[:, h, :], q_feat[:, h, :], start=True, stop=True)
                    last.then_inc(num_psum.sem, 1)
                    at(2, 3)
                    pe.wait_ge(*aT_ready(i, 1))
                    tokens_out(bank[0], w["XWoT"], aT).then_inc(xo_psum.sem, 1)
                    at(4)

                passes(pe, ahead, chain)




def experts(nc, d, x_all, ident, lut_w, w_in, c_weights_in):
    EXPERTS, INNER, TOP_P = 8, 512, 0.9
    N = BATCH * TOK
    IT = INNER // P
    PAIR = 2
    HALF = N * P // 2
    UNITS = PAIR * 2 * IT
    with ExitStack() as ctx:
        def sb(name, shape, dt=F32):
            return ctx.enter_context(nc.sbuf_tensor(name, shape, dt))

        def sig(name, per=0):
            return Signal(ctx.enter_context(nc.semaphore(name)), per)

        bank = [ctx.enter_context(nc.psum_tensor(f"b_bank{n}", [P, 512], F32)) for n in range(8)]
        SIZE = KT * INNER
        w_hi, w_lo = sb("w_hi", [P, PAIR, 3, SIZE], F32R), sb("w_lo", [P, PAIR, 3, SIZE], F32R)
        router = sb("router", [P, KT, EXPERTS])
        earlier = sb("earlier", [P, EXPERTS, EXPERTS])
        stats, mean_var = sb("b_stats", [P, N, 6]), sb("b_mean_var", [P, N, 2])
        eps, half_neg, var_eps, rstd = (sb("b_" + n, [P, N]) for n in ("eps", "half_neg", "var_eps", "rstd"))
        lnx, lnT = sb("b_lnx", [P, N, DIM]), sb("b_lnT", [P, KT, N * P])
        lnT_hi, lnT_lo = sb("lnT_hi", [P, KT, N * P], F32R), sb("lnT_lo", [P, KT, N * P], F32R)
        top, total = sb("r_top", [P, N]), sb("r_total", [P, N])
        prob, before = sb("prob", [P, N, EXPERTS]), sb("before", [P, N, EXPERTS])
        above, above_eq = sb("above", [P, N, EXPERTS, EXPERTS]), sb("above_eq", [P, N, EXPERTS, EXPERTS])
        weight = sb("weight", [P, EXPERTS, N])
        weight_e = sb("weight_e", [P, PAIR, N])
        g_tanh, g_silu = sb("b_g_tanh", [P, 2, HALF]), sb("b_g_silu", [P, 2, HALF])
        h_full = sb("h_full", [P, 2, HALF])
        h_hi, h_lo = sb("h_hi", [P, 2, IT, HALF], F32R), sb("h_lo", [P, 2, IT, HALF], F32R)
        LUT, LUT_COLS = 16, 3 * 6 * DIM
        PER_PASS, SLICES = LUT // (EXPERTS // PAIR), 4
        lut_idx, lut_hit = sb("lut_idx", [P, LUT_COLS], I32), sb("lut_hit", [P, LUT_COLS // SLICES])
        lut_val, lut_key = sb("lut_val", [P, LUT]), sb("lut_key", [P, LUT])
        val_now, key_now = sb("val_now", [P, PER_PASS]), sb("key_now", [P, PER_PASS])
        lut_flat = lut_w["all"]

        const_in, set_ = sig("b_const_in"), sig("b_set")
        stats_ready, rstd_ready, ln_ready, lnT_psum, lnT_ready = (sig("b_" + n) for n in (
            "stats_ready", "rstd_ready", "ln_ready", "lnT_psum", "lnT_ready"))
        logit_psum, shifted, prob_exp = (sig(n) for n in ("logit_psum", "shifted", "prob_exp"))
        pool_step, prologue_step = sig("b_pool_step"), sig("b_prologue_step")
        weights_in, w_hi_ready, w_lo_ready = ([sig(f"b_{n}{e}", k) for e in range(PAIR)] for n, k in (
            ("weights_in", 48), ("w_hi_ready", 3), ("w_lo_ready", 3)))
        lnT_hi_ready, lnT_lo_ready = sig("lnT_hi_ready"), sig("lnT_lo_ready")
        gate_psum, gate_tanh, gate_silu, h_full_ready, h_hi_ready, h_lo_ready = (sig("b_" + n, UNITS) for n in (
            "gate_psum", "gate_tanh", "gate_silu", "h_full_ready", "h_hi_ready", "h_lo_ready"))
        weight_ready = sig("weight_ready", 1)
        lut_hit_pool = sb("lut_hit_pool", [P, LUT_COLS // SLICES])
        pool_hit_ready, pool_lut_added = sig("pool_hit_ready", UNITS // 2), sig("pool_lut_added", UNITS // 2)
        lut_now, lut_hit_ready, lut_added = sig("lut_now", 1), sig("lut_hit_ready", UNITS // 2), sig("lut_added", UNITS // 2)
        y_psum, y_added = sig("y_psum", UNITS // 2), sig("y_added", UNITS // 2)
        HALVES = UNITS // IT
        PASSES = EXPERTS // PAIR
        SPLIT_AT = {2 + 2 * n: (1, n) for n in range(3)}
        SPLIT_AT.update({10 + 2 * n: (0, n) for n in range(3)})

        def passes(eng, body):
            body(0, True, True)
            with eng.Fori(1, PASSES - 1) as i:
                body(i, False, True)
            body(PASSES - 1, False, False)

        def split_of(i, u, more):
            if u not in SPLIT_AT or (SPLIT_AT[u][0] == 0 and not more):
                return None
            place, n = SPLIT_AT[u]
            return (i if place else i + 1), place, n

        def three(pe, dst, hi, lo, moving_hi, moving_lo, first, last):
            pe.matmul(dst, hi, moving_hi, start=first, stop=False)
            pe.matmul(dst, hi, moving_lo, start=False, stop=False)
            return pe.matmul(dst, lo, moving_hi, start=False, stop=last)

        with nc.Block() as block:
            @block.sync
            def _(sp):
                def load(i, e):
                    for n, (name, tiles) in enumerate((("gateT", KT), ("upT", KT), ("downT", IT))):
                        sp.dma_start(w_in[:, e, n].rearrange("p (k n) -> p k n", k=tiles),
                                     d[name][i * PAIR + e].rearrange("(k p) n -> p k n", p=P)).then_inc(weights_in[e].sem, 16)

                for e in range(PAIR):
                    load(0, e)
                sp.dma_start(router[:], d["routerT"].rearrange("(k p) e -> p k e", p=P)).then_inc(const_in.sem, 16)
                sp.dma_start(earlier[:], d["earlier"].partition_broadcast(P)).then_inc(const_in.sem, 16)
                sp.dma_start(lut_val[:], d["lut"].partition_broadcast(P)).then_inc(const_in.sem, 16)
                sp.dma_start(lut_key[:], d["lut_key"].partition_broadcast(P)).then_inc(const_in.sem, 16)
                for n, name in enumerate(("gate_idx", "up_idx")):
                    sp.dma_start(lut_idx[:, n * 6 * DIM:(n + 1) * 6 * DIM].rearrange("p (k n) -> p k n", k=KT),
                                 d[name].rearrange("(k p) n -> p k n", p=P)).then_inc(const_in.sem, 16)
                sp.dma_start(lut_idx[:, 12 * DIM:].rearrange("p (c n) -> p c n", c=6),
                             d["down_idx"].rearrange("(c p) n -> p c n", p=P)).then_inc(const_in.sem, 16)

                with sp.Fori(0, PASSES - 1) as i:
                    for e in range(PAIR):
                        sp.wait_ge(*w_lo_ready[e](i, 3))
                        load(i + 1, e)
                for e, weights in enumerate(last_block_weights(w_in)):
                    sp.wait_ge(*w_lo_ready[e](PASSES - 1, 3))
                    for name, t in weights.items():
                        src = d[name].rearrange("g d e -> d g e" if name in ("w0T", "w1T", "w2T") else "(k p) n -> p k n",
                                                **({} if name in ("w0T", "w1T", "w2T") else {"p": P}))
                        sp.dma_start(t, src).then_inc(c_weights_in.sem, 16)

            @block.gpsimd
            def _(pool):
                pool.memset(eps[:], LN_EPS).then_inc(set_.sem, 1)
                pool.memset(half_neg[:], -0.5).then_inc(set_.sem, 1)
                pool.wait_ge(set_.sem, 2)
                pool.wait_ge(stats_ready.sem, 1)
                pool.tensor_tensor(var_eps[:], mean_var[:, :, 1], eps[:], ALU.add).then_inc(pool_step.sem, 1)
                pool.wait_ge(pool_step.sem, 1)
                pool.tensor_tensor(rstd[:], var_eps[:], half_neg[:], ALU.pow).then_inc(rstd_ready.sem, 1)

                def split(i, e, n):
                    pool.wait_ge(*w_hi_ready[e](i, n + 1))
                    pool.tensor_tensor(w_lo[:, e, n], w_in[:, e, n], w_hi[:, e, n].bitcast(F32), ALU.subtract).then_inc(w_lo_ready[e].sem, 1)

                def body(i, first, more):
                    for u in range(UNITS):
                        s = split_of(i, u, more)
                        if s:
                            split(*s)
                        h, c = u // IT, u % IT
                        pool.wait_ge(*h_hi_ready(i, u + 1))
                        pool.tensor_tensor(h_lo[:, h % 2, c], h_full[:, u % 2], h_hi[:, h % 2, c].bitcast(F32),
                                           ALU.subtract).then_inc(h_lo_ready.sem, 1)
                        if u % 2:
                            part = slice(u % SLICES * (LUT_COLS // SLICES), (u % SLICES + 1) * (LUT_COLS // SLICES))
                            pool.wait_ge(*pool_hit_ready(i, u // 2 + 1))
                            pool.tensor_tensor(lut_flat[:, part], lut_flat[:, part], lut_hit_pool[:], ALU.add).then_inc(pool_lut_added.sem, 1)

                for n in range(3):
                    split(0, 0, n)
                passes(pool, body)

            @block.scalar
            def _(act):
                for n in range(4):
                    k, h = n // 2, n % 2
                    act.wait_ge(lnT_psum.sem, n + 1)
                    act.copy(lnT[:, k, h * HALF:(h + 1) * HALF], bank[n][:]).then_inc(lnT_ready.sem, 1)
                    act.wait_ge(lnT_ready.sem, n + 1)
                    act.copy(lnT_hi[:, k, h * HALF:(h + 1) * HALF], lnT[:, k, h * HALF:(h + 1) * HALF]).then_inc(lnT_hi_ready.sem, 1)

                def split(i, e, n):
                    act.wait_ge(*weights_in[e](i, 48))
                    act.copy(w_hi[:, e, n], w_in[:, e, n]).then_inc(w_hi_ready[e].sem, 1)

                for n in range(3):
                    split(0, 0, n)
                act.wait_ge(shifted.sem, 1)
                act.activation(prob[:], prob[:], ACT.Exp).then_inc(prob_exp.sem, 1)

                def body(i, first, more):
                    for u in range(UNITS):
                        h, c = u // IT, u % IT
                        act.wait_ge(*gate_psum(i, u + 1))
                        if u >= 2 or not first:
                            act.wait_ge(*gate_silu(i, u - 1))
                        act.activation(g_tanh[:, u % 2], bank[u % 2][:], ACT.Tanh, scale=0.5).then_inc(gate_tanh.sem, 1)
                        s = split_of(i, u, more)
                        if s:
                            split(*s)
                        act.wait_ge(*h_full_ready(i, u + 1))
                        act.copy(h_hi[:, h % 2, c], h_full[:, u % 2]).then_inc(h_hi_ready.sem, 1)

                passes(act, body)

            @block.vector
            def _(dve):
                n_ = [0]

                def step(ins):
                    n_[0] += 1
                    ins.then_inc(prologue_step.sem, 1)
                    dve.wait_ge(prologue_step.sem, n_[0])

                for n in range(N):
                    last = dve.bn_stats(stats[:, n, :], x_all[:, n, :])
                step(last)
                for n in range(N):
                    last = dve.bn_aggr(mean_var[:, n, :], stats[:, n, :])
                last.then_inc(stats_ready.sem, 1)
                dve.wait_ge(rstd_ready.sem, 1)
                for n in range(N):
                    dve.tensor_scalar(lnx[:, n, :], x_all[:, n, :], mean_var[:, n, 0:1], rstd[:, n:n + 1],
                                      ALU.subtract, ALU.mult).then_inc(ln_ready.sem, 1)
                for n in range(4):
                    k, h = n // 2, n % 2
                    cols = slice(h * HALF, (h + 1) * HALF)
                    dve.wait_ge(lnT_hi_ready.sem, n + 1)
                    dve.tensor_tensor(lnT_lo[:, k, cols], lnT[:, k, cols], lnT_hi[:, k, cols].bitcast(F32),
                                      ALU.subtract).then_inc(lnT_lo_ready.sem, 1)
                dve.wait_ge(logit_psum.sem, 1)
                logits = bank[4][:, 0:N * EXPERTS].rearrange("p (n e) -> p n e", e=EXPERTS)
                step(dve.tensor_reduce(top[:], logits, AX.X, ALU.max))
                dve.tensor_tensor(prob[:], logits, top[:].unsqueeze(2).to_broadcast([P, N, EXPERTS]),
                                  ALU.subtract).then_inc(shifted.sem, 1)
                dve.wait_ge(prob_exp.sem, 1)
                step(dve.tensor_reduce(total[:], prob[:], AX.X, ALU.add))
                step(dve.reciprocal(total[:], total[:]))
                step(dve.tensor_tensor(prob[:], prob[:], total[:].unsqueeze(2).to_broadcast([P, N, EXPERTS]), ALU.mult))
                dve.wait_ge(const_in.sem, 112)
                for n in range(N):
                    pj = prob[:, n].unsqueeze(1).to_broadcast([P, EXPERTS, EXPERTS])
                    pe = prob[:, n].unsqueeze(2).to_broadcast([P, EXPERTS, EXPERTS])
                    dve.tensor_tensor(above[:, n], pj, pe, ALU.is_gt)
                    last = dve.tensor_tensor(above_eq[:, n], pj, pe, ALU.is_ge)
                step(last)
                for n in range(N):
                    last = dve.tensor_tensor(above_eq[:, n], above_eq[:, n], earlier[:], ALU.mult)
                step(last)
                step(dve.tensor_tensor(above[:].rearrange("p a b c -> p (a b c)"), above[:].rearrange("p a b c -> p (a b c)"),
                                       above_eq[:].rearrange("p a b c -> p (a b c)"), ALU.max))
                for n in range(N):
                    pj = prob[:, n].unsqueeze(1).to_broadcast([P, EXPERTS, EXPERTS])
                    last = dve.tensor_tensor(above[:, n], above[:, n], pj, ALU.mult)
                step(last)
                step(dve.tensor_reduce(before[:], above[:], AX.X, ALU.add))
                step(dve.memset(lut_flat[:], 0.0))
                step(dve.scalar_tensor_tensor(weight[:].rearrange("p e n -> p n e"), before[:], TOP_P, prob[:], ALU.is_le, ALU.mult))
                dve.wait_ge(prologue_step.sem, n_[0])

                def add_y(i, h):
                    for b in range(2):
                        dve.wait_ge(*y_psum(i, 2 * h + b + 1))
                        for t in range(2):
                            n = (h % 2) * 4 + b * 2 + t
                            last = dve.scalar_tensor_tensor(x_all[:, n, :], bank[4 + h % 2 * 2 + b][:, t * DIM:(t + 1) * DIM],
                                                            weight_e[:, h // 2, n:n + 1], x_all[:, n, :], ALU.mult, ALU.add)
                        last.then_inc(y_added.sem, 1)

                def body(i, first, more):
                    if not first:
                        dve.wait_ge(*pool_hit_ready(i, 0))
                    dve.tensor_copy(val_now[:], lut_val[:, bass.ds(i * PER_PASS, PER_PASS)])
                    dve.tensor_copy(key_now[:], lut_key[:, bass.ds(i * PER_PASS, PER_PASS)]).then_inc(lut_now.sem, 1)
                    dve.wait_ge(*lut_now(i, 1))
                    for u in range(UNITS):
                        h = u // IT
                        dve.wait_ge(*gate_tanh(i, u + 1))
                        dve.scalar_tensor_tensor(g_silu[:, u % 2], g_tanh[:, u % 2], 1.0, bank[u % 2][:], ALU.add,
                                                 ALU.mult).then_inc(gate_silu.sem, 1)
                        if u >= 2 or not first:
                            dve.wait_ge(*h_lo_ready(i, u - 1))
                        dve.wait_ge(*gate_silu(i, u + 1))
                        dve.scalar_tensor_tensor(h_full[:, u % 2], g_silu[:, u % 2], 0.5, bank[2 + u % 2][:],
                                                 ALU.mult, ALU.mult).then_inc(h_full_ready.sem, 1)
                        v, part = u // SLICES, slice(u % SLICES * (LUT_COLS // SLICES), (u % SLICES + 1) * (LUT_COLS // SLICES))
                        hit, ready = ((lut_hit, lut_hit_ready), (lut_hit_pool, pool_hit_ready))[u % 2]
                        if u % 2 and not (first and u == 1):
                            dve.wait_ge(*pool_lut_added(i, u // 2))
                        dve.tensor_scalar(hit[:], lut_idx[:, part], key_now[:, v:v + 1], val_now[:, v:v + 1],
                                          ALU.is_equal, ALU.mult).then_inc(ready.sem, 1)
                        if u % 2 == 0:
                            dve.wait_ge(*lut_hit_ready(i, u // 2 + 1))
                            dve.tensor_tensor(lut_flat[:, part], lut_flat[:, part], lut_hit[:], ALU.add).then_inc(lut_added.sem, 1)
                            dve.wait_ge(*lut_added(i, u // 2 + 1))
                        if u % IT == 1 and h >= 1:
                            add_y(i, h - 1)
                        elif u == 1:
                            if not first:
                                add_y(i - 1, HALVES - 1)
                                dve.wait_ge(*y_added(i, 0))
                            dve.tensor_copy(weight_e[:], weight[:, bass.ds(i * PAIR, PAIR), :]).then_inc(weight_ready.sem, 1)
                            dve.wait_ge(*weight_ready(i, 1))

                passes(dve, body)
                add_y(PASSES - 1, HALVES - 1)
                dve.wait_ge(*y_added(PASSES - 1, UNITS // 2))

            @block.tensor
            def _(pe):
                for n in range(4):
                    k, h = n // 2, n % 2
                    for t in range(4):
                        pe.wait_ge(ln_ready.sem, h * 4 + t + 1)
                        last = pe.transpose(bank[n][:, t * P:(t + 1) * P], lnx[:, h * 4 + t, k * P:(k + 1) * P], ident[:])
                    last.then_inc(lnT_psum.sem, 1)
                pe.wait_ge(lnT_ready.sem, 4)
                pe.wait_ge(const_in.sem, 112)
                for n in range(N):
                    for k in range(KT):
                        last = pe.matmul(bank[4][:, n * EXPERTS:(n + 1) * EXPERTS], lnT[:, k, n * P:(n + 1) * P], router[:, k, :],
                                         start=(k == 0), stop=(k == KT - 1))
                last.then_inc(logit_psum.sem, 1)
                pe.wait_ge(lnT_lo_ready.sem, 4)

                def down(i, h):
                    e, half = h // 2, h % 2
                    pe.wait_ge(*h_lo_ready(i, IT * (h + 1)))
                    pe.wait_ge(*w_lo_ready[e](i, 3))
                    for b in range(2):
                        if h >= 2 or not (isinstance(i, int) and i == 0):
                            pe.wait_ge(*y_added(i, 2 * (h - 2) + b + 1))
                        for t in range(2):
                            for c in range(IT):
                                tokens = slice((b * 2 + t) * P, (b * 2 + t + 1) * P)
                                cols = slice(c * DIM, (c + 1) * DIM)
                                last = three(pe, bank[4 + half * 2 + b][:, t * DIM:(t + 1) * DIM],
                                             h_hi[:, half, c, tokens], h_lo[:, half, c, tokens],
                                             w_hi[:, e, 2, cols], w_lo[:, e, 2, cols], c == 0, c == IT - 1)
                        last.then_inc(y_psum.sem, 1)

                def body(i, first, more):
                    for u in range(UNITS):
                        e, h, c = u // (2 * IT), (u // IT) % 2, u % IT
                        if c == 0 and h == 0:
                            pe.wait_ge(*w_lo_ready[e](i, 2))
                        if u >= 2 or not first:
                            pe.wait_ge(*h_full_ready(i, u - 1))
                        tokens = slice(h * HALF, (h + 1) * HALF)
                        for n, b in ((0, 0), (1, 2)):
                            for k in range(KT):
                                cols = slice(k * INNER + c * P, k * INNER + (c + 1) * P)
                                last = three(pe, bank[b + u % 2][:], w_hi[:, e, n, cols], w_lo[:, e, n, cols],
                                             lnT_hi[:, k, tokens], lnT_lo[:, k, tokens], k == 0, k == KT - 1)
                        last.then_inc(gate_psum.sem, 1)
                        if c == 1 and u >= IT:
                            down(i, u // IT - 1)
                        elif c == 1 and not first:
                            down(i - 1, HALVES - 1)

                passes(pe, body)
                down(PASSES - 1, HALVES - 1)


def fast_weights_softmax_and_lut(nc, d, out, x_all, ident, lut_w, landing, weights_in):
    HEADS, HD = 16, 16
    QK_SCALE = 1.0 / HD ** 0.5
    FW_EPS, L2_EPS = 1e-6, 1e-5
    GROUP = 4
    GROUPS = HEADS // GROUP
    PARTS = 3
    TERMS = 6
    STACK = TERMS * HD
    DEEP = STACK + PARTS
    CHUNK = 512
    CHUNKS = -(-CTX // CHUNK)
    K_SLOTS = 4
    IT = 6
    INNER = 688

    def width(c):
        return min(CHUNK, CTX - c * CHUNK)

    with ExitStack() as ctx:
        def sb(name, shape, dt=F32):
            return ctx.enter_context(nc.sbuf_tensor(name, shape, dt))

        def sig(name, per=0):
            return Signal(ctx.enter_context(nc.semaphore(name)), per)

        def stages(name, n):
            sem = ctx.enter_context(nc.semaphore(name))
            return [Signal(sem, n, k) for k in range(n)]

        def psum(name, banks=1):
            return ctx.enter_context(nc.psum_tensor(name, [P, banks * 512], F32))

        bank = [psum(f"c_bank{n}") for n in range(8)]

        k_dram = nc.dram_tensor("k_parts", (BATCH, PARTS, DIM, CTX), BF16, kind="Internal").ap()
        q_dram = nc.dram_tensor("q_parts", (BATCH, PARTS, DIM, SEQ), BF16, kind="Internal").ap()

        w, fast = last_block_weights(landing)
        w["CWo"] = fast.pop("CWo")
        loads = len(w) + len(fast)
        w_s, b_s = sb("w_s", [P, KT, 2]), sb("b_s", [P, 2])
        fw_g, fw_b, bv, bo = sb("fw_g", [P, P]), sb("fw_b", [P, P]), sb("bv", [P, DIM]), sb("bo", [P, DIM])
        bq, bk = sb("bq", [P, KT]), sb("bk", [P, KT])
        sel = sb("sel", [P, P])
        ident_b = sb("ident_b", [P, P], BF16)
        ctxT = sb("c_ctxT", [P, KT, CTX])
        stats, mean_var = sb("c_stats", [P, 4, 6]), sb("c_mean_var", [P, 4, 2])
        var_eps, rstd, half_neg, half_pos = (sb("c_" + n, [P, 4]) for n in ("var_eps", "rstd", "half_neg", "half_pos"))
        eps, fw_eps, l2_eps = (sb("c_" + n, [P, 4]) for n in ("eps", "fw_eps", "l2_eps"))
        wait_pad = sb("c_wait_pad", [P, 1])
        lnx, lnT = sb("c_lnx", [P, TOK, DIM]), sb("c_lnT", [P, KT, SEQ])
        f_tanh, f_silu, f_h, f_spare = (sb("c_" + n, [P, 2 * SEQ]) for n in ("f_tanh", "f_silu", "f_h", "f_spare"))
        q_silu, q_sq = (t[:].rearrange("p (n e) -> p n e", n=4) for t in (f_silu, f_spare))
        fo = f_spare[:].rearrange("p (n e) -> p n e", n=4)
        foT, q_full = (t[:].rearrange("p (k s) -> p k s", k=KT) for t in (f_tanh, f_h))
        q_norm = sb("q_norm", [P, 4])
        qT = sb("c_qT", [P, TOK, P, 2])
        s_in, s_tanh = sb("s_in", [P, 4]), sb("s_tanh", [P, 4])
        x4_ahead, x4, x5, x6 = (sb(n, [P, TOK, DIM]) for n in ("x4_ahead", "x4", "x5", "x6"))
        v_ahead = sb("v_ahead", [P, CTILES, DIM])
        k_full = sb("k_full", [P, K_SLOTS, CHUNK])
        k_part = sb("k_part", [P, K_SLOTS, PARTS, CHUNK], BF16)
        q_part = sb("q_part", [P, PARTS, KT, SEQ], BF16)
        v_all = sb("c_v", [P, CTILES, HEADS * (HD + 1) + 32 - HD - 1])
        v_sb = v_all[:, :, 0:HEADS * (HD + 1)].rearrange("p t (h e) -> p t h e", e=HD + 1)
        k_stack = sb("k_stack", [P, 2, GROUP, CTX], BF16)
        ones_row = sb("ones_row", [PARTS, CTX], BF16)
        q_stack = sb("q_stack", [P, HEADS, SEQ], BF16)
        chunk_max = sb("chunk_max", [P, 2 * GROUP, CHUNKS])
        neg_max = sb("neg_max", [P, 2 * GROUP])
        max_part = sb("max_part", [P, TOK, PARTS, GROUP], BF16)
        max_row = sb("max_row", [PARTS * GROUP, SEQ], BF16)
        probs = sb("probs", [P, 2, GROUP, 2, SEQ])
        u_sb, den = sb("u_sb", [P, SEQ]), sb("c_den", [P, SEQ])
        attT = sb("attT", [P, GROUPS, SEQ])
        gu = sb("gu", [P, IT, SEQ])

        const_in, set_, v_set, v_end_set, ones_in = (sig(n) for n in ("c_const_in", "c_set", "v_set", "v_end_set", "c_ones_in"))
        ahead_step, behind_step, max_step = sig("ahead_step", 15), sig("behind_step", 5), sig("max_step", 4 * GROUPS)
        pool_ahead, pool_behind = sig("pool_ahead", 4), sig("pool_behind", 1)
        behind_done, stored = sig("behind_done", 1), sig("c_stored", 16)
        ctx_in = sig("c_ctx_in", 16)
        k_psum, k_full_ready, k_rest_ready, k_part1_ready, k_parts_ready = (sig("c_" + n, 2 * CHUNKS) for n in (
            "k_psum", "k_full_ready", "k_rest_ready", "k_part1_ready", "k_parts_ready"))
        k_written = [sig(f"k_written{n}", 16 * 2 * CHUNKS // K_SLOTS) for n in range(K_SLOTS)]
        v_psum, v_ready, v_copied = sig("c_v_psum", 7), sig("c_v_ready", 7), sig("v_copied", 2)
        stats_ready, rstd_ready = sig("c_stats_ready", 3), sig("c_rstd_ready", 4)
        norm_ready, lnT_psum, lnT_ready = (sig("c_" + n, 2) for n in ("norm_ready", "lnT_psum", "lnT_ready"))
        b_stats_ready, b_rstd_ready, b_norm_ready, b_lnT_psum, b_lnT_ready = (sig("behind_" + n, 1) for n in (
            "stats_ready", "rstd_ready", "norm_ready", "lnT_psum", "lnT_ready"))
        fq_psum, s_psum, fqT_psum, fg_psum, fo_psum, foT_psum, fwo_psum, q_psum = stages("fast_psum", 8)
        fq_tanh, s_tanh_ready, fqT_ready, fg_tanh, foT_ready = stages("fast_act", 5)
        s_in_ready, fq_squares, fq_ready, fh_ready, fo_ready, x4_ready, q_parts_ready = stages("fast_dve", 7)
        q_written, q_stacked = sig("q_written", 32), [sig(f"q_stacked{g}", 16 * TERMS) for g in range(GROUPS)]
        k_stacked = [[sig(f"k_stacked{n}{half}", 2 * 16 * TERMS) for half in "ab"] for n in range(2)]
        MAXES = 2 * GROUP * CHUNKS
        MAX_BANKS = (0, 1, 7)
        max_psum, max_read = sig("max_psum", GROUPS * MAXES), sig("max_read", GROUPS * MAXES)
        max_part_ready, max_row_psum, max_row_ready = (sig(n, GROUPS) for n in ("max_part_ready", "max_row_psum", "max_row_ready"))
        max_stacked = sig("max_stacked", GROUPS * 48)
        HALF = 2 * CHUNK
        HALF_STEPS = HALF // P // 2 * GROUP
        PAIRS = 7
        STEPS = 26
        MAX_BY = 20
        score_psum, prob_ready = sig("c_score_psum", GROUPS * STEPS), sig("c_prob_ready", GROUPS * STEPS)
        tiles_added = sig("tiles_added", GROUPS * PAIRS)
        u_ready, den_psum, den_inverse, head_ready = (sig(n, GROUPS) for n in ("u_ready", "c_den_psum", "den_inverse", "head_ready"))
        x4_kept, den_copied = sig("x4_kept", 1), sig("den_copied", GROUPS)
        co_psum, x5_ready = sig("co_psum", 1), sig("x5_ready", 1)
        gu_psum, gu_tanh, gu_ready = sig("gu_psum", IT // 2), sig("gu_tanh", IT // 2), sig("gu_ready", IT // 2)
        ffn_psum = sig("ffn_psum", 1)

        K_AT = [46 + 5 * u // 2 for u in range(2 * CHUNKS)]
        V_AT = [65 + t for t in range(CTILES)]
        GU_AT = [84 + 5 * p for p in range(IT // 2)]
        KV_STEPS = range(46, 82)

        vector_load = {5: 2, 8: 1, 16: 4, 18: 1.5, 25: 2, 28: 2, 30: 4, 36: 2.5, 38: 1, 43: 2, 44: 2.5, 12: 3, 78: 2, 80: 1,
                       86: 2, 91: 2, 96: 2, 103: 1}
        vector_load.update({7 + g * STEPS: 3 for g in range(GROUPS)})
        vector_load.update({V_AT[2 * b] + 2: 1 for b in range(PAIRS)})

        ROWS_STEP = MAX_BY + 2

        def score_bank(g, t):
            return bank[2 + (g * (STEPS + 1) + t + (t > ROWS_STEP)) % 2]

        def rows_bank(g):
            return bank[2 + ((g - 1) % GROUPS * (STEPS + 1) + ROWS_STEP + 1) % 2]

        def maxes_schedule(g):
            load = [vector_load.get(g * STEPS + t, 0) for t in range(MAX_BY)]
            begun = [0]
            for t in range(MAX_BY):
                due = (sum(load) + MAXES) * (t + 1) / MAX_BY - sum(load[:t + 1])
                begun.append(min(MAXES, max(begun[-1], round(due))))
            begun[-1] = MAXES
            return begun

        def maxes_before(g, t, ahead):
            if (g == GROUPS - 1 and not ahead) or t >= MAX_BY:
                return range(0)
            begun = maxes_schedule(g)
            return range(begun[t], begun[t + 1])

        def following(i, g):
            return (i, g + 1) if g + 1 < GROUPS else (i + 1, 0)

        def preceding(i, g):
            return (i, g - 1) if g else (i - 1, GROUPS - 1)

        def alone(i):
            return isinstance(i, int) and i == 0

        def gate_up(i, p):
            n = ((4, 5), (0, 1), (2, 3))[p] if last_alone(i) else (4, 5)
            return bank[n[0]], bank[n[1]]

        def last_alone(i):
            return isinstance(i, int) and i == BATCH - 1

        def kv_bank(i, n):
            return bank[(2 if alone(i) else 4) + n % 2]

        steps_alone = sorted(range(GROUPS * STEPS), key=lambda s: s - KV_STEPS.start + 14 if s in KV_STEPS else s)

        def passes(eng, ahead_of, body, behind_of):
            ahead_of(0)
            body(0, True, True)
            with eng.Fori(1, BATCH - 1) as i:
                body(i, False, True)
            body(BATCH - 1, False, False)
            behind_of(BATCH - 1)

        def wide(t):
            return t[:].rearrange("p a b -> p (a b)")

        consts_list = ([(w_s, d["w_s"].rearrange("(k p) n -> p k n", p=P)), (b_s, d["b_s"].partition_broadcast(P)),
                          (fw_g, d["fw_g"].partition_broadcast(P)), (fw_b, d["fw_b"].partition_broadcast(P)),
                          (bv, d["bv"].partition_broadcast(P)), (bo, d["bo"].partition_broadcast(P)),
                          (bq, d["bq"]), (bk, d["bk"]), (sel, d["sel"])])
        with nc.Block() as block:
            @block.sync
            def _(sp):
                for t, src in consts_list:
                    sp.dma_start(t[:], src).then_inc(const_in.sem, 16)
                sp.dma_start(ctxT[:], d["ctxT"][0].rearrange("(k p) s -> p k s", p=P)).then_inc(ctx_in.sem, 16)
                sp.wait_ge(set_.sem, 7)
                for n in range(2):
                    for h in range(GROUP):
                        sp.dma_start(k_stack[STACK:DEEP, n, h], ones_row[:]).then_inc(ones_in.sem, 16)
                sp.sem_inc(stored.sem, 16)

                def write_k(i, u):
                    a, c = u // CHUNKS, u % CHUNKS
                    sp.wait_ge(*k_parts_ready(i, u + 1))
                    sp.dma_start(k_dram[i, :, a * P:(a + 1) * P, c * CHUNK:c * CHUNK + width(c)].rearrange("n p s -> p n s"),
                                 k_part[:, u % K_SLOTS, :, 0:width(c)]).then_inc(k_written[u % K_SLOTS].sem, 16)

                def stack_k(i, g, half):
                    c0, c1 = ((0, HALF), (HALF, CTX))[half]
                    row = 0
                    for part, times in ((0, 3), (1, 2), (2, 1)):
                        src = k_dram[i, part, g * GROUP * HD:(g + 1) * GROUP * HD, c0:c1].rearrange("(h e) s -> e h s", e=HD)
                        for r in range(times):
                            sp.dma_start(k_stack[row:row + HD, g % 2, :, c0:c1], src).then_inc(k_stacked[g % 2][half].sem, 16)
                            row += HD

                def write_q(i):
                    sp.wait_ge(*q_parts_ready(i, 1))
                    for k in range(KT):
                        sp.dma_start(q_dram[i, :, k * P:(k + 1) * P, :].rearrange("n p s -> p n s"), q_part[:, :, k, :]).then_inc(q_written.sem, 16)
                    sp.wait_ge(*q_written(i, 32))

                def stack_q(i, g, waits=()):
                    row = 0
                    for parts in (3, 2, 1):
                        for part in range(parts):
                            src = q_dram[i, part, g * GROUP * HD:(g + 1) * GROUP * HD, :].rearrange("(h e) s -> e h s", e=HD)
                            if row // HD < len(waits):
                                sp.wait_ge(*waits[row // HD])
                            sp.dma_start(q_stack[row:row + HD, g * GROUP:(g + 1) * GROUP], src).then_inc(q_stacked[g].sem, 16)
                            row += HD

                def stack_max(i, g):
                    sp.wait_ge(*max_row_ready(i, g + 1))
                    for n in range(PARTS):
                        sp.dma_start(q_stack[STACK + n:STACK + n + 1, g * GROUP:(g + 1) * GROUP, :],
                                     max_row[n * GROUP:(n + 1) * GROUP, :]).then_inc(max_stacked.sem, 16)

                def load_ctx(i):
                    sp.wait_ge(*v_psum(i - 1, 7))
                    sp.dma_start(ctxT[:], d["ctxT"][i % BATCH].rearrange("(k p) s -> p k s", p=P)).then_inc(ctx_in.sem, 16)

                def store(i):
                    sp.wait_ge(*behind_done(i, 1))
                    sp.dma_start(out[i].rearrange("(j p) c -> p j c", p=P), x6[:]).then_inc(stored.sem, 16)

                def ahead(i):
                    for u in range(2 * CHUNKS):
                        write_k(i, u)
                    for k in k_written:
                        sp.wait_ge(*k(i, k.per))
                    for g in range(2):
                        for half in range(2):
                            stack_k(i, g, half)
                    write_q(i)
                    stack_q(i, 0)
                    for g in range(1, GROUPS):
                        stack_q(i, g)
                    load_ctx(i + 1)
                    stack_max(i, 0)

                def body(i, first, more):
                    for g in range(GROUPS):
                        ni, ng = (i, g + 2) if g + 2 < GROUPS else (i + 1, g + 2 - GROUPS)
                        if g + 2 < GROUPS or more:
                            sp.wait_ge(*score_psum(i, g * STEPS + HALF_STEPS))
                            stack_k(ni, ng, 0)
                        if g + 1 < GROUPS or more:
                            stack_max(*following(i, g))
                        if g + 2 < GROUPS or more:
                            sp.wait_ge(*score_psum(i, (g + 1) * STEPS))
                            stack_k(ni, ng, 1)
                        if more and g == 0:
                            write_q(i + 1)
                            stack_q(i + 1, 0)
                        elif more and g == 1:
                            for u in range(2 * CHUNKS):
                                write_k(i + 1, u)
                            stack_q(i + 1, 1, [k(i + 1, k.per) for k in k_written])
                        elif more and g == 2:
                            stack_q(i + 1, 2)
                        elif more and g == 3:
                            stack_q(i + 1, 3)
                            load_ctx(i + 2)
                    if not first:
                        store(i - 1)

                passes(sp, ahead, body, store)
                sp.wait_ge(stored.sem, 16 * (BATCH + 1))
                sp.wait_ge(ctx_in.sem, 16 * (BATCH + 1))

            @block.gpsimd
            def _(pool):
                for t, v in ((eps, LN_EPS), (fw_eps, FW_EPS), (l2_eps, 2 * L2_EPS), (half_neg, -0.5), (half_pos, 0.5)):
                    pool.memset(t[:], v).then_inc(set_.sem, 1)
                pool.tensor_copy(ident_b[:], ident[:]).then_inc(set_.sem, 1)
                pool.memset(ones_row[:], 1.0).then_inc(set_.sem, 1)
                pool.wait_ge(set_.sem, 7)

                def root_of_var(i, wait, done, k, cols, e, step, n):
                    pool.wait_ge(*wait(i, k))
                    pool.tensor_tensor(var_eps[:, 0:cols], mean_var[:, 0:cols, 1], e[:, 0:cols], ALU.add).then_inc(step.sem, 1)
                    pool.wait_ge(*step(i, n))
                    pool.tensor_tensor(rstd[:, 0:cols], var_eps[:, 0:cols], half_neg[:, 0:cols], ALU.pow).then_inc(done.sem, 1)

                def ahead_step_at(i, s):
                    if s == 6:
                        root_of_var(i, stats_ready, rstd_ready, 1, TOK, eps, pool_ahead, 1)
                    elif s == 17:
                        pool.wait_ge(*fq_squares(i, 1))
                        pool.tensor_tensor(q_norm[:], q_norm[:], half_pos[:], ALU.pow).then_inc(pool_ahead.sem, 1)
                        pool.wait_ge(*pool_ahead(i, 2))
                        pool.tensor_tensor(q_norm[:], q_norm[:], l2_eps[:], ALU.add).then_inc(rstd_ready.sem, 1)
                    elif s == 29:
                        root_of_var(i, stats_ready, rstd_ready, 2, 4, fw_eps, pool_ahead, 3)
                    elif s == 37:
                        root_of_var(i, stats_ready, rstd_ready, 3, TOK, eps, pool_ahead, 4)
                    if s - 6 in K_AT:
                        u = K_AT.index(s - 6)
                        m, sl = width(u % CHUNKS), u % K_SLOTS
                        pool.wait_ge(*k_part1_ready(i, u + 1))
                        pool.tensor_tensor(k_part[:, sl, 2, 0:m], k_full[:, sl, 0:m], k_part[:, sl, 1, 0:m],
                                           ALU.subtract).then_inc(k_parts_ready.sem, 1)
                    if s - 3 in K_AT:
                        u = K_AT.index(s - 3)
                        m, sl = width(u % CHUNKS), u % K_SLOTS
                        pool.wait_ge(*k_full_ready(i, u + 1))
                        pool.tensor_tensor(k_full[:, sl, 0:m], k_full[:, sl, 0:m], k_part[:, sl, 0, 0:m],
                                           ALU.subtract).then_inc(k_rest_ready.sem, 1)

                def ahead(i):
                    for s in steps_alone:
                        ahead_step_at(i, s)
                        if s == 7:
                            pool.memset(v_all[:], 0.0).then_inc(v_set.sem, 1)
                            pool.wait_ge(v_set.sem, 1)
                            pool.memset(v_sb[:, :, :, HD:HD + 1], 1.0).then_inc(v_set.sem, 1)

                def behind(i):
                    root_of_var(i, b_stats_ready, b_rstd_ready, 1, TOK, eps, pool_behind, 1)

                def body(i, first, more):
                    if more:
                        for s in range(GROUPS * STEPS):
                            ahead_step_at(i + 1, s)
                    if not first:
                        behind(i - 1)

                passes(pool, ahead, body, behind)

            @block.scalar
            def _(act):
                act.wait_ge(const_in.sem, 16 * len(consts_list))

                def ahead_step_at(i, s):
                    if s in (11, 40):
                        k = 1 if s == 11 else 2
                        act.wait_ge(*lnT_psum(i, k))
                        act.copy(wide(lnT), bank[5][:]).then_inc(lnT_ready.sem, 1)
                    elif s == 15:
                        act.wait_ge(*fq_psum(i, 1))
                        act.activation(f_tanh[:], bank[4][:], ACT.Tanh, scale=0.5).then_inc(fq_tanh.sem, 1)
                    elif s == 17:
                        act.wait_ge(*s_in_ready(i, 1))
                        act.activation(s_tanh[:], s_in[:], ACT.Tanh, scale=0.5).then_inc(s_tanh_ready.sem, 1)
                    elif s == 20:
                        act.wait_ge(*fqT_psum(i, 1))
                        for j in range(TOK):
                            last = act.copy(qT[:, j].rearrange("p t h -> p h t"),
                                            bank[5][:, j * SEQ:(j + 1) * SEQ].rearrange("p (h t) -> p h t", h=2))
                        last.then_inc(fqT_ready.sem, 1)
                    elif s == 24:
                        act.wait_ge(*fg_psum(i, 1))
                        act.activation(f_tanh[:], bank[5][:], ACT.Tanh, scale=0.5).then_inc(fg_tanh.sem, 1)
                    elif s == 33:
                        act.wait_ge(*foT_psum(i, 1))
                        act.copy(f_tanh[:], bank[5][:]).then_inc(foT_ready.sem, 1)
                    if s - 2 in K_AT:
                        u = K_AT.index(s - 2)
                        a, sl = u // CHUNKS, u % K_SLOTS
                        m = width(u % CHUNKS)
                        act.wait_ge(*k_psum(i, u + 1))
                        if u >= K_SLOTS:
                            act.wait_ge(*k_written[sl](i, 16 * (u // K_SLOTS)))
                        act.activation(k_full[:, sl, 0:m], kv_bank(i, u)[:, 0:m], ACT.Identity, bias=bk[:, a:a + 1])
                        act.activation(k_part[:, sl, 0, 0:m], kv_bank(i, u)[:, 0:m], ACT.Identity,
                                       bias=bk[:, a:a + 1]).then_inc(k_full_ready.sem, 1)
                    if s - 5 in K_AT:
                        u = K_AT.index(s - 5)
                        m, sl = width(u % CHUNKS), u % K_SLOTS
                        act.wait_ge(*k_rest_ready(i, u + 1))
                        act.copy(k_part[:, sl, 1, 0:m], k_full[:, sl, 0:m]).then_inc(k_part1_ready.sem, 1)

                def copy_v(i, g0, g1):
                    act.wait_ge(*v_ready(i, 7))
                    act.copy(v_sb[:, :, g0 * GROUP:g1 * GROUP, 0:HD],
                             v_ahead[:, :, g0 * GROUP * HD:g1 * GROUP * HD].rearrange("p t (h e) -> p t h e", e=HD)).then_inc(v_copied.sem, 1)

                def behind_step_at(i, s):
                    if s == 83:
                        act.wait_ge(*b_lnT_psum(i, 1))
                        act.copy(wide(lnT), bank[5][:]).then_inc(b_lnT_ready.sem, 1)
                    elif s - 1 in GU_AT:
                        p = GU_AT.index(s - 1)
                        act.wait_ge(*gu_psum(i, p + 1))
                        if p >= 1:
                            act.wait_ge(*gu_ready(i, p))
                        act.activation(f_tanh[:], gate_up(i, p)[0][:], ACT.Tanh, scale=0.5).then_inc(gu_tanh.sem, 1)

                def copy_u(i, g):
                    act.wait_ge(*tiles_added(i, PAIRS * (g + 1)))
                    if g >= 1 or not isinstance(i, int) or i >= 1:
                        act.wait_ge(*head_ready(i, g))
                    act.copy(u_sb[:], bank[6][:, 0:SEQ]).then_inc(u_ready.sem, 1)

                def copy_den(i, g):
                    act.wait_ge(*den_psum(i, g + 1))
                    act.copy(den[:], bank[6][:, SEQ:]).then_inc(den_copied.sem, 1)

                def body(i, first, more):
                    for g in range(GROUPS):
                        for t in range(STEPS):
                            n, b, s = g * STEPS + t, min(t // 4, PAIRS - 1), g * STEPS + t
                            act.wait_ge(*score_psum(i, n + 1))
                            if not first or g * PAIRS + b >= 2:
                                act.wait_ge(*tiles_added(i, g * PAIRS + b - 1))
                            if t < STEPS - 2:
                                act.activation(probs[:, (g * PAIRS + b) % 2, t % 4].rearrange("p t s -> p (t s)"), score_bank(g, t)[:],
                                               ACT.Exp).then_inc(prob_ready.sem, 1)
                            else:
                                m = rows(CTILES - 1)
                                act.activation(probs[0:m, (g * PAIRS + b) % 2, t % 2 * 2:t % 2 * 2 + 2, 0, :],
                                               score_bank(g, t)[0:m, :].rearrange("p (h s) -> p h s", h=2),
                                               ACT.Exp).then_inc(prob_ready.sem, 1)
                            if t == 2 and not (first and g == 0):
                                copy_u(*preceding(i, g))
                            if t == 4 and not (first and g == 0):
                                copy_den(*preceding(i, g))
                            if s == 4 and not first:
                                copy_v(i, 3, 4)
                            if more:
                                ahead_step_at(i + 1, s)
                            if s == 81 and more:
                                act.wait_ge(*tiles_added(i, 3 * PAIRS))
                                copy_v(i + 1, 0, 3)
                            if not first:
                                behind_step_at(i - 1, s)
                    
                def ahead(i):
                    for s in steps_alone:
                        ahead_step_at(i, s)
                    act.wait_ge(v_set.sem, 2)
                    copy_v(i, 0, 3)
                    copy_v(i, 3, 4)

                def behind(i):
                    copy_u(i, GROUPS - 1)
                    copy_den(i, GROUPS - 1)
                    for s in range(GROUPS * STEPS):
                        behind_step_at(i, s)

                passes(act, ahead, body, behind)

            @block.vector
            def _(dve):

                def moments(i, src, count, step, n, ready):
                    for j in range(count):
                        last = dve.bn_stats(stats[:, j, :], src(j))
                    last.then_inc(step.sem, 1)
                    dve.wait_ge(*step(i, n))
                    dve.memset(wait_pad[:], 0.0)
                    for j in range(count):
                        last = dve.bn_aggr(mean_var[:, j, :], stats[:, j, :])
                    last.then_inc(ready.sem, 1)

                def normalize(src, ready):
                    for j in range(TOK):
                        last = dve.tensor_scalar(lnx[:, j, :], src(j), mean_var[:, j, 0:1], rstd[:, j:j + 1],
                                                 ALU.subtract, ALU.mult)
                    last.then_inc(ready.sem, 1)

                def ahead_step_at(i, s):
                    def step(ins, n):
                        ins.then_inc(ahead_step.sem, 1)
                        dve.wait_ge(*ahead_step(i, n))

                    def x3(j):
                        return x_all[:, TOK * i + j, :]

                    fo_p = bank[4][:].rearrange("p (a b) -> p a b", b=P)
                    if s == 5:
                        moments(i, x3, TOK, ahead_step, 1, stats_ready)
                    elif s == 8:
                        dve.wait_ge(*rstd_ready(i, 1))
                        normalize(x3, norm_ready)
                    elif s == 16:
                        dve.wait_ge(*s_psum(i, 1))
                        dve.tensor_tensor(s_in[:].rearrange("p (j g) -> p j g", g=2), bank[5][:, 0:4].rearrange("p (j g) -> p j g", g=2),
                                          b_s[:].unsqueeze(1).to_broadcast([P, TOK, 2]), ALU.add).then_inc(s_in_ready.sem, 1)
                        dve.wait_ge(*fq_tanh(i, 1))
                        step(dve.scalar_tensor_tensor(f_silu[:], f_tanh[:], 1.0, bank[4][:], ALU.add, ALU.mult), 2)
                        step(dve.tensor_tensor(q_sq, q_silu, q_silu, ALU.mult), 3)
                        dve.tensor_reduce(q_norm[:], q_sq, AX.X, ALU.add).then_inc(fq_squares.sem, 1)
                    elif s == 18:
                        dve.wait_ge(*rstd_ready(i, 2))
                        step(dve.reciprocal(q_norm[:], q_norm[:]), 4)
                        dve.tensor_tensor(q_silu, q_silu, q_norm[:].unsqueeze(2).to_broadcast([P, 4, P]),
                                          ALU.mult).then_inc(fq_ready.sem, 1)
                    elif s == 21:
                        dve.wait_ge(*s_tanh_ready(i, 1))
                        step(dve.scalar_tensor_tensor(s_in[:], s_tanh[:], 1.0, s_in[:], ALU.add, ALU.mult), 5)
                    elif s == 25:
                        dve.wait_ge(*fg_tanh(i, 1))
                        step(dve.scalar_tensor_tensor(f_silu[:], f_tanh[:], 1.0, bank[5][:], ALU.add, ALU.mult), 6)
                        dve.scalar_tensor_tensor(f_h[:], f_silu[:], 0.5, bank[4][:], ALU.mult, ALU.mult).then_inc(fh_ready.sem, 1)
                    elif s == 28:
                        dve.wait_ge(*fo_psum(i, 1))
                        moments(i, lambda j: fo_p[:, j, :], 4, ahead_step, 7, stats_ready)
                    elif s == 30:
                        dve.wait_ge(*rstd_ready(i, 3))
                        for j in range(4):
                            last = dve.tensor_scalar(fo[:, j, :], fo_p[:, j, :], mean_var[:, j, 0:1], rstd[:, j:j + 1], ALU.subtract, ALU.mult)
                        step(last, 8)
                        step(dve.tensor_tensor(fo, fo, fw_g[:].unsqueeze(1).to_broadcast([P, 4, P]), ALU.mult), 9)
                        step(dve.tensor_tensor(fo, fo, fw_b[:].unsqueeze(1).to_broadcast([P, 4, P]), ALU.add), 10)
                        dve.scalar_tensor_tensor(fo, fo, 0.5, s_in[:].unsqueeze(2).to_broadcast([P, 4, P]), ALU.mult,
                                                 ALU.mult).then_inc(fo_ready.sem, 1)
                    elif s == 36:
                        dve.wait_ge(*fwo_psum(i, 1))
                        for j in range(TOK):
                            last = dve.tensor_tensor(x4_ahead[:, j, :], x3(j), bank[4][:, j * DIM:(j + 1) * DIM], ALU.add)
                        last.then_inc(x4_ready.sem, 1)
                        dve.wait_ge(*x4_ready(i, 1))
                        moments(i, lambda j: x4_ahead[:, j, :], TOK, ahead_step, 11, stats_ready)
                    elif s == 38:
                        dve.wait_ge(*rstd_ready(i, 4))
                        normalize(lambda j: x4_ahead[:, j, :], norm_ready)
                    elif s == 43:
                        dve.wait_ge(*q_psum(i, 1))
                        for k in range(KT):
                            last = dve.tensor_scalar(q_full[:, k, :], bank[4][:, k * SEQ:(k + 1) * SEQ], bq[:, k:k + 1], QK_SCALE,
                                                     ALU.add, ALU.mult)
                        step(last, 12)
                        dve.tensor_copy(q_part[:, 0], q_full).then_inc(ahead_step.sem, 1)
                    elif s == 44:
                        dve.wait_ge(*ahead_step(i, 13))
                        step(dve.tensor_tensor(q_full, q_full, q_part[:, 0], ALU.subtract), 14)
                        step(dve.tensor_copy(q_part[:, 1], q_full), 15)
                        dve.tensor_tensor(q_part[:, 2], q_full, q_part[:, 1], ALU.subtract).then_inc(q_parts_ready.sem, 1)
                    if s - 2 in V_AT[::2]:
                        b = V_AT[::2].index(s - 2)
                        if b == 0 and (not isinstance(i, int) or i >= 1):
                            dve.wait_ge(*v_copied(i, 0))
                        dve.wait_ge(*v_psum(i, b + 1))
                        for t in range(2 * b, min(2 * b + 2, CTILES)):
                            m = rows(t)
                            last = dve.tensor_tensor(v_ahead[0:m, t, :], kv_bank(i, b)[0:m, t % 2 * DIM:(t % 2 + 1) * DIM], bv[0:m], ALU.add)
                        last.then_inc(v_ready.sem, 1)

                def behind_step_at(i, s):
                    def step(ins, n):
                        ins.then_inc(behind_step.sem, 1)
                        dve.wait_ge(*behind_step(i, n))

                    if s == 12:
                        dve.wait_ge(*co_psum(i, 1))
                        for j in range(TOK):
                            last = dve.tensor_tensor(x5[:, j, :], x4[:, j, :], bank[4][:, j * DIM:(j + 1) * DIM], ALU.add)
                        step(last, 1)
                        dve.tensor_tensor(x5[:], x5[:], bo[:].unsqueeze(1).to_broadcast([P, TOK, DIM]), ALU.add).then_inc(x5_ready.sem, 1)
                    elif s == 78:
                        dve.wait_ge(*x5_ready(i, 1))
                        moments(i, lambda j: x5[:, j, :], TOK, behind_step, 2, b_stats_ready)
                    elif s == 80:
                        dve.wait_ge(*b_rstd_ready(i, 1))
                        normalize(lambda j: x5[:, j, :], b_norm_ready)
                    elif s - 2 in GU_AT:
                        p = GU_AT.index(s - 2)
                        dve.wait_ge(*gu_tanh(i, p + 1))
                        gate, up = gate_up(i, p)
                        step(dve.scalar_tensor_tensor(f_silu[:], f_tanh[:], 1.0, gate[:], ALU.add, ALU.mult), 3 + p)
                        dve.scalar_tensor_tensor(gu[:, 2 * p:2 * p + 2, :].rearrange("p a b -> p (a b)"), f_silu[:], 0.5,
                                                 up[:], ALU.mult, ALU.mult).then_inc(gu_ready.sem, 1)
                    elif s == 103:
                        dve.wait_ge(*ffn_psum(i, 1))
                        dve.wait_ge(*stored(i, 16))
                        for j in range(TOK):
                            last = dve.tensor_tensor(x6[:, j, :], x5[:, j, :], bank[4][:, j * DIM:(j + 1) * DIM], ALU.add)
                        last.then_inc(behind_done.sem, 1)

                def chunk_maxes(i, g, units):
                    for u in units:
                        c, n = u // (2 * GROUP), g * MAXES + u
                        dve.wait_ge(*max_psum(i, n + 1))
                        dve.tensor_reduce(chunk_max[:, u % (2 * GROUP), c:c + 1], bank[MAX_BANKS[n % 3]][:, 0:width(c)], AX.X,
                                          ALU.max).then_inc(max_read.sem, 1)

                def max_parts(i, g):
                    def step(ins, n):
                        ins.then_inc(max_step.sem, 1)
                        dve.wait_ge(*max_step(i, 4 * g + n))

                    dve.wait_ge(*max_read(i, (g + 1) * MAXES))
                    step(dve.tensor_reduce(neg_max[:], chunk_max[:], AX.X, ALU.max, negate=True), 1)
                    view = neg_max[:].rearrange("p (h j) -> p j h", j=TOK)
                    step(dve.tensor_copy(max_part[:, :, 0, :], view), 2)
                    step(dve.tensor_tensor(view, view, max_part[:, :, 0, :], ALU.subtract), 3)
                    step(dve.tensor_copy(max_part[:, :, 1, :], view), 4)
                    dve.tensor_tensor(max_part[:, :, 2, :], view, max_part[:, :, 1, :], ALU.subtract).then_inc(max_part_ready.sem, 1)

                def max_row_copy(i, g):
                    dve.wait_ge(*max_row_psum(i, g + 1))
                    if g >= 1 or not isinstance(i, int) or i >= 1:
                        dve.wait_ge(*max_stacked(i, 48 * g))
                    dve.tensor_copy(max_row[:], rows_bank(g)[0:PARTS * GROUP, 0:SEQ]).then_inc(max_row_ready.sem, 1)

                def finish_group(i, g):
                    dve.wait_ge(*den_copied(i, g + 1))
                    dve.reciprocal(den[:], den[:]).then_inc(den_inverse.sem, 1)
                    dve.wait_ge(*den_inverse(i, g + 1))
                    dve.tensor_tensor(attT[:, g, :], u_sb[:], den[:], ALU.mult).then_inc(head_ready.sem, 1)

                def keep_x4(i):
                    dve.wait_ge(*x4_ready(i, 1))
                    if not isinstance(i, int) or i >= 1:
                        dve.wait_ge(*x5_ready(i, 0))
                    dve.tensor_copy(x4[:], x4_ahead[:]).then_inc(x4_kept.sem, 1)
                    dve.wait_ge(*x4_kept(i, 1))

                def body(i, first, more):
                    for g in range(GROUPS):
                        for t in range(STEPS):
                            s = g * STEPS + t
                            ni, ng = following(i, g)
                            chunk_maxes(ni, ng, maxes_before(g, t, more))
                            if t == MAX_BY and (g < GROUPS - 1 or more):
                                max_parts(ni, ng)
                            if t == MAX_BY + 2 and (g < GROUPS - 1 or more):
                                max_row_copy(ni, ng)
                            if t == 7 and not (first and g == 0):
                                finish_group(*preceding(i, g))
                            if not first:
                                behind_step_at(i - 1, s)
                            if s == 12:
                                keep_x4(i)
                            if more:
                                ahead_step_at(i + 1, s)

                def ahead(i):
                    for s in steps_alone:
                        ahead_step_at(i, s)
                        if s == 9:
                            dve.memset(v_ahead[:, CTILES - 1, :], 0.0).then_inc(v_end_set.sem, 1)
                            dve.wait_ge(const_in.sem, 16 * len(consts_list))
                            dve.wait_ge(v_end_set.sem, 1)
                    chunk_maxes(i, 0, range(MAXES))
                    max_parts(i, 0)
                    max_row_copy(i, 0)

                def behind(i):
                    finish_group(i, GROUPS - 1)
                    for s in range(GROUPS * STEPS):
                        behind_step_at(i, s)

                passes(dve, ahead, body, behind)

            @block.tensor
            def _(pe):
                def transposed(dst, src):
                    for a in range(KT):
                        for b in range(TOK):
                            last = pe.transpose(dst[:, a * SEQ + b * P:a * SEQ + (b + 1) * P], src[:, b, a * P:(a + 1) * P], ident[:])
                    return last

                def channels_out(dst, weight, act_t, a):
                    for k in range(KT):
                        last = pe.matmul(dst, weight[:, k, a * P:(a + 1) * P], act_t[:, k, :], start=(k == 0), stop=(k == KT - 1))
                    return last

                def tokens_out(dst, weight, act_t, tiles=range(TOK)):
                    for j in tiles:
                        for k in range(KT):
                            last = pe.matmul(dst[:, j * DIM:(j + 1) * DIM], act_t[:, k, j * P:(j + 1) * P], weight[:, k, :],
                                             start=(k == 0), stop=(k == KT - 1))
                    return last

                pe.wait_ge(weights_in.sem, 16 * loads)
                pe.wait_ge(const_in.sem, 16 * len(consts_list))

                def ahead_step_at(i, s):
                    if s == 10:
                        pe.wait_ge(*norm_ready(i, 1))
                        transposed(bank[5], lnx).then_inc(lnT_psum.sem, 1)
                    elif s == 13:
                        pe.wait_ge(*lnT_ready(i, 1))
                        if not isinstance(i, int):
                            pe.wait_ge(*x5_ready(i - 1, 0))
                        tokens_out(bank[4], w["FWq"], lnT, (0,))
                    elif s == 14:
                        tokens_out(bank[4], w["FWq"], lnT, (1,)).then_inc(fq_psum.sem, 1)
                    elif s == 15:
                        for j in range(TOK):
                            for k in range(KT):
                                last = pe.matmul(bank[5][:, 2 * j:2 * j + 2], lnT[:, k, j * P:(j + 1) * P], w_s[:, k, :],
                                                 start=(k == 0), stop=(k == KT - 1))
                        last.then_inc(s_psum.sem, 1)
                    elif s == 20:
                        pe.wait_ge(*s_in_ready(i, 1))
                        pe.wait_ge(*fq_ready(i, 1))
                        for n in range(4):
                            last = pe.transpose(bank[5][:, n * P:(n + 1) * P], q_silu[:, n, :], ident[:])
                        last.then_inc(fqT_psum.sem, 1)
                    elif s in (22, 23):
                        if s == 22:
                            pe.wait_ge(*fqT_ready(i, 1))
                        b, name = (4, "w2T") if s == 22 else (5, "w0T")
                        for g in range(2):
                            last = pe.matmul(bank[b][:, g * SEQ:(g + 1) * SEQ], fast[name][:, g, :],
                                             qT[:, g].rearrange("p t h -> p (t h)"), start=True, stop=True)
                        if s == 23:
                            last.then_inc(fg_psum.sem, 1)
                    elif s == 28:
                        pe.wait_ge(*fh_ready(i, 1))
                        for j in range(TOK):
                            for g in range(2):
                                last = pe.matmul(bank[4][:, (2 * j + g) * P:(2 * j + g + 1) * P], f_h[:, g * SEQ + j * P:g * SEQ + (j + 1) * P],
                                                 fast["w1T"][:, g, :], start=True, stop=True)
                        last.then_inc(fo_psum.sem, 1)
                    elif s == 33:
                        pe.wait_ge(*fo_ready(i, 1))
                        transposed(bank[5], fo.rearrange("p (j g) e -> p j (g e)", g=2)).then_inc(foT_psum.sem, 1)
                    elif s == 35:
                        pe.wait_ge(*foT_ready(i, 1))
                        tokens_out(bank[4], w["FWo"], foT, (0,))
                    elif s == 36:
                        tokens_out(bank[4], w["FWo"], foT, (1,)).then_inc(fwo_psum.sem, 1)
                    elif s == 39:
                        pe.wait_ge(*norm_ready(i, 2))
                        transposed(bank[5], lnx).then_inc(lnT_psum.sem, 1)
                    elif s == 41:
                        pe.wait_ge(*lnT_ready(i, 2))
                        channels_out(bank[4][:, 0:SEQ], w["CWq"], lnT, 0)
                    elif s == 42:
                        channels_out(bank[4][:, SEQ:], w["CWq"], lnT, 1).then_inc(q_psum.sem, 1)
                    if s in K_AT:
                        u = K_AT.index(s)
                        a, c = u // CHUNKS, u % CHUNKS
                        if u == 0:
                            pe.wait_ge(*ctx_in(i, 16))
                        if u == 0 and not alone(i):
                            pe.wait_ge(*q_parts_ready(i, 1))
                        if u >= 2:
                            pe.wait_ge(*k_full_ready(i, u - 1))
                    for k in range(KT):
                        if s - k in K_AT:
                            u = K_AT.index(s - k)
                            a, c = u // CHUNKS, u % CHUNKS
                            last = pe.matmul(kv_bank(i, u)[:, 0:width(c)], w["CWk"][:, k, a * P:(a + 1) * P],
                                             ctxT[:, k, c * CHUNK:c * CHUNK + width(c)], start=(k == 0), stop=(k == KT - 1))
                            if k == KT - 1:
                                last.then_inc(k_psum.sem, 1)
                    if s in V_AT:
                        t = V_AT.index(s)
                        b, m = t // 2, rows(t)
                        if t in (0, 2):
                            pe.wait_ge(*k_full_ready(i, 2 * CHUNKS - 1 + b))
                        elif t % 2 == 0:
                            pe.wait_ge(*v_ready(i, b - 1))
                        for k in range(KT):
                            last = pe.matmul(kv_bank(i, b)[0:m, t % 2 * DIM:(t % 2 + 1) * DIM], ctxT[:, k, t * P:t * P + m],
                                             w["CWv"][:, k, :], start=(k == 0), stop=(k == KT - 1))
                        if t % 2 == 1 or t == CTILES - 1:
                            last.then_inc(v_psum.sem, 1)

                def behind_step_at(i, s):
                    if s in (9, 10):
                        j = s - 9
                        if s == 9:
                            pe.wait_ge(*head_ready(i, GROUPS))
                        for g in range(GROUPS):
                            last = pe.matmul(bank[4][:, j * DIM:(j + 1) * DIM], attT[:, g, j * P:(j + 1) * P], w["CWo"][:, g, :],
                                             start=(g == 0), stop=(g == GROUPS - 1))
                        if s == 10:
                            last.then_inc(co_psum.sem, 1)
                    elif s == 82:
                        pe.wait_ge(*b_norm_ready(i, 1))
                        transposed(bank[5], lnx).then_inc(b_lnT_psum.sem, 1)
                    elif s in GU_AT:
                        p = GU_AT.index(s)
                        if p == 0:
                            pe.wait_ge(*b_lnT_ready(i, 1))
                        elif not last_alone(i):
                            pe.wait_ge(*gu_ready(i, p))
                        for a in range(2):
                            channels_out(gate_up(i, p)[0][:, a * SEQ:(a + 1) * SEQ], lut_w["gate"], lnT, 2 * p + a)
                    elif s - 1 in GU_AT:
                        p = GU_AT.index(s - 1)
                        for a in range(2):
                            last = channels_out(gate_up(i, p)[1][:, a * SEQ:(a + 1) * SEQ], lut_w["up"], lnT, 2 * p + a)
                        last.then_inc(gu_psum.sem, 1)
                    elif s >= 98:
                        j, c0 = (s - 98) // 3, (s - 98) % 3 * 2
                        if s == 98:
                            pe.wait_ge(*gu_ready(i, IT // 2))
                        for c in (c0, c0 + 1):
                            m = min(P, INNER - c * P)
                            last = pe.matmul(bank[4][:, j * DIM:(j + 1) * DIM], gu[0:m, c, j * P:(j + 1) * P], lut_w["down"][0:m, c, :],
                                             start=(c == 0), stop=(c == IT - 1))
                        if s == 103:
                            last.then_inc(ffn_psum.sem, 1)

                def max_scores(i, g, units, first=False):
                    for u in units:
                        n, h, j, c = g * MAXES + u, u // 2 % GROUP, u % 2, u // (2 * GROUP)
                        if u == 0:
                            pe.wait_ge(*q_stacked[g](i, 96))
                        if u in (0, MAXES // 2):
                            pe.wait_ge(*k_stacked[g % 2][u * 2 // MAXES](i, 96 * (g // 2 + 1)))
                        if n >= 3:
                            pe.wait_ge(*max_read(i, n - 2))
                        elif not first:
                            pe.wait_ge(*max_read(i, min(n - 1, 0)))
                        pe.matmul(bank[MAX_BANKS[n % 3]][:, 0:width(c)], q_stack[0:STACK, g * GROUP + h, j * P:(j + 1) * P],
                                  k_stack[0:STACK, g % 2, h, c * CHUNK:c * CHUNK + width(c)], start=True,
                                  stop=True).then_inc(max_psum.sem, 1)

                def max_rows(i, g):
                    pe.wait_ge(*max_part_ready(i, g + 1))
                    for j in range(TOK):
                        last = pe.matmul(rows_bank(g)[0:PARTS * GROUP, j * P:(j + 1) * P],
                                         max_part[:, j].rearrange("p n h -> p (n h)"), ident_b[:], start=True, stop=True)
                    last.then_inc(max_row_psum.sem, 1)

                def scores(i, g, t, first):
                    n = g * STEPS + t
                    if t == 0:
                        pe.wait_ge(*max_stacked(i, 48 * (g + 1)))
                    if t == ROWS_STEP + 1:
                        pe.wait_ge(*prob_ready(i, n))
                    elif n >= 2 or not first:
                        pe.wait_ge(*prob_ready(i, n - 1))
                    for e in range(2):
                        h, tile = (t % 4, t // 4 * 2 + e) if t < STEPS - 2 else (t % 2 * 2 + e, CTILES - 1)
                        m = rows(tile)
                        last = pe.matmul(score_bank(g, t)[0:m, e * SEQ:(e + 1) * SEQ], k_stack[0:DEEP, g % 2, h, tile * P:tile * P + m],
                                         q_stack[0:DEEP, g * GROUP + h, :], start=True, stop=True)
                    last.then_inc(score_psum.sem, 1)

                def add_values(i, g, tile, first):
                    b, m = tile // 2, rows(tile)
                    if tile % 2 == 0:
                        pe.wait_ge(*prob_ready(i, g * STEPS + min(4 * b + 4, STEPS)))
                    if tile == 0 and (g >= 1 or not first):
                        pe.wait_ge(*den_copied(i, g))
                    if tile == 0 and g in (0, GROUPS - 1):
                        pe.wait_ge(*v_copied(i, 1 if g == 0 else 2))
                    for h in range(GROUP):
                        first_col = (g * GROUP + h) * (HD + 1)
                        last = pe.matmul(bank[6][32 * h:32 * h + 32, 0:SEQ], v_all[0:m, tile, first_col:first_col + 32],
                                         probs[0:m, (g * PAIRS + b) % 2, h, tile % 2, :], start=(tile == 0), stop=(tile == CTILES - 1))
                    if tile % 2 == 1 or tile == CTILES - 1:
                        last.then_inc(tiles_added.sem, 1)

                def sum_rows(i, g):
                    pe.wait_ge(*u_ready(i, g + 1))
                    pe.matmul(bank[6][:, SEQ:], sel[:], u_sb[:], start=True, stop=True).then_inc(den_psum.sem, 1)

                def body(i, first, more):
                    for g in range(GROUPS):
                        for t in range(STEPS):
                            s = g * STEPS + t
                            ni, ng = following(i, g)
                            pi, pg = preceding(i, g)
                            if t == ROWS_STEP + 2 and (g < GROUPS - 1 or more):
                                pe.wait_ge(*max_row_ready(ni, ng + 1))
                            scores(i, g, t, first)
                            units = maxes_before(g, t, more)
                            max_scores(ni, ng, units[:1])
                            if t == ROWS_STEP and (g < GROUPS - 1 or more):
                                pe.wait_ge(*prob_ready(i, g * STEPS + t))
                                max_rows(ni, ng)
                            if t < 2 and not (first and g == 0):
                                add_values(pi, pg, CTILES - 2 + t, first)
                            if t >= 5 and t % 4 < 3 and t % 4 > 0:
                                add_values(i, g, t // 4 * 2 - 2 + (t % 4 - 1), first)
                            if t == 4 and not (first and g == 0):
                                sum_rows(pi, pg)
                            if not first:
                                behind_step_at(i - 1, s)
                            if more:
                                ahead_step_at(i + 1, s)
                            max_scores(ni, ng, units[1:])

                def ahead(i):
                    for s in steps_alone:
                        ahead_step_at(i, s)
                    pe.wait_ge(set_.sem, 7)
                    pe.wait_ge(ones_in.sem, 16 * 2 * GROUP)
                    max_scores(i, 0, range(MAXES), True)
                    max_rows(i, 0)

                def behind(i):
                    add_values(i, GROUPS - 1, CTILES - 2, False)
                    add_values(i, GROUPS - 1, CTILES - 1, False)
                    sum_rows(i, GROUPS - 1)
                    for s in range(GROUPS * STEPS):
                        behind_step_at(i, s)

                passes(pe, ahead, body, behind)


def last_block_weights(landing):
    def cut(place, n, kt, cols):
        flat = landing[:, place].rearrange("p m n -> p (m n)")
        return flat[:, n:n + kt * cols].rearrange("p (k c) -> p k c", k=kt)

    one, two = {}, {"CWo": cut(1, 0, 4, DIM)}
    for n, name in enumerate(("FWq", "FWo", "CWq", "CWk", "CWv")):
        one[name] = cut(0, n * KT * DIM, KT, DIM)
    for n, name in enumerate(("w0T", "w1T", "w2T")):
        two[name] = cut(1, 4 * DIM + n * KT * P, KT, P)
    return one, two


def build(nc, d, out):
    with ExitStack() as ctx:
        x_all = ctx.enter_context(nc.sbuf_tensor("x_all", [P, BATCH * TOK, DIM], F32))
        ident = ctx.enter_context(nc.sbuf_tensor("ident", [P, P], F32))
        lut_all = ctx.enter_context(nc.sbuf_tensor("lut_all", [P, 3 * 6 * DIM], F32))
        lut_w = {"all": lut_all,
                 "gate": lut_all[:, 0:6 * DIM].rearrange("p (k n) -> p k n", k=KT),
                 "up": lut_all[:, 6 * DIM:12 * DIM].rearrange("p (k n) -> p k n", k=KT),
                 "down": lut_all[:, 12 * DIM:].rearrange("p (c n) -> p c n", c=6)}
        attention_and_context(nc, d, x_all, ident)
        landing = ctx.enter_context(nc.sbuf_tensor("landing", [P, 2, 3, KT * 512], F32))
        c_weights_in = Signal(ctx.enter_context(nc.semaphore("c_weights_in")))
        experts(nc, d, x_all, ident, lut_w, landing, c_weights_in)
        fast_weights_softmax_and_lut(nc, d, out, x_all, ident, lut_w, landing, c_weights_in)


def layout(inputs):
    import numpy as np

    def a(n):
        return np.asarray(inputs[n])

    def t(n):
        return np.ascontiguousarray(a(n).T)

    def col(n):
        return np.ascontiguousarray(a(n).reshape(KT, P).T)

    d = {"x": a("x"), "ctxT": np.ascontiguousarray(a("ctx_2048").transpose(0, 2, 1))}
    for n in ("r", "k", "v", "g", "o"):
        d[f"W{n}T"] = t(f"L0_attn_W{n}")
    for n in ("k", "v", "r", "g"):
        d["maa_" + n] = col("L0_attn_time_maa_" + n)
    d["time_decay"] = a("L0_attn_time_decay").reshape(-1)
    d["faaaa"] = a("L0_attn_time_faaaa").reshape(-1)
    d["gamma"], d["beta"] = a("L0_attn_gamma"), a("L0_attn_beta")
    for n in ("q", "g", "kv", "o"):
        d[f"XW{n}T"] = t(f"L0_xattn_W{n}")
    d["xbg"] = col("L0_xattn_bg")
    key = np.arange(P)[:, None]
    tok = np.concatenate([np.arange(SEQ), np.arange(P)])[None, :]
    d["delta"] = np.maximum(tok - key - 1, 0).astype(np.float32)
    d["strict"] = (tok > key).astype(np.float32)
    d["diag"] = (tok == key).astype(np.float32)
    d["headmask"] = (np.arange(P)[:, None] // 8 == np.arange(P // 8)[None, :]).astype(np.float32)
    d["blk16"] = (np.arange(P)[:, None] // 16 == np.arange(P)[None, :] // 16).astype(np.float32)
    d["routerT"] = t("L0_ffn_router_w")
    for n in ("gate", "up", "down"):
        d[n + "T"] = np.ascontiguousarray(a(f"L0_ffn_{n}_w").transpose(0, 2, 1))
    d["lut"], d["lut_key"] = a("L1_ffn_lut"), np.arange(16, dtype=np.float32)
    for n in ("gate", "up"):
        d[n + "_idx"] = np.ascontiguousarray(np.pad(a(f"L1_ffn_{n}_idx").T, ((0, 0), (0, 768 - 688))))
    d["down_idx"] = np.ascontiguousarray(np.pad(a("L1_ffn_down_idx").T, ((0, 768 - 688), (0, 0))))
    qkv = a("L1_attn_W_qkv")
    d["FWq"] = np.ascontiguousarray(np.concatenate([qkv[:, 0:P], qkv[:, 3 * P:4 * P]], axis=1))
    d["FWo"], d["w_s"], d["b_s"] = a("L1_attn_W_o"), a("L1_attn_W_s"), a("L1_attn_b_s")
    d["fw_g"], d["fw_b"] = a("L1_attn_ln_g"), a("L1_attn_ln_b")
    for n in range(3):
        d[f"w{n}T"] = np.ascontiguousarray(a(f"L1_attn_w{n}").transpose(0, 2, 1))
    for n in ("q", "k", "v"):
        d["CW" + n] = t("L1_xattn_W" + n)
    d["CWo"] = np.ascontiguousarray(np.pad(a("L1_xattn_Wo").T.reshape(16, 16, DIM), ((0, 0), (0, 16), (0, 0))).reshape(512, DIM))
    d["bq"], d["bk"], d["bv"], d["bo"] = col("L1_xattn_bq"), col("L1_xattn_bk"), a("L1_xattn_bv"), a("L1_xattn_bo")
    rows_, cols_ = np.arange(P)[:, None], np.arange(P)[None, :]
    d["sel"] = ((rows_ % 32 == 16) & (rows_ // 32 == cols_ // 32)).astype(np.float32)
    d["earlier"] = np.tril(np.ones((8, 8), np.float32), -1)
    d["ident"] = np.eye(P, dtype=np.float32)
    return d


def kernel(**inputs):
    import concourse.bacc as bacc
    from concourse.bass_utils import run_bass_kernel_spmd

    nc = bacc.Bacc("TRN2", target_bir_lowering=False, num_devices=1)
    arrays = {"in_" + k: v for k, v in layout(inputs).items()}
    d = {k[3:]: nc.dram_tensor(k, v.shape, mybir.dt.from_np(v.dtype), kind="ExternalInput").ap() for k, v in arrays.items()}
    out = nc.dram_tensor("out", (BATCH, SEQ, DIM), F32, kind="ExternalOutput").ap()
    build(nc, d, out)
    r = run_bass_kernel_spmd(nc, [arrays], core_ids=[0])
    return r.results[0]["out"]
```
